# Optimizing a Trainium2 kernel written in Bass

```python
import numpy as np
import jax
import jax.numpy as jnp

def _softmax(x, axis=-1):
    return jax.nn.softmax(x, axis=axis)
def _gelu(x):
    return jax.nn.gelu(x, approximate=True)
def _silu(x):
    return jax.nn.silu(x)
def _sigmoid(x):
    return jax.nn.sigmoid(x)
def _layernorm(x, axis=-1, eps=1e-5):
    m = jnp.mean(x, axis=axis, keepdims=True)
    v = jnp.var(x, axis=axis, keepdims=True)
    return (x - m) / jnp.sqrt(v + eps)
def _scatter_add(tgt, idx, src, axis=0):
    return tgt.at[idx].add(src)
def _segment_sum(src, seg, n):
    return jax.ops.segment_sum(src, seg, n)

kernel_name = 'mk_adj_resnorm_d4_adj_256_97251b'

def setup_inputs(seed: int = 0):
    np.random.seed(seed)
    _w = jnp.asarray
    def _rec_inputs():
        import jax
        import jax.numpy as jnp
        _gk = jax.random.key(seed)
        x = -0.0003929 + 0.9999 * jax.random.normal(jax.random.fold_in(_gk, 1), (128, 64, 256), jnp.float32)
        _a = jax.random.bernoulli(jax.random.fold_in(_gk, 2), 0.0625, (64, 64))
        _a = jnp.logical_or(_a, jnp.swapaxes(_a, -1, -2))
        _a = jnp.logical_or(_a, jnp.eye(64, dtype=bool))
        _af = _a.astype(jnp.float32)
        _af = _af * jax.random.uniform(jax.random.fold_in(_gk, 3), (64, 64), jnp.float32, 0.05, 1)
        adj = _af
        return x, adj
    x, adj = _rec_inputs()
    def _L0_gnn_setup():
        import jax, jax.numpy as jnp
        import numpy as np
        EPS = 1e-05

        def _batchnorm(x, gamma, beta):
            mu = jnp.mean(x, axis=0)
            var = jnp.var(x, axis=0)
            return (x - mu) * jax.lax.rsqrt(var + EPS) * gamma + beta
        key = jax.random.key(seed)
        ks = jax.random.split(key, 4)
        b, n, d, h, o = (32, 2048, 256, 512, 256)
        features = jax.random.normal(ks[0], (b, n, d), dtype=jnp.float32)
        A = jax.random.uniform(ks[1], (n, n), dtype=jnp.float32)
        lim1 = float(np.sqrt(6.0 / (d + h)))
        W1 = jax.random.uniform(ks[2], (h, d), minval=-lim1, maxval=lim1, dtype=jnp.float32)
        b1 = jnp.zeros((h,), jnp.float32)
        lim2 = float(np.sqrt(6.0 / (h + o)))
        W2 = jax.random.uniform(ks[3], (o, h), minval=-lim2, maxval=lim2, dtype=jnp.float32)
        b2 = jnp.zeros((o,), jnp.float32)
        g1 = jnp.ones((h,), jnp.float32)
        be1 = jnp.zeros((h,), jnp.float32)
        g2 = jnp.ones((o,), jnp.float32)
        be2 = jnp.zeros((o,), jnp.float32)
        return {'features': features, 'A': A, 'W1': W1, 'b1': b1, 'g1': g1, 'be1': be1, 'W2': W2, 'b2': b2, 'g2': g2, 'be2': be2}
    _L0_gnn_all = _L0_gnn_setup()
    _L0_gnn_in = {k: v for k, v in _L0_gnn_all.items() if k in ('W1', 'b1', 'g1', 'be1', 'W2', 'b2', 'g2', 'be2', )}
    del _L0_gnn_all

    def _L1_gnn_setup():
        import jax, jax.numpy as jnp
        import numpy as np
        EPS_LN = 1e-05

        def _layernorm(x, g, b):
            mu = x.mean(-1, keepdims=True)
            var = ((x - mu) ** 2).mean(-1, keepdims=True)
            return (x - mu) / jnp.sqrt(var + EPS_LN) * g + b
        key = jax.random.key(seed)
        B, N, D, H = (4, 2048, 256, 4)
        hid = int(D * 2.0)
        ks = jax.random.split(key, 12)
        x = jax.random.normal(ks[0], (B, N, D), jnp.float32)
        Au = jax.random.uniform(ks[1], (N, N)) < 0.004
        A = jnp.logical_or(Au, Au.T)
        A = A.at[jnp.arange(N), jnp.arange(N)].set(False)
        Af = A.astype(jnp.float32)
        deg = Af.sum(axis=1)
        L = jnp.diag(deg) - Af
        adjacency = Af + jnp.eye(N, dtype=jnp.float32)
        s = lambda k, sh, f: jax.random.normal(k, sh, jnp.float32) * f
        sc = 1.0 / np.sqrt(D)
        Wc = s(ks[2], (D, D), sc)
        bc = jnp.zeros((D,), jnp.float32)
        Wq = s(ks[3], (D, D), sc)
        Wk = s(ks[4], (D, D), sc)
        Wv = s(ks[5], (D, D), sc)
        Wo = s(ks[6], (D, D), sc)
        bo = jnp.zeros((D,), jnp.float32)
        W1 = s(ks[7], (D, hid), sc)
        b1 = jnp.zeros((hid,), jnp.float32)
        W2 = s(ks[8], (hid, D), 1.0 / np.sqrt(hid))
        b2 = jnp.zeros((D,), jnp.float32)
        g1 = jnp.ones((D,), jnp.float32)
        be1 = jnp.zeros((D,), jnp.float32)
        g2 = jnp.ones((D,), jnp.float32)
        be2 = jnp.zeros((D,), jnp.float32)
        g3 = jnp.ones((D,), jnp.float32)
        be3 = jnp.zeros((D,), jnp.float32)
        return dict(x=x, L=L, adjacency=adjacency, Wc=Wc, bc=bc, g1=g1, be1=be1, Wq=Wq, Wk=Wk, Wv=Wv, Wo=Wo, bo=bo, g2=g2, be2=be2, W1=W1, b1=b1, W2=W2, b2=b2, g3=g3, be3=be3)
    _L1_gnn_all = _L1_gnn_setup()
    _L1_gnn_in = {k: v for k, v in _L1_gnn_all.items() if k in ('Wc', 'bc', 'g1', 'be1', 'Wq', 'Wk', 'Wv', 'Wo', 'bo', 'g2', 'be2', 'W1', 'b1', 'W2', 'b2', 'g3', 'be3', )}
    del _L1_gnn_all

    def _L2_gnn_setup():
        import jax, jax.numpy as jnp
        import numpy as np
        B, T, D, H = (64, 2048, 256, 256)
        MAX_SKIP = 4

        def _lstm_last(Wih, Whh, bih, bhh, xs):
            N, _, Hd = xs.shape
            bias = bih + bhh

            def step(carry, x_t):
                h, c = carry
                g = x_t @ Wih.T + h @ Whh.T + bias
                i, f, gg, o = jnp.split(g, 4, axis=-1)
                c = jax.nn.sigmoid(f) * c + jax.nn.sigmoid(i) * jnp.tanh(gg)
                h = jax.nn.sigmoid(o) * jnp.tanh(c)
                return ((h, c), None)
            init = (jnp.zeros((N, Hd), xs.dtype), jnp.zeros((N, Hd), xs.dtype))
            (h_last, _), _ = jax.lax.scan(step, init, jnp.swapaxes(xs, 0, 1))
            return h_last
        key = jax.random.key(seed)
        ks = jax.random.split(key, 8)
        s = 0.05
        x = jax.random.normal(ks[0], (B, T, D), jnp.float32)
        adj = jax.random.uniform(ks[1], (T, T), jnp.float32) / T
        Wg0 = jax.random.normal(ks[2], (D, H), jnp.float32) * s
        bg0 = jnp.zeros((H,), jnp.float32)
        Wg1 = jax.random.normal(ks[3], (H, H), jnp.float32) * s
        bg1 = jnp.zeros((H,), jnp.float32)
        Wih = jax.random.normal(ks[4], (MAX_SKIP, 4 * H, H), jnp.float32) * s
        Whh = jax.random.normal(ks[5], (MAX_SKIP, 4 * H, H), jnp.float32) * s
        bih = jax.random.normal(ks[6], (MAX_SKIP, 4 * H), jnp.float32) * s
        bhh = jax.random.normal(ks[7], (MAX_SKIP, 4 * H), jnp.float32) * s
        return dict(x=x, adj=adj, Wg0=Wg0, bg0=bg0, Wg1=Wg1, bg1=bg1, Wih=Wih, Whh=Whh, bih=bih, bhh=bhh)
    _L2_gnn_all = _L2_gnn_setup()
    _L2_gnn_in = {k: v for k, v in _L2_gnn_all.items() if k in ('Wg0', 'bg0', 'Wg1', 'bg1', 'Wih', 'Whh', 'bih', 'bhh', )}
    del _L2_gnn_all

    def _L3_gnn_setup():
        import jax, jax.numpy as jnp
        import numpy as np
        ALPHA = 0.2
        key = jax.random.key(seed)
        k1, k2, k3, k4 = jax.random.split(key, 4)
        B, N, Fin, Fout = (8, 2048, 256, 256)
        h = jax.random.normal(k1, (B, N, Fin), dtype=jnp.float32)
        adj = jax.random.randint(k2, (N, N), 0, 2).astype(jnp.float32)
        adj = jnp.maximum(adj, jnp.eye(N, dtype=jnp.float32))

        def xavier(k, shape, gain=1.414):
            fan_in, fan_out = (shape[0], shape[1])
            a = gain * np.sqrt(6.0 / (fan_in + fan_out))
            return jax.random.uniform(k, shape, dtype=jnp.float32, minval=-a, maxval=a)
        W = xavier(k3, (Fin, Fout))
        a = xavier(k4, (2 * Fout, 1))
        return {'h': h, 'adj_matrix': adj, 'W': W, 'a': a}
    _L3_gnn_all = _L3_gnn_setup()
    _L3_gnn_in = {k: v for k, v in _L3_gnn_all.items() if k in ('W', 'a', )}
    del _L3_gnn_all

    return {
        "x": x,
        "adj": adj,
        "L0_gnn_W1": _L0_gnn_in["W1"],
        "L0_gnn_b1": _L0_gnn_in["b1"],
        "L0_gnn_g1": _L0_gnn_in["g1"],
        "L0_gnn_be1": _L0_gnn_in["be1"],
        "L0_gnn_W2": _L0_gnn_in["W2"],
        "L0_gnn_b2": _L0_gnn_in["b2"],
        "L0_gnn_g2": _L0_gnn_in["g2"],
        "L0_gnn_be2": _L0_gnn_in["be2"],
        "L1_gnn_Wc": _L1_gnn_in["Wc"],
        "L1_gnn_bc": _L1_gnn_in["bc"],
        "L1_gnn_g1": _L1_gnn_in["g1"],
        "L1_gnn_be1": _L1_gnn_in["be1"],
        "L1_gnn_Wq": _L1_gnn_in["Wq"],
        "L1_gnn_Wk": _L1_gnn_in["Wk"],
        "L1_gnn_Wv": _L1_gnn_in["Wv"],
        "L1_gnn_Wo": _L1_gnn_in["Wo"],
        "L1_gnn_bo": _L1_gnn_in["bo"],
        "L1_gnn_g2": _L1_gnn_in["g2"],
        "L1_gnn_be2": _L1_gnn_in["be2"],
        "L1_gnn_W1": _L1_gnn_in["W1"],
        "L1_gnn_b1": _L1_gnn_in["b1"],
        "L1_gnn_W2": _L1_gnn_in["W2"],
        "L1_gnn_b2": _L1_gnn_in["b2"],
        "L1_gnn_g3": _L1_gnn_in["g3"],
        "L1_gnn_be3": _L1_gnn_in["be3"],
        "L2_gnn_Wg0": _L2_gnn_in["Wg0"],
        "L2_gnn_bg0": _L2_gnn_in["bg0"],
        "L2_gnn_Wg1": _L2_gnn_in["Wg1"],
        "L2_gnn_bg1": _L2_gnn_in["bg1"],
        "L2_gnn_Wih": _L2_gnn_in["Wih"],
        "L2_gnn_Whh": _L2_gnn_in["Whh"],
        "L2_gnn_bih": _L2_gnn_in["bih"],
        "L2_gnn_bhh": _L2_gnn_in["bhh"],
        "L3_gnn_W": _L3_gnn_in["W"],
        "L3_gnn_a": _L3_gnn_in["a"],
    }

def reference(x, adj, L0_gnn_W1, L0_gnn_b1, L0_gnn_g1, L0_gnn_be1, L0_gnn_W2, L0_gnn_b2, L0_gnn_g2, L0_gnn_be2, L1_gnn_Wc, L1_gnn_bc, L1_gnn_g1, L1_gnn_be1, L1_gnn_Wq, L1_gnn_Wk, L1_gnn_Wv, L1_gnn_Wo, L1_gnn_bo, L1_gnn_g2, L1_gnn_be2, L1_gnn_W1, L1_gnn_b1, L1_gnn_W2, L1_gnn_b2, L1_gnn_g3, L1_gnn_be3, L2_gnn_Wg0, L2_gnn_bg0, L2_gnn_Wg1, L2_gnn_bg1, L2_gnn_Wih, L2_gnn_Whh, L2_gnn_bih, L2_gnn_bhh, L3_gnn_W, L3_gnn_a):
    import jax
    import jax.numpy as jnp
    def _L0_gnn_ref(features, A, W1, b1, g1, be1, W2, b2, g2, be2):
        import jax, jax.numpy as jnp
        import numpy as np
        EPS = 1e-05

        def _batchnorm(x, gamma, beta):
            mu = jnp.mean(x, axis=0)
            var = jnp.var(x, axis=0)
            return (x - mu) * jax.lax.rsqrt(var + EPS) * gamma + beta
        b, n, d = features.shape
        A_norm = A + jnp.eye(n, dtype=A.dtype)
        deg = jnp.sum(A_norm, axis=0) + jnp.sum(A_norm, axis=1) - jnp.diagonal(A_norm)
        dinv = jax.lax.rsqrt(deg)
        A_hat = A_norm * dinv[:, None] * dinv[None, :]
        agg = jnp.einsum('nm,bmd->bnd', A_hat, features)
        x = agg.reshape(-1, d)
        h = jax.nn.relu(_batchnorm(x @ W1.T + b1, g1, be1))
        out = h @ W2.T + b2
        out = _batchnorm(out, g2, be2)
        return out.reshape(b, n, -1)

    def _L1_gnn_ref(x, L, adjacency, Wc, bc, g1, be1, Wq, Wk, Wv, Wo, bo, g2, be2, W1, b1, W2, b2, g3, be3):
        import jax, jax.numpy as jnp
        import numpy as np
        EPS_LN = 1e-05

        def _layernorm(x, g, b):
            mu = x.mean(-1, keepdims=True)
            var = ((x - mu) ** 2).mean(-1, keepdims=True)
            return (x - mu) / jnp.sqrt(var + EPS_LN) * g + b
        B, N, D = x.shape
        H = 4
        hd = D // H
        eig = jnp.linalg.eigvalsh(L)
        lam_max = eig[-1] + 1e-08
        L_norm = 2.0 * L / lam_max - jnp.eye(N, dtype=L.dtype)
        xp = jnp.einsum('mn,bnf->bmf', L_norm, x)
        h = xp @ Wc + bc
        h = _layernorm(h, g1, be1)
        h = jax.nn.relu(h)
        x1 = h + x
        q = (x1 @ Wq).reshape(B, N, H, hd).transpose(0, 2, 1, 3)
        k = (x1 @ Wk).reshape(B, N, H, hd).transpose(0, 2, 1, 3)
        v = (x1 @ Wv).reshape(B, N, H, hd).transpose(0, 2, 1, 3)
        scores = jnp.einsum('bhnd,bhmd->bhnm', q, k) / np.sqrt(hd).astype(np.float32)
        scores = jnp.where(adjacency[None, None] > 0, scores, jnp.float32(-1000000000.0))
        attn = jax.nn.softmax(scores, axis=-1)
        o = jnp.einsum('bhnm,bhmd->bhnd', attn, v)
        o = o.transpose(0, 2, 1, 3).reshape(B, N, D)
        o = o @ Wo + bo
        x2 = _layernorm(x1 + o, g2, be2)
        m = jax.nn.gelu(x2 @ W1 + b1, approximate=False) @ W2 + b2
        return _layernorm(x2 + m, g3, be3)

    def _L2_gnn_ref(x, adj, Wg0, bg0, Wg1, bg1, Wih, Whh, bih, bhh):
        import jax, jax.numpy as jnp
        import numpy as np
        B, T, D, H = (64, 2048, 256, 256)
        MAX_SKIP = 4

        def _lstm_last(Wih, Whh, bih, bhh, xs):
            N, _, Hd = xs.shape
            bias = bih + bhh

            def step(carry, x_t):
                h, c = carry
                g = x_t @ Wih.T + h @ Whh.T + bias
                i, f, gg, o = jnp.split(g, 4, axis=-1)
                c = jax.nn.sigmoid(f) * c + jax.nn.sigmoid(i) * jnp.tanh(gg)
                h = jax.nn.sigmoid(o) * jnp.tanh(c)
                return ((h, c), None)
            init = (jnp.zeros((N, Hd), xs.dtype), jnp.zeros((N, Hd), xs.dtype))
            (h_last, _), _ = jax.lax.scan(step, init, jnp.swapaxes(xs, 0, 1))
            return h_last
        h = jax.nn.relu(jnp.einsum('ts,bsh->bth', adj, x @ Wg0 + bg0))
        h = jax.nn.relu(jnp.einsum('ts,bsh->bth', adj, h @ Wg1 + bg1))
        Bv, Tv, Hd = h.shape
        for p in range(1, MAX_SKIP + 1):
            nw = Tv // p
            wins = h[:, :nw * p, :].reshape(Bv * nw, p, Hd)
            last = _lstm_last(Wih[p - 1], Whh[p - 1], bih[p - 1], bhh[p - 1], wins)
            idx = jnp.arange(nw) * p + (p - 1)
            h = h.at[:, idx, :].set(last.reshape(Bv, nw, Hd))
        return h

    def _L3_gnn_ref(h, adj_matrix, W, a):
        import jax, jax.numpy as jnp
        import numpy as np
        ALPHA = 0.2
        Fout = W.shape[1]
        Wh = jnp.einsum('bnf,fo->bno', h, W)
        a1, a2 = (a[:Fout, 0], a[Fout:, 0])
        s1 = Wh @ a1
        s2 = Wh @ a2
        e = s1[:, :, None] + s2[:, None, :]
        e = jnp.where(e >= 0, e, ALPHA * e)
        e = jnp.where(adj_matrix[None] == 0, -jnp.inf, e)
        attention = jax.nn.softmax(e, axis=-1)
        h_prime = jnp.einsum('bij,bjo->bio', attention, Wh)
        return h_prime

    x = _layernorm(x + _L0_gnn_ref(x, adj, L0_gnn_W1, L0_gnn_b1, L0_gnn_g1, L0_gnn_be1, L0_gnn_W2, L0_gnn_b2, L0_gnn_g2, L0_gnn_be2), axis=-1)
    x = _layernorm(x + _L1_gnn_ref(x, adj, adj, L1_gnn_Wc, L1_gnn_bc, L1_gnn_g1, L1_gnn_be1, L1_gnn_Wq, L1_gnn_Wk, L1_gnn_Wv, L1_gnn_Wo, L1_gnn_bo, L1_gnn_g2, L1_gnn_be2, L1_gnn_W1, L1_gnn_b1, L1_gnn_W2, L1_gnn_b2, L1_gnn_g3, L1_gnn_be3), axis=-1)
    x = _layernorm(x + _L2_gnn_ref(x, adj, L2_gnn_Wg0, L2_gnn_bg0, L2_gnn_Wg1, L2_gnn_bg1, L2_gnn_Wih, L2_gnn_Whh, L2_gnn_bih, L2_gnn_bhh), axis=-1)
    x = _layernorm(x + _L3_gnn_ref(x, adj, L3_gnn_W, L3_gnn_a), axis=-1)
    return x


_drawn_inputs = setup_inputs


def setup_inputs(seed=0):
    import zlib

    import numpy as np

    out = dict(_drawn_inputs(seed))
    spreads = {'L0_gnn_b1': (0.0, 0.8),
     'L0_gnn_g1': (1.0, 0.2),
     'L0_gnn_be1': (0.0, 0.1),
     'L0_gnn_b2': (0.0, 0.8),
     'L0_gnn_g2': (1.0, 0.2),
     'L0_gnn_be2': (0.0, 0.1),
     'L1_gnn_bc': (0.0, 0.1),
     'L1_gnn_g1': (1.0, 0.2),
     'L1_gnn_be1': (0.0, 0.1),
     'L1_gnn_bo': (0.0, 0.1),
     'L1_gnn_g2': (1.0, 0.2),
     'L1_gnn_be2': (0.0, 0.1),
     'L1_gnn_b1': (0.0, 0.1),
     'L1_gnn_b2': (0.0, 0.1),
     'L1_gnn_g3': (1.0, 0.2),
     'L1_gnn_be3': (0.0, 0.1),
     'L2_gnn_bg0': (0.0, 0.1),
     'L2_gnn_bg1': (0.0, 0.275)}
    factors = {'L2_gnn_Whh': 4.861, 'L2_gnn_bih': 2.676, 'L2_gnn_bhh': 2.799}
    for name, (base, spread) in spreads.items():
        noise = np.random.default_rng([zlib.crc32(name.encode()), seed]).standard_normal(out[name].shape)
        drawn = base * np.exp(spread * noise) if base else spread * noise
        out[name] = jnp.asarray(drawn.astype(out[name].dtype))
    for name, factor in factors.items():
        out[name] = (out[name] * factor).astype(out[name].dtype)
    return out
```

```python
from contextlib import ExitStack

import concourse.bass as bass
from concourse import mybir

F32 = mybir.dt.float32
F16 = mybir.dt.float16
ALU = mybir.AluOpType
ACT = mybir.ActivationFunctionType
AX = mybir.AxisListType

P = 128
BATCH, NODES, DIM = 128, 64, 256
HID = 2 * DIM
HEADS = 4
HEAD_DIM = DIM // HEADS
GATES = 4 * DIM
SKIPS = 4
KT = DIM // P
HT = HID // P
TILE = 512
BLK = TILE // P
TILE_BATCHES = TILE // NODES
TILES = BATCH * NODES // TILE
STREAMS = 2
ROUNDS = TILES // STREAMS
BANKS = 4
EPS = 1e-5
WSCALE = 256.0
UNSCALE = 1.0 / WSCALE
SQUARINGS = 28
NEG_L1, NEG_OFF, NEG_L3 = -1.0e9, -2.0e9, -1.0e30

WEIGHTS = [("l0_w1", DIM, HID), ("l0_w2", HID, DIM), ("wc", DIM, DIM), ("wq", DIM, DIM), ("wk", DIM, DIM),
           ("wv", DIM, DIM), ("wo", DIM, DIM), ("w1", DIM, HID), ("w2", HID, DIM), ("wg0", DIM, DIM),
           ("wg1", DIM, DIM), ("w3", DIM, DIM)]
WEIGHTS += [(f"wih{p}", DIM, GATES) for p in range(1, SKIPS + 1)]
WEIGHTS += [(f"whh{p}", DIM, GATES) for p in range(2, SKIPS + 1)]
UNIT = 1024


def weight_places():
    at, place = 0, {}
    for name, rows, width in WEIGHTS:
        place[name] = (at, width)
        at += rows // P * width
    return place, at


W_AT, W_COLS = weight_places()
UNITS = W_COLS // UNIT
assert UNITS * UNIT == W_COLS

COLS = [("b1", HT), ("g1", HT), ("be1", HT), ("b2", KT), ("g2", KT), ("be2", KT), ("l1_b1", HT),
        ("bih", SKIPS * GATES // P), ("bhh", SKIPS * GATES // P), ("a", 2 * KT)]
ROWS = ["bc", "g1", "be1", "bo", "g2", "be2", "b2", "g3", "be3", "bg0", "bg1"]


def col_places():
    at, place = 0, {}
    for name, n in COLS:
        place[name] = (at, n)
        at += n
    return place, at


C_AT, C_COLS = col_places()

CELLS = [(1, 0, 0), (1, 0, TILE // 2)]
CELLS += [(p, step, None) for p in range(2, SKIPS + 1) for step in range(p)]
NCELL = len(CELLS)
GATE_I, GATE_F, GATE_G, GATE_O = range(4)
NORMS = 7
LN_L0, LN_G1, LN_G2, LN_G3, LN_L1, LN_L2, LN_L3 = range(NORMS)


def cell_width(c):
    p = CELLS[c][0]
    return TILE // 2 if p == 1 else TILE_BATCHES * (NODES // p)


def cell_tokens(buf, c):
    p, step, first = CELLS[c]
    if first is not None:
        return buf[:, :, first:first + TILE // 2]
    windows = NODES // p
    return buf.rearrange("q k (b t) -> q k b t", t=NODES)[:, :, :, step:step + (windows - 1) * p + 1:p]


def like_cell(ap, c):
    p, _, first = CELLS[c]
    return ap if first is not None else ap.rearrange("q k (b w) -> q k b w", b=TILE_BATCHES)


def is_last_step(c):
    return CELLS[c][1] == CELLS[c][0] - 1


def build(nc, x, adj, adj_t, wpack, w3t, cols, rows, out):
    ctx = ExitStack()
    with ctx:
        def sb(name, shape, dt=F32):
            return ctx.enter_context(nc.sbuf_tensor(name, shape, dt))

        def sem(name):
            return ctx.enter_context(nc.semaphore(name))

        def sems(name):
            return [sem(f"{name}_{s}") for s in range(STREAMS)]

        w_hi = sb("w_hi", [P, W_COLS], F16)
        w_lo = sb("w_lo", [P, W_COLS], F16)
        col = sb("col", [P, C_COLS])
        row = sb("row", [P, len(ROWS), DIM])
        ident = sb("ident", [P, P])
        a_bd = sb("a_bd", [P, P])
        at_bd = sb("at_bd", [P, P])
        gcn_t = sb("gcn_t", [P, P])
        cheb_t = sb("cheb_t", [P, P])
        mask1 = sb("mask1", [P, P])
        mask3 = sb("mask3", [P, P])
        lstm_b = sb("lstm_b", [P, SKIPS * GATES // P])
        wa1 = sb("wa1", [P, 2, KT], F16)
        wa2 = sb("wa2", [P, 2, KT, P], F16)
        bn1 = sb("bn1", [P, 2, HT])
        bn2 = sb("bn2", [P, 2, KT])
        small = sb("small", [P, 64])
        act_in = [sb(f"act_in_{s}", [P, KT, TILE]) for s in range(STREAMS)]
        xa = [sb(f"xa_{s}", [P, BLK, DIM]) for s in range(STREAMS)]
        t = [sb(f"t_{s}", [P, BLK, DIM]) for s in range(STREAMS)]
        x1 = [sb(f"x1_{s}", [P, BLK, DIM]) for s in range(STREAMS)]
        xb = [sb(f"xb_{s}", [P, BLK, DIM]) for s in range(STREAMS)]
        hl_a = [sb(f"hl_a_{s}", [P, 2, KT, TILE], F16) for s in range(STREAMS)]
        hl_b = [sb(f"hl_b_{s}", [P, 2, KT, TILE], F16) for s in range(STREAMS)]
        pool_mem = [sb(f"pool_mem_{s}", [P, 5 * KT * TILE]) for s in range(STREAMS)]
        stats = [sb(f"stats_{s}", [P, BLK, 6]) for s in range(STREAMS)]
        mv = [sb(f"mv_{s}", [P, BLK, 2]) for s in range(STREAMS)]
        ve = [sb(f"ve_{s}", [P, BLK]) for s in range(STREAMS)]
        rstd = [sb(f"rstd_{s}", [P, BLK]) for s in range(STREAMS)]
        nmr = [sb(f"nmr_{s}", [P, BLK]) for s in range(STREAMS)]
        zero = sb("zero", [P, 1])
        hold = sb("hold", [P, 32])
        nhalf = sb("nhalf", [P, 2 * BLK])
        smax = [sb(f"smax_{s}", [P, BLK * HEADS]) for s in range(STREAMS)]
        ssum = [sb(f"ssum_{s}", [P, BLK * HEADS]) for s in range(STREAMS)]
        bnst1 = sb("bnst1", [P, HT, TILES, 6])
        bnst2 = sb("bnst2", [P, KT, TILES, 6])
        ps = [ctx.enter_context(nc.psum_tensor(f"ps_{s}", [P, BANKS, 512], F32)) for s in range(STREAMS)]

        h_dram = nc.dram_tensor("h_scratch", [TILES, P, HT, TILE], F32, kind="Internal").ap()
        o_dram = nc.dram_tensor("o_scratch", [TILES, P, KT, TILE], F32, kind="Internal").ap()
        x_tiles = x.rearrange("(r s b2 b) n d -> r s (b n) b2 d", r=ROUNDS, s=STREAMS, b=P // NODES)
        out_tiles = out.rearrange("(r s b2 b) n d -> r s (b n) b2 d", r=ROUNDS, s=STREAMS, b=P // NODES)
        h_tiles = h_dram.rearrange("(r s) p m n -> r s p m n", s=STREAMS)
        o_tiles = o_dram.rearrange("(r s) p m n -> r s p m n", s=STREAMS)

        def weight(name, k, c0, n):
            at, width = W_AT[name]
            a = at + k * width + c0
            return w_hi[:, a:a + n], w_lo[:, a:a + n]

        def vec(name, m):
            return col[:, C_AT[name][0] + m:C_AT[name][0] + m + 1]

        def vecs(name):
            a, n = C_AT[name]
            return col[:, a:a + n]

        def row_of(name):
            return row[:, ROWS.index(name), :].unsqueeze(1).broadcast_to([P, BLK, DIM])

        def product(o, l, r, first, last):
            nc.tensor.matmul(o, l[0], r[0], start=first, stop=False, skip_group_check=True)
            nc.tensor.matmul(o, l[0], r[1], start=False, stop=False, skip_group_check=True)
            return nc.tensor.matmul(o, l[1], r[0], start=False, stop=last, skip_group_check=True)

        def zeros_like(ap):
            z = zero[:, 0:1]
            while len(z.shape) < len(ap.shape):
                z = z.unsqueeze(1)
            return z.broadcast_to(list(ap.shape))

        def by_token(s, b):
            return ps[s][:, b:b + 2, :].rearrange("p b (c f) -> p (b c) f", f=DIM)

        def by_feature(s, b):
            return ps[s][:, b:b + KT, :]

        used = []

        with ExitStack() as pctx:
            def psem(name):
                used.append(pctx.enter_context(nc.semaphore(name)))
                return used[-1]

            zeroed = psem("zeroed")
            adj_in = psem("adj_in")
            vec_in = psem("vec_in")
            w_in = [psem(f"w_in_{b}") for b in range(2)]
            unit_hi = psem("unit_hi")
            unit_lo = psem("unit_lo")
            ident_ok = psem("ident_ok")
            step = psem("step")
            pow_ok = psem("pow_ok")
            gcn_ps = psem("gcn_ps")
            sq_ps = psem("sq_ps")
            sq_ready = psem("sq_ready")
            lam_ps = psem("lam_ps")
            wa_ps = psem("wa_ps")
            stage = [act_in[b][:, :, :].rearrange("p k n -> p (k n)") for b in range(2)]
            w3t_sb = xa[0]
            ones = x1[0][:, 0, 0:P]
            scaled = x1[0][:, 1, 0:P]
            sym = x1[0][0:NODES, 2, 0:NODES]
            powr = x1[0][0:NODES, 3, 0:NODES]
            junk = x1[1][0:NODES, 0, 0:NODES]
            junk_full = x1[1][:, 1, 0:P]
            tr_part = small[0:NODES, 0:1]
            inv_tr = small[0:NODES, 1:2]
            lam_part = small[0:NODES, 2:4]
            rsum, csum, diag, deg, dinv = (small[:, 8 + j:9 + j] for j in range(5))
            lam_r, lam_c = small[:, 13:14], small[:, 14:15]
            lam_v = small[:, 16:18]
            wa_f = small[:, 20:20 + 2 * KT]
            SQ = ps[0][0:NODES, 0, 0:NODES]
            TR = ps[0][:, 1, 0:1]
            LAM = ps[0][:, 2, 0:2]
            GCN = ps[0][:, 3, 0:P]
            WA = ps[1][:, 0, 0:2 * KT]

            block = pctx.enter_context(nc.Block())

            @block.sync
            def _(sp):
                sp.wait_ge(zeroed, 2)
                for b in range(2):
                    d = slice(b * NODES, (b + 1) * NODES)
                    sp.dma_start(a_bd[d, d], adj).then_inc(adj_in, 16)
                    sp.dma_start(at_bd[d, d], adj_t).then_inc(adj_in, 16)
                sp.dma_start(col[:, :], cols).then_inc(vec_in, 16)
                sp.dma_start(w3t_sb[:, 0:KT, :], w3t).then_inc(vec_in, 16)
                sp.dma_start(row[:, :, :], rows.partition_broadcast(P)).then_inc(vec_in, 16)
                for b in range(2):
                    sp.dma_start(stage[b], wpack[:, bass.ts(b, UNIT)]).then_inc(w_in[b], 16)
                with sp.Fori(1, UNITS // 2) as u:
                    for b in range(2):
                        sp.wait_ge(unit_lo, u * 2 + b - 1)
                        sp.dma_start(stage[b], wpack[:, bass.ds(u * (2 * UNIT) + b * UNIT, UNIT)]).then_inc(w_in[b], 16)

            @block.gpsimd
            def _(pool):
                nc.gpsimd.memset(a_bd[:, :], 0.0).then_inc(zeroed, 1)
                nc.gpsimd.memset(at_bd[:, :], 0.0).then_inc(zeroed, 1)
                nc.gpsimd.memset(ident[:, :], 0.0).then_inc(ident_ok, 1)
                nc.gpsimd.memset(ones, 1.0).then_inc(ident_ok, 1)
                nc.gpsimd.memset(nhalf[:, :], -0.5).then_inc(ident_ok, 1)
                nc.gpsimd.memset(zero[:, :], 0.0).then_inc(ident_ok, 1)
                pool.wait_ge(ident_ok, 4)
                nc.gpsimd.affine_select(out=ident[:, :], in_=ident[:, :], compare_op=ALU.not_equal, fill=1.0, base=0,
                                        pattern=[[-1, P]], channel_multiplier=1).then_inc(ident_ok, 1)
                pool.wait_ge(step, 5)
                nc.gpsimd.tensor_tensor(dinv, deg, nhalf[:, 0:1], ALU.pow).then_inc(pow_ok, 1)

            @block.scalar
            def _(act):
                with act.Fori(0, UNITS // 2) as u:
                    for b in range(2):
                        act.wait_ge(w_in[b], u * 16 + 16)
                        nc.scalar.activation(w_hi[:, bass.ds(u * (2 * UNIT) + b * UNIT, UNIT)], stage[b], ACT.Copy,
                                             scale=WSCALE).then_inc(unit_hi, 1)

            @block.tensor
            def _(pe):
                pe.wait_ge(step, 6)
                pe.wait_ge(ident_ok, 5)
                nc.tensor.transpose(GCN, scaled, ident[:, :]).then_inc(gcn_ps, 1)
                pe.wait_ge(vec_in, 48)
                for half in range(2):
                    for kt in range(KT):
                        for ot in range(KT):
                            mm = nc.tensor.matmul(WA[:, half * KT + kt:half * KT + kt + 1],
                                                  w3t_sb[:, ot, kt * P:(kt + 1) * P],
                                                  vec("a", half * KT + ot), start=(ot == 0), stop=(ot == KT - 1))
                mm.then_inc(wa_ps, 1)
                with pe.Fori(0, SQUARINGS) as k:
                    pe.wait_ge(sq_ready, k * 2 + 2)
                    nc.tensor.matmul(TR, ones[0:NODES, :], tr_part, start=True, stop=True)
                    nc.tensor.matmul(SQ, powr, powr, start=True, stop=True).then_inc(sq_ps, 1)
                pe.wait_ge(sq_ready, 2 * SQUARINGS + 3)
                nc.tensor.matmul(LAM, ones[0:NODES, :], lam_part, start=True, stop=True).then_inc(lam_ps, 1)

            @block.vector
            def _(dve):
                dve.wait_ge(adj_in, 64)
                dve.wait_ge(ident_ok, 5)
                nc.vector.reduce_sum(rsum, a_bd[:, :], axis=AX.X).then_inc(step, 1)
                nc.vector.reduce_sum(csum, at_bd[:, :], axis=AX.X).then_inc(step, 1)
                nc.vector.tensor_tensor_reduce(junk_full, a_bd[:, :], ident[:, :], 1.0, 0.0, ALU.mult, ALU.add,
                                               diag).then_inc(step, 1)
                dve.wait_ge(step, 3)
                nc.vector.scalar_tensor_tensor(deg, rsum, 1.0, csum, ALU.add, ALU.add).then_inc(step, 1)
                dve.wait_ge(step, 4)
                nc.vector.tensor_tensor(deg, deg, diag, ALU.subtract).then_inc(step, 1)
                dve.wait_ge(pow_ok, 1)
                nc.vector.tensor_tensor(junk_full, a_bd[:, :], ident[:, :], ALU.add).then_inc(sq_ready, 1)
                dve.wait_ge(sq_ready, 1)
                nc.vector.tensor_scalar(scaled, junk_full, dinv, None, ALU.mult).then_inc(step, 1)
                dve.wait_ge(gcn_ps, 1)
                nc.vector.tensor_scalar(gcn_t[:, :], GCN, dinv, None, ALU.mult).then_inc(step, 1)
                nc.vector.tensor_scalar(mask1[:, :], a_bd[:, :], 0.0, NEG_L1, ALU.is_le, ALU.mult).then_inc(step, 1)
                nc.vector.tensor_scalar(mask3[:, :], a_bd[:, :], 0.0, NEG_L3, ALU.is_equal, ALU.mult).then_inc(step, 1)
                dve.wait_ge(step, 9)
                nc.vector.memset(mask1[0:NODES, NODES:P], NEG_OFF).then_inc(step, 1)
                nc.vector.memset(mask1[NODES:P, 0:NODES], NEG_OFF).then_inc(step, 1)
                dve.wait_ge(vec_in, 48)
                nc.vector.tensor_tensor(lstm_b[:, :], vecs("bih"), vecs("bhh"), ALU.add).then_inc(step, 1)
                dve.wait_ge(wa_ps, 1)
                nc.vector.tensor_scalar(wa_f, WA, WSCALE, None, ALU.mult).then_inc(step, 1)
                dve.wait_ge(step, 13)
                nc.vector.tensor_copy(wa1[:, 0, :], wa_f[:, 0:KT]).then_inc(step, 1)
                nc.vector.tensor_copy(wa2[:, 0, :, :], wa_f[:, KT:2 * KT].unsqueeze(2).broadcast_to([P, KT, P]))\
                    .then_inc(step, 1)
                dve.wait_ge(step, 15)
                nc.vector.tensor_tensor(wa1[:, 1, :], wa_f[:, 0:KT], wa1[:, 0, :], ALU.subtract).then_inc(step, 1)
                nc.vector.tensor_tensor(wa2[:, 1, :, :], wa_f[:, KT:2 * KT].unsqueeze(2).broadcast_to([P, KT, P]),
                                        wa2[:, 0, :, :], ALU.subtract).then_inc(step, 1)
                nc.vector.tensor_tensor(sym, a_bd[0:NODES, 0:NODES], at_bd[0:NODES, 0:NODES], ALU.add).then_inc(step, 1)
                dve.wait_ge(step, 18)
                nc.vector.tensor_scalar(sym, sym, 0.5, None, ALU.mult).then_inc(step, 1)
                dve.wait_ge(step, 19)
                nc.vector.tensor_copy(powr, sym).then_inc(step, 1)
                dve.wait_ge(step, 20)
                nc.vector.tensor_tensor_reduce(junk, powr, powr, 1.0, 0.0, ALU.mult, ALU.add, tr_part)\
                    .then_inc(sq_ready, 1)
                with dve.Fori(0, SQUARINGS) as k:
                    dve.wait_ge(sq_ps, k + 1)
                    nc.vector.reciprocal(inv_tr, TR[0:NODES, :]).then_inc(step, 1)
                    dve.wait_ge(step, k + 21)
                    nc.vector.tensor_scalar(powr, SQ, inv_tr, None, ALU.mult).then_inc(sq_ready, 1)
                    dve.wait_ge(sq_ready, k * 2 + 3)
                    nc.vector.tensor_tensor_reduce(junk, powr, powr, 1.0, 0.0, ALU.mult, ALU.add, tr_part)\
                        .then_inc(sq_ready, 1)
                dve.wait_ge(sq_ready, 2 * SQUARINGS + 2)
                nc.vector.tensor_tensor_reduce(junk, sym, powr, 1.0, 0.0, ALU.mult, ALU.add, lam_part[:, 0:1])\
                    .then_inc(pow_ok, 1)
                dve.wait_ge(pow_ok, 2)
                nc.vector.tensor_tensor_reduce(junk, ident[0:NODES, 0:NODES], powr, 1.0, 0.0, ALU.mult, ALU.add,
                                               lam_part[:, 1:2]).then_inc(sq_ready, 1)
                dve.wait_ge(lam_ps, 1)
                nc.vector.tensor_copy(lam_v, LAM).then_inc(pow_ok, 1)
                dve.wait_ge(pow_ok, 3)
                nc.vector.reciprocal(lam_r, lam_v[:, 1:2]).then_inc(pow_ok, 1)
                dve.wait_ge(pow_ok, 4)
                nc.vector.tensor_scalar(lam_c, lam_v[:, 0:1], lam_r, 1e-8, ALU.mult, ALU.add).then_inc(pow_ok, 1)
                dve.wait_ge(pow_ok, 5)
                nc.vector.reciprocal(lam_r, lam_c).then_inc(pow_ok, 1)
                dve.wait_ge(pow_ok, 6)
                nc.vector.tensor_scalar(lam_c, lam_r, 2.0, None, ALU.mult).then_inc(pow_ok, 1)
                dve.wait_ge(pow_ok, 7)
                nc.vector.scalar_tensor_tensor(cheb_t[:, :], at_bd[:, :], lam_c, ident[:, :], ALU.mult, ALU.subtract)\
                    .then_inc(pow_ok, 1)
                with dve.Fori(0, UNITS // 2) as u:
                    for b in range(2):
                        part = bass.ds(u * (2 * UNIT) + b * UNIT, UNIT)
                        dve.wait_ge(unit_hi, u * 2 + b + 1)
                        nc.vector.scalar_tensor_tensor(w_lo[:, part], stage[b], WSCALE, w_hi[:, part], ALU.mult,
                                                       ALU.subtract).then_inc(unit_lo, 1)

        with ExitStack() as pctx:
            def psems(name):
                used.extend(pctx.enter_context(nc.semaphore(f"{name}_{s}")) for s in range(STREAMS))
                return used[-STREAMS:]

            x_in, agg_ps, agg_hi, agg_lo, hid_ps, hid_out, hid_stats, hid_stored = (
                psems(n) for n in ("p1_x_in", "agg_ps", "agg_hi", "agg_lo", "hid_ps", "hid_out", "hid_stats", "hid_stored"))
            hid = [pool_mem[s][:, 0:HT * TILE].rearrange("p (m n) -> p m n", m=HT) for s in range(STREAMS)]
            bn_step, bn_pow = psems("bn1")
            block = pctx.enter_context(nc.Block())

            @block.sync
            def _(sp):
                def store(s, n):
                    sp.wait_ge(hid_out[s], n * HT + 1)
                    sp.dma_start(h_tiles[bass.ds(n - 1, 1), s].rearrange("o p m n -> (o p) m n"), hid[s])\
                        .then_inc(hid_stored[s], 16)

                for s in range(STREAMS):
                    sp.dma_start(xa[s][:, :, :], x_tiles[0, s]).then_inc(x_in[s], 16)
                with sp.Fori(1, ROUNDS) as r:
                    for s in range(STREAMS):
                        sp.wait_ge(agg_ps[s], r)
                        sp.dma_start(xa[s][:, :, :], x_tiles[bass.ds(r, 1), s].rearrange("o p b d -> (o p) b d"))\
                            .then_inc(x_in[s], 16)
                    for s in range(STREAMS):
                        store(s, r)
                for s in range(STREAMS):
                    store(s, ROUNDS)
                for s in range(STREAMS):
                    sp.wait_ge(hid_stored[s], 16 * ROUNDS + 1)

            @block.tensor
            def _(pe):
                def aggregate(s, n):
                    pe.wait_ge(x_in[s], n * 16)
                    pe.wait_ge(hid_out[s], n * HT - HT + 1)
                    for f in range(KT):
                        for b in range(BLK):
                            mm = nc.tensor.matmul(ps[s][:, f, b * P:(b + 1) * P], xa[s][:, b, f * P:(f + 1) * P],
                                                  gcn_t[:, :], start=True, stop=True)
                    mm.then_inc(agg_ps[s], 1)

                def hidden(s, n):
                    pe.wait_ge(agg_lo[s], n)
                    agg = hl_a[s]
                    for m in range(HT):
                        bank = (m + 2) % BANKS
                        for k in range(KT):
                            mm = product(ps[s][:, bank, :], weight("l0_w1", k, m * P, P),
                                         (agg[:, 0, k, :], agg[:, 1, k, :]), k == 0, k == KT - 1)
                        mm.then_inc(hid_ps[s], 1)

                with pe.Fori(0, ROUNDS) as r:
                    for s in range(STREAMS):
                        aggregate(s, r + 1)
                    for s in range(STREAMS):
                        hidden(s, r + 1)

            @block.scalar
            def _(act):
                for s in range(STREAMS):
                    nc.scalar.activation(small[:, 40 + s:41 + s], ident[:, 0:1], ACT.Copy).then_inc(hid_out[s], 1)

                def agg_high(s, n):
                    act.wait_ge(agg_ps[s], n)
                    nc.scalar.copy(hl_a[s][:, 0, :, :], by_feature(s, 0)).then_inc(agg_hi[s], 1)

                def hid_bias(s, n):
                    act.wait_ge(hid_stored[s], n * 16 - 15)
                    act.wait_ge(hid_stats[s], n)
                    for m in range(HT):
                        act.wait_ge(hid_ps[s], n * HT - (HT - 1 - m))
                        nc.scalar.activation(hid[s][:, m, :], ps[s][:, (m + 2) % BANKS, :], ACT.Identity,
                                             bias=vec("b1", m), scale=UNSCALE).then_inc(hid_out[s], 1)

                with act.Fori(0, ROUNDS) as r:
                    for s in range(STREAMS):
                        agg_high(s, r + 1)
                    for s in range(STREAMS):
                        hid_bias(s, r + 1)

            @block.vector
            def _(dve):
                for s in range(STREAMS):
                    nc.vector.memset(small[:, 42 + s:43 + s], 0.0).then_inc(hid_stats[s], 1)
                    nc.vector.memset(small[:, 44 + s:45 + s], 0.0).then_inc(hid_stored[s], 1)

                def agg_low(s, n):
                    dve.wait_ge(agg_hi[s], n)
                    nc.vector.tensor_tensor(hl_a[s][:, 1, :, :], by_feature(s, 0), hl_a[s][:, 0, :, :], ALU.subtract)\
                        .then_inc(agg_lo[s], 1)

                def hid_stat(s, r):
                    for m in range(HT):
                        dve.wait_ge(hid_out[s], r * HT + m + 2)
                        st = nc.vector.bn_stats(bnst1[:, m, bass.ds(r * STREAMS + s, 1), :]
                                                .rearrange("p o c -> p (o c)"), hid[s][:, m, :])
                    st.then_inc(hid_stats[s], 1)

                with dve.Fori(0, ROUNDS) as r:
                    for s in range(STREAMS):
                        agg_low(s, r + 1)
                    for s in range(STREAMS):
                        hid_stat(s, r)
                for s in range(STREAMS):
                    dve.wait_ge(hid_stats[s], ROUNDS + 1)
                for m in range(HT):
                    nc.vector.bn_aggr(small[:, 2 * m:2 * m + 2], bnst1[:, m, :, :].rearrange("p t c -> p (t c)"))\
                        .then_inc(bn_step, 1)
                m_v = small[:, 0:2 * HT].rearrange("p (m c) -> p m c", c=2)
                dve.wait_ge(bn_step, HT)
                nc.vector.tensor_scalar(small[:, 16:16 + HT], m_v[:, :, 1], EPS, None, ALU.add).then_inc(bn_step, 1)
                dve.wait_ge(bn_pow, 1)
                nc.vector.tensor_tensor(bn1[:, 0, :], vecs("g1"), small[:, 24:24 + HT], ALU.mult).then_inc(bn_step, 1)
                dve.wait_ge(bn_step, HT + 2)
                nc.vector.tensor_tensor(small[:, 32:32 + HT], m_v[:, :, 0], bn1[:, 0, :], ALU.mult).then_inc(bn_step, 1)
                dve.wait_ge(bn_step, HT + 3)
                nc.vector.tensor_tensor(bn1[:, 1, :], vecs("be1"), small[:, 32:32 + HT], ALU.subtract).then_inc(bn_step, 1)

            @block.gpsimd
            def _(pool):
                pool.wait_ge(bn_step, HT + 1)
                nc.gpsimd.tensor_tensor(small[:, 24:24 + HT], small[:, 16:16 + HT], nhalf[:, 0:HT], ALU.pow)\
                    .then_inc(bn_pow, 1)

        with ExitStack() as pctx:
            def psems(name):
                return [pctx.enter_context(nc.semaphore(f"{name}_{s}")) for s in range(STREAMS)]

            h_in, rel, rel_hi, rel_lo, o_ps, o_out, o_stats, o_stored = (
                psems(n) for n in ("h_in", "rel", "rel_hi", "rel_lo", "o_ps", "o_out", "o_stats", "o_stored"))
            hid = [pool_mem[s][:, 0:HT * TILE].rearrange("p (m n) -> p m n", m=HT) for s in range(STREAMS)]
            hl = [[hl_a[s], hl_b[s]] for s in range(STREAMS)]
            bn_step = pctx.enter_context(nc.semaphore("bn2_step"))
            bn_pow = pctx.enter_context(nc.semaphore("bn2_pow"))
            block = pctx.enter_context(nc.Block())

            @block.sync
            def _(sp):
                for done in used:
                    sp.sem_clear(done)

                def store(s, n):
                    sp.wait_ge(o_out[s], n * KT + 1)
                    sp.dma_start(o_tiles[bass.ds(n - 1, 1), s].rearrange("o p m n -> (o p) m n"), act_in[s][:, :, :])\
                        .then_inc(o_stored[s], 16)

                for s in range(STREAMS):
                    sp.dma_start(hid[s], h_tiles[0, s]).then_inc(h_in[s], 16)
                with sp.Fori(1, ROUNDS) as r:
                    for s in range(STREAMS):
                        sp.wait_ge(rel_lo[s], r * HT)
                        sp.dma_start(hid[s], h_tiles[bass.ds(r, 1), s].rearrange("o p m n -> (o p) m n"))\
                            .then_inc(h_in[s], 16)
                    for s in range(STREAMS):
                        store(s, r)
                for s in range(STREAMS):
                    store(s, ROUNDS)
                for s in range(STREAMS):
                    sp.wait_ge(o_stored[s], 16 * ROUNDS + 1)

            @block.scalar
            def _(act):
                def relu(s, n):
                    act.wait_ge(h_in[s], n * 16)
                    for m in range(HT):
                        nc.scalar.activation(hid[s][:, m, :], hid[s][:, m, :], ACT.Relu, bias=bn1[:, 1, m:m + 1],
                                             scale=bn1[:, 0, m:m + 1]).then_inc(rel[s], 1)

                def out_bias(s, n):
                    act.wait_ge(o_ps[s], n + 1)
                    act.wait_ge(o_stored[s], n * 16 - 15)
                    act.wait_ge(o_stats[s], n)
                    for m in range(KT):
                        nc.scalar.activation(act_in[s][:, m, :], ps[s][:, m, :], ACT.Identity, bias=vec("b2", m),
                                             scale=UNSCALE).then_inc(o_out[s], 1)

                for s in range(STREAMS):
                    nc.scalar.activation(small[:, 40 + s:41 + s], ident[:, 0:1], ACT.Copy).then_inc(o_out[s], 1)
                with act.Fori(0, ROUNDS) as r:
                    for s in range(STREAMS):
                        relu(s, r + 1)
                    for s in range(STREAMS):
                        out_bias(s, r + 1)

            @block.gpsimd
            def _(pool):
                def high(s, n):
                    pool.wait_ge(o_ps[s], n)
                    for m in range(HT):
                        pool.wait_ge(rel[s], n * HT - (HT - 1 - m))
                        nc.gpsimd.tensor_tensor(hl[s][m // KT][:, 0, m % KT, :], hid[s][:, m, :],
                                                zero[:, 0:1].broadcast_to([P, TILE]), ALU.add).then_inc(rel_hi[s], 1)

                with pool.Fori(0, ROUNDS) as r:
                    for s in range(STREAMS):
                        high(s, r + 1)
                pool.wait_ge(bn_step, KT + 1)
                nc.gpsimd.tensor_tensor(small[:, 24:24 + KT], small[:, 16:16 + KT], nhalf[:, 0:KT], ALU.pow)\
                    .then_inc(bn_pow, 1)

            @block.vector
            def _(dve):
                for s in range(STREAMS):
                    nc.vector.memset(small[:, 42 + s:43 + s], 0.0).then_inc(o_stats[s], 1)
                    nc.vector.memset(small[:, 44 + s:45 + s], 0.0).then_inc(o_stored[s], 1)
                    nc.vector.memset(small[:, 46 + s:47 + s], 0.0).then_inc(o_ps[s], 1)

                def low(s, n):
                    for m in range(HT):
                        dve.wait_ge(rel_hi[s], n * HT - (HT - 1 - m))
                        nc.vector.tensor_tensor(hl[s][m // KT][:, 1, m % KT, :], hid[s][:, m, :],
                                                hl[s][m // KT][:, 0, m % KT, :], ALU.subtract).then_inc(rel_lo[s], 1)

                def out_stat(s, r):
                    for m in range(KT):
                        dve.wait_ge(o_out[s], r * KT + m + 2)
                        st = nc.vector.bn_stats(bnst2[:, m, bass.ds(r * STREAMS + s, 1), :]
                                                .rearrange("p o c -> p (o c)"), act_in[s][:, m, :])
                    st.then_inc(o_stats[s], 1)

                with dve.Fori(0, ROUNDS) as r:
                    for s in range(STREAMS):
                        low(s, r + 1)
                    for s in range(STREAMS):
                        out_stat(s, r)
                for s in range(STREAMS):
                    dve.wait_ge(o_stats[s], ROUNDS + 1)
                for m in range(KT):
                    nc.vector.bn_aggr(small[:, 2 * m:2 * m + 2], bnst2[:, m, :, :].rearrange("p t c -> p (t c)"))\
                        .then_inc(bn_step, 1)
                m_v = small[:, 0:2 * KT].rearrange("p (m c) -> p m c", c=2)
                dve.wait_ge(bn_step, KT)
                nc.vector.tensor_scalar(small[:, 16:16 + KT], m_v[:, :, 1], EPS, None, ALU.add).then_inc(bn_step, 1)
                dve.wait_ge(bn_pow, 1)
                nc.vector.tensor_tensor(bn2[:, 0, :], vecs("g2"), small[:, 24:24 + KT], ALU.mult).then_inc(bn_step, 1)
                dve.wait_ge(bn_step, KT + 2)
                nc.vector.tensor_tensor(small[:, 32:32 + KT], m_v[:, :, 0], bn2[:, 0, :], ALU.mult).then_inc(bn_step, 1)
                dve.wait_ge(bn_step, KT + 3)
                nc.vector.tensor_tensor(bn2[:, 1, :], vecs("be2"), small[:, 32:32 + KT], ALU.subtract).then_inc(bn_step, 1)

            @block.tensor
            def _(pe):
                def second(s, n):
                    pe.wait_ge(o_out[s], n * KT - KT + 1)
                    for k in range(HT):
                        pe.wait_ge(rel_lo[s], n * HT - (HT - 1 - k))
                        half = hl[s][k // KT]
                        for m in range(KT):
                            mm = product(ps[s][:, m, :], weight("l0_w2", k, m * P, P),
                                         (half[:, 0, k % KT, :], half[:, 1, k % KT, :]), k == 0, k == HT - 1)
                    mm.then_inc(o_ps[s], 1)

                with pe.Fori(0, ROUNDS) as r:
                    for s in range(STREAMS):
                        second(s, r + 1)

        with ExitStack() as pctx:
            def psems(name):
                return [pctx.enter_context(nc.semaphore(f"{name}_{s}")) for s in range(STREAMS)]

            x_in, o_in, out_stored, banks_free = (psems(n) for n in ("x_in", "o_in", "out_stored", "banks_free"))
            y_ok, y_ps = psems("y_ok"), psems("y_ps")
            t_ok, ln_stats, ln_mv, ln_ve, ln_rstd, ln_nmr, ln_out = (
                psems(n) for n in ("t_ok", "ln_stats", "ln_mv", "ln_ve", "ln_rstd", "ln_nmr", "ln_out"))
            feat_ps, feat_hi, feat_lo = psems("feat_ps"), psems("feat_hi"), psems("feat_lo")
            hc_ps, wo_ps, w2_ps, wg_ps, wg_ok = (psems(n) for n in ("hc_ps", "wo_ps", "w2_ps", "wg_ps", "wg_ok"))
            scaled_ok, shifted_ok, pre_ok, x1_ok, x2_ok = (
                psems(n) for n in ("scaled_ok", "shifted_ok", "pre_ok", "x1_ok", "x2_ok"))
            q_ps, k_ps, v_ps, q_ok, k_ok, v_ok = (psems(n) for n in ("q_ps", "k_ps", "v_ps", "q_ok", "k_ok", "v_ok"))
            score_ps, masked_ok, nmax_ok, exp_ok, inv_ok, prob_ok, prob_ps, prob_t = (
                psems(n) for n in ("score_ps", "masked_ok", "nmax_ok", "exp_ok", "inv_ok", "prob_ok", "prob_ps", "prob_t"))
            w1_ps, gelu_ok, gelu_hi, gelu_lo = (psems(n) for n in ("w1_ps", "gelu_ok", "gelu_hi", "gelu_lo"))
            gate_ps, gate_ok, ig_ok, fc_ok, c_ok, tanh_ok, h_ok, h_hi, h_lo = (
                psems(n) for n in ("gate_ps", "gate_ok", "ig_ok", "fc_ok", "c_ok", "tanh_ok", "h_ok", "h_hi", "h_lo"))
            hf_ps, wh_ps, wh_ok, s_ps, s1_ok, e_ok, lrelu_ok, emask_ok, enmax_ok, eexp_ok, einv_ok, att_ps, att_t, av_ps = (
                psems(n) for n in ("hf_ps", "wh_ps", "wh_ok", "s_ps", "s1_ok", "e_ok", "lrelu_ok", "emask_ok", "enmax_ok",
                                   "eexp_ok", "einv_ok", "att_ps", "att_t", "av_ps"))

            XP, X1T, OT, X2T, XBT, H0, H1, XCT = range(8)
            FEATS = 8
            feat_dst = [hl_a, hl_b, hl_a, hl_b, hl_a, hl_b, hl_a, hl_b]
            feat_bank = [2, 2, 0, 0, 0, 0, 0, 2]
            feat_relu = [H0, H1]
            SCORE_BANK = [2, 3, 0, 1]
            HID_BANK = [2, 3, 0, 1]

            def at(n, each, j):
                return n * each - (each - 1 - j)

            GATE_LIST = [[GATE_I, GATE_G, GATE_O] if CELLS[c][1] == 0 else [GATE_I, GATE_G, GATE_F, GATE_O]
                         for c in range(NCELL)]
            GATE_AT = [sum(len(g) for g in GATE_LIST[:c]) for c in range(NCELL)]
            NGATE = sum(len(g) for g in GATE_LIST)
            STEPPED = [c for c in range(NCELL) if CELLS[c][1] > 0]

            def score(s, b, h):
                c = (b % 2 * 2 + h // 2) * P
                return ps[s][:, SCORE_BANK[b // 2 * 2] + h % 2, c:c + P]

            def gate_at(n, c, j):
                return at(n, NGATE, GATE_AT[c] + j)

            mem = pool_mem
            q = [m[:, 0:1024].rearrange("p (k n) -> p k n", k=KT) for m in mem]
            kk = [m[:, 1024:2048].rearrange("p (k n) -> p k n", k=KT) for m in mem]
            prob_tr = [m[:, 0:2048].rearrange("p (b h n) -> p b h n", b=BLK, h=HEADS) for m in mem]
            vv = [m[:, 2048:3072].rearrange("p (b d) -> p b d", b=BLK) for m in mem]
            prob = [m[:, 3072:5120].rearrange("p (b h n) -> p b h n", b=BLK, h=HEADS) for m in mem]
            gelu = [m[:, 0:2048].rearrange("p (m n) -> p m n", m=HT) for m in mem]
            gelu_hl = [m[:, 2048:4096].bitcast(F16).rearrange("p (c m n) -> p c m n", c=2, m=HT) for m in mem]
            wg = [m[:, 0:1024].rearrange("p (b d) -> p b d", b=BLK) for m in mem]
            gates = [m[:, 0:2048].rearrange("p (g n) -> p g n", g=4) for m in mem]
            cell_c = [m[:, 2048:2560] for m in mem]
            cell_t = [m[:, 2560:3072] for m in mem]
            cell_h = [m[:, 3072:3584] for m in mem]
            cell_hl = [m[:, 3584:4096].bitcast(F16).rearrange("p (c n) -> p c n", c=2) for m in mem]
            state = [m[:, 4096:5120].rearrange("p (k n) -> p k n", k=KT) for m in mem]
            state_hl = feat_dst[H1]
            wh = [m[:, 0:1024].rearrange("p (b d) -> p b d", b=BLK) for m in mem]
            logit = [m[:, 1024:1536].rearrange("p (b n) -> p b n", b=BLK) for m in mem]
            att = [m[:, 1536:2048].rearrange("p (b n) -> p b n", b=BLK) for m in mem]
            att_tr = [m[:, 2048:2560].rearrange("p (b n) -> p b n", b=BLK) for m in mem]
            s1 = [small[:, 8 + BLK * s:8 + BLK * s + BLK] for s in range(STREAMS)]
            xc = x1

            block = pctx.enter_context(nc.Block())

            @block.sync
            def _(sp):
                def load_o(s, r):
                    sp.dma_start(act_in[s][:, :, :], o_tiles[bass.ds(r, 1), s].rearrange("o p m n -> (o p) m n"))\
                        .then_inc(o_in[s], 16)

                def load_x(s, r):
                    sp.dma_start(xa[s][:, :, :], x_tiles[bass.ds(r, 1), s].rearrange("o p b d -> (o p) b d"))\
                        .then_inc(x_in[s], 16)

                def store(s, n):
                    sp.wait_ge(ln_out[s], at(n, NORMS, LN_L3))
                    sp.dma_start(out_tiles[bass.ds(n - 1, 1), s].rearrange("o p b d -> (o p) b d"), xb[s][:, :, :])\
                        .then_inc(out_stored[s], 16)

                for s in range(STREAMS):
                    load_o(s, 0)
                    load_x(s, 0)
                with sp.Fori(1, ROUNDS) as r:
                    for s in range(STREAMS):
                        sp.wait_ge(y_ps[s], r)
                        load_o(s, r)
                    for s in range(STREAMS):
                        sp.wait_ge(pre_ok[s], r * 3)
                        load_x(s, r)
                    for s in range(STREAMS):
                        store(s, r)
                for s in range(STREAMS):
                    store(s, ROUNDS)
                for s in range(STREAMS):
                    sp.wait_ge(out_stored[s], 16 * ROUNDS + 1)

            @block.tensor
            def _(pe):
                def turn_y(s, n):
                    pe.wait_ge(banks_free[s], n)
                    pe.wait_ge(y_ok[s], n * KT)
                    for f in range(KT):
                        for b in range(BLK):
                            mm = nc.tensor.transpose(by_token(s, 0)[:, b, f * P:(f + 1) * P],
                                                     act_in[s][:, f, b * P:(b + 1) * P], ident[:, :])
                    mm.then_inc(y_ps[s], 1)

                def chebyshev(s, n):
                    pe.wait_ge(ln_out[s], at(n, NORMS, LN_L0))
                    for f in range(KT):
                        for b in range(BLK):
                            mm = nc.tensor.matmul(by_feature(s, feat_bank[XP])[:, f, b * P:(b + 1) * P],
                                                  xa[s][:, b, f * P:(f + 1) * P], cheb_t[:, :], start=True, stop=True)
                    mm.then_inc(feat_ps[s], 1)

                def dense(s, src, name, bank):
                    kts = src.shape[2]
                    for b in range(BLK):
                        for k in range(kts):
                            mm = product(by_token(s, bank)[:, b, :],
                                         (src[:, 0, k, b * P:(b + 1) * P], src[:, 1, k, b * P:(b + 1) * P]),
                                         weight(name, k, 0, DIM), k == 0, k == kts - 1)
                    return mm

                def conv(s, n):
                    pe.wait_ge(feat_lo[s], at(n, FEATS, XP))
                    dense(s, hl_a[s][:, :, :, :], "wc", 0).then_inc(hc_ps[s], 1)

                def turn(s, src, j):
                    for f in range(KT):
                        for b in range(BLK):
                            mm = nc.tensor.transpose(by_feature(s, feat_bank[j])[:, f, b * P:(b + 1) * P],
                                                     src[s][:, b, f * P:(f + 1) * P], ident[:, :])
                    mm.then_inc(feat_ps[s], 1)

                def turn_x1(s, n):
                    pe.wait_ge(x1_ok[s], n)
                    turn(s, x1, X1T)

                def qkv(s, n):
                    pe.wait_ge(feat_lo[s], at(n, FEATS, X1T))
                    src = hl_b[s]
                    for name, bank, done in (("wq", 0, q_ps), ("wk", 2, k_ps)):
                        for m in range(KT):
                            for k in range(KT):
                                mm = product(ps[s][:, bank + m, :], weight(name, k, m * P, P),
                                             (src[:, 0, k, :], src[:, 1, k, :]), k == 0, k == KT - 1)
                        mm.then_inc(done[s], 1)
                    pe.wait_ge(q_ok[s], n)
                    dense(s, src[:, :, :, :], "wv", 0).then_inc(v_ps[s], 1)

                def scores(s, n):
                    pe.wait_ge(k_ok[s], n)
                    for b in range(BLK):
                        if b == 2:
                            pe.wait_ge(v_ok[s], n)
                        for h in range(HEADS):
                            d = slice(h % 2 * HEAD_DIM, h % 2 * HEAD_DIM + HEAD_DIM)
                            mm = nc.tensor.matmul(score(s, b, h), q[s][d, h // 2, b * P:(b + 1) * P],
                                                  kk[s][d, h // 2, b * P:(b + 1) * P], start=True, stop=True)
                            if b % 2 == 1 and h >= HEADS - 2:
                                mm.then_inc(score_ps[s], 1)

                def turn_probs(s, n):
                    for b in range(BLK):
                        if b % 2 == 0:
                            pe.wait_ge(masked_ok[s], at(n, BLK, b + 1))
                        pe.wait_ge(prob_ok[s], at(n, BLK, b))
                        for h in range(HEADS):
                            mm = nc.tensor.transpose(ps[s][:, SCORE_BANK[b], h * P:(h + 1) * P], prob[s][:, b, h, :],
                                                     ident[:, :])
                        mm.then_inc(prob_ps[s], 1)

                def attend(s, n):
                    pe.wait_ge(prob_t[s], n * BLK)
                    for b in range(BLK):
                        for h in range(HEADS):
                            d = slice(h % 2 * HEAD_DIM, h % 2 * HEAD_DIM + HEAD_DIM)
                            mm = nc.tensor.matmul(ps[s][d, feat_bank[OT] + h // 2, b * P:(b + 1) * P],
                                                  vv[s][:, b, h * HEAD_DIM:(h + 1) * HEAD_DIM], prob_tr[s][:, b, h, :],
                                                  start=True, stop=True)
                    mm.then_inc(feat_ps[s], 1)

                def attn_out(s, n):
                    pe.wait_ge(feat_lo[s], at(n, FEATS, OT))
                    dense(s, hl_a[s][:, :, :, :], "wo", 2).then_inc(wo_ps[s], 1)

                def turn_x2(s, n):
                    pe.wait_ge(x2_ok[s], n)
                    turn(s, x1, X2T)

                def mlp_up(s, n):
                    pe.wait_ge(feat_lo[s], at(n, FEATS, X2T))
                    src = hl_b[s]
                    for m in range(HT):
                        for k in range(KT):
                            mm = product(ps[s][:, HID_BANK[m], :], weight("w1", k, m * P, P),
                                         (src[:, 0, k, :], src[:, 1, k, :]), k == 0, k == KT - 1)
                        mm.then_inc(w1_ps[s], 1)

                def mlp_down(s, n):
                    pe.wait_ge(gelu_lo[s], n * HT)
                    dense(s, gelu_hl[s], "w2", 2).then_inc(w2_ps[s], 1)

                def turn_xb(s, n):
                    pe.wait_ge(ln_out[s], at(n, NORMS, LN_L1))
                    turn(s, xb, XBT)

                def gcn_dense(s, n, j):
                    pe.wait_ge(feat_lo[s], at(n, FEATS, (XBT, H0)[j]))
                    dense(s, (hl_a, hl_b)[j][s][:, :, :, :], ("wg0", "wg1")[j], 2).then_inc(wg_ps[s], 1)

                def gcn_mix(s, n, j):
                    pe.wait_ge(wg_ok[s], at(n, 2, j))
                    for f in range(KT):
                        for b in range(BLK):
                            mm = nc.tensor.matmul(by_feature(s, 0)[:, f, b * P:(b + 1) * P],
                                                  wg[s][:, b, f * P:(f + 1) * P], at_bd[:, :], start=True, stop=True)
                    mm.then_inc(feat_ps[s], 1)

                def cell(s, n, c):
                    p, step, _ = CELLS[c]
                    w = cell_width(c)
                    if c == 0:
                        pe.wait_ge(feat_lo[s], at(n, FEATS, H1))
                    elif step == 0 and p > 1:
                        pe.wait_ge(h_lo[s], at(n, NCELL, c - 1))
                    if c > 0:
                        pe.wait_ge(gate_ok[s], gate_at(n, c, -1))
                    tok = [cell_tokens(state_hl[s][:, half, :, :], c) for half in range(2)]
                    for j, g in enumerate(GATE_LIST[c]):
                        for m in range(KT):
                            o = ps[s][:, g, m * w:(m + 1) * w]
                            o = o if p == 1 else o.rearrange("q (b w) -> q b w", b=TILE_BATCHES)
                            for k in range(KT):
                                mm = product(o, weight(f"wih{p}", k, (g * KT + m) * P, P), (tok[0][:, k], tok[1][:, k]),
                                             m == 0 and k == 0, step == 0 and m == KT - 1 and k == KT - 1)
                        if step == 0:
                            mm.then_inc(gate_ps[s], 1)
                    if step > 0:
                        pe.wait_ge(h_lo[s], at(n, NCELL, c - 1))
                        for j, g in enumerate(GATE_LIST[c]):
                            for m in range(KT):
                                for k in range(KT):
                                    mm = product(ps[s][:, g, m * w:(m + 1) * w],
                                                 weight(f"whh{p}", k, (g * KT + m) * P, P),
                                                 (cell_hl[s][:, 0, k * w:(k + 1) * w], cell_hl[s][:, 1, k * w:(k + 1) * w]),
                                                 False, m == KT - 1 and k == KT - 1)
                            mm.then_inc(gate_ps[s], 1)

                def turn_state(s, n):
                    pe.wait_ge(h_ok[s], n * NCELL)
                    pe.wait_ge(gate_ok[s], n * NGATE)
                    for f in range(KT):
                        for b in range(BLK):
                            mm = nc.tensor.transpose(by_token(s, 0)[:, b, f * P:(f + 1) * P],
                                                     state[s][:, f, b * P:(b + 1) * P], ident[:, :])
                    mm.then_inc(hf_ps[s], 1)

                def turn_xc(s, n):
                    pe.wait_ge(ln_out[s], at(n, NORMS, LN_L2))
                    turn(s, xc, XCT)

                def gat_dense(s, n):
                    pe.wait_ge(feat_lo[s], at(n, FEATS, XCT))
                    src = hl_b[s]
                    for k in range(KT):
                        product(ps[s][:, 2, :], (wa2[:, 0, k, :], wa2[:, 1, k, :]), (src[:, 0, k, :], src[:, 1, k, :]),
                                k == 0, k == KT - 1)
                    for b in range(BLK):
                        for k in range(KT):
                            mm = product(ps[s][:, 3, b:b + 1],
                                         (src[:, 0, k, b * P:(b + 1) * P], src[:, 1, k, b * P:(b + 1) * P]),
                                         (wa1[:, 0, k:k + 1], wa1[:, 1, k:k + 1]), k == 0, k == KT - 1)
                    mm.then_inc(s_ps[s], 1)
                    dense(s, src[:, :, :, :], "w3", 0).then_inc(wh_ps[s], 1)

                def turn_att(s, n):
                    pe.wait_ge(eexp_ok[s], n)
                    for b in range(BLK):
                        mm = nc.tensor.transpose(ps[s][:, 2, b * P:(b + 1) * P], att[s][:, b, :], ident[:, :])
                    mm.then_inc(att_ps[s], 1)

                def gat_mix(s, n):
                    pe.wait_ge(wh_ok[s], n)
                    pe.wait_ge(att_t[s], n)
                    for b in range(BLK):
                        mm = nc.tensor.matmul(by_token(s, 0)[:, b, :], att_tr[s][:, b, :], wh[s][:, b, :],
                                              start=True, stop=True)
                    mm.then_inc(av_ps[s], 1)

                with pe.Fori(1, ROUNDS + 1) as n:
                    for stage in (turn_y, chebyshev, conv, turn_x1, qkv, scores, turn_probs, attend, attn_out, turn_x2,
                                  mlp_up, mlp_down, turn_xb):
                        for s in range(STREAMS):
                            stage(s, n)
                    for j in range(2):
                        for s in range(STREAMS):
                            gcn_dense(s, n, j)
                        for s in range(STREAMS):
                            gcn_mix(s, n, j)
                    for c in range(NCELL):
                        for s in range(STREAMS):
                            cell(s, n, c)
                    for stage in (turn_state, turn_xc, gat_dense, turn_att, gat_mix):
                        for s in range(STREAMS):
                            stage(s, n)

            @block.scalar
            def _(act):
                def norm_y(s, n):
                    act.wait_ge(o_in[s], n * 16)
                    for m in range(KT):
                        nc.scalar.activation(act_in[s][:, m, :], act_in[s][:, m, :], ACT.Identity,
                                             bias=bn2[:, 1, m:m + 1], scale=bn2[:, 0, m:m + 1]).then_inc(y_ok[s], 1)

                def ln_apply(s, n, j, dst):
                    act.wait_ge(ln_nmr[s], at(n, NORMS, j))
                    for b in range(BLK):
                        op = nc.scalar.activation(dst[s][:, b, :], t[s][:, b, :], ACT.Identity, bias=nmr[s][:, b:b + 1],
                                                  scale=rstd[s][:, b:b + 1])
                    op.then_inc(ln_out[s], 1)

                def high(s, n, j):
                    act.wait_ge(feat_ps[s], at(n, FEATS, j))
                    nc.scalar.activation(feat_dst[j][s][:, 0, :, :], by_feature(s, feat_bank[j]),
                                         ACT.Relu if j in feat_relu else ACT.Copy).then_inc(feat_hi[s], 1)

                def take_qk(s, n):
                    act.wait_ge(q_ps[s], n)
                    nc.scalar.activation(q[s], by_feature(s, 0), ACT.Copy, scale=UNSCALE * HEAD_DIM ** -0.5)\
                        .then_inc(q_ok[s], 1)
                    act.wait_ge(k_ps[s], n)
                    nc.scalar.activation(kk[s], by_feature(s, 2), ACT.Copy, scale=UNSCALE).then_inc(k_ok[s], 1)

                def exps(s, n):
                    for b in range(BLK):
                        act.wait_ge(nmax_ok[s], at(n, BLK, b))
                        for h in range(HEADS):
                            i = b * HEADS + h
                            op = nc.scalar.activation(prob[s][:, b, h, :], prob[s][:, b, h, :], ACT.Exp,
                                                      bias=smax[s][:, i:i + 1], accum_out=ssum[s][:, i:i + 1])
                        op.then_inc(exp_ok[s], 1)

                def take_probs(s, n):
                    for b in range(BLK):
                        act.wait_ge(prob_ps[s], at(n, BLK, b))
                        nc.scalar.copy(prob_tr[s][:, b, :, :], ps[s][:, SCORE_BANK[b], :]
                                       .rearrange("p (h n) -> p h n", h=HEADS)).then_inc(prob_t[s], 1)

                def gelus(s, n):
                    for m in range(HT):
                        act.wait_ge(w1_ps[s], at(n, HT, m))
                        nc.scalar.activation(gelu[s][:, m, :], ps[s][:, HID_BANK[m], :], ACT.Gelu, bias=vec("l1_b1", m),
                                             scale=UNSCALE).then_inc(gelu_ok[s], 1)

                def cell(s, n, c):
                    p = CELLS[c][0]
                    w = cell_width(c)
                    if c == 1:
                        act.wait_ge(h_ok[s], at(n, NCELL, 0))
                    for j, g in enumerate(GATE_LIST[c]):
                        act.wait_ge(gate_ps[s], gate_at(n, c, j))
                        for m in range(KT):
                            bias = ((p - 1) * 4 + g) * KT + m
                            op = nc.scalar.activation(gates[s][:, g, m * w:(m + 1) * w], ps[s][:, g, m * w:(m + 1) * w],
                                                      ACT.Tanh if g == GATE_G else ACT.Sigmoid,
                                                      bias=lstm_b[:, bias:bias + 1], scale=UNSCALE)
                        op.then_inc(gate_ok[s], 1)
                    act.wait_ge(c_ok[s], at(n, NCELL, c))
                    nc.scalar.activation(cell_t[s][:, 0:KT * w], cell_c[s][:, 0:KT * w], ACT.Tanh).then_inc(tanh_ok[s], 1)

                def take_wh(s, n):
                    act.wait_ge(wh_ps[s], n)
                    nc.scalar.activation(wh[s], by_token(s, 0), ACT.Copy, scale=UNSCALE).then_inc(wh_ok[s], 1)

                def gat_exps(s, n):
                    act.wait_ge(enmax_ok[s], n)
                    for b in range(BLK):
                        op = nc.scalar.activation(att[s][:, b, :], att[s][:, b, :], ACT.Exp, bias=smax[s][:, b:b + 1],
                                                  accum_out=ssum[s][:, b:b + 1])
                    op.then_inc(eexp_ok[s], 1)

                def take_att(s, n):
                    act.wait_ge(att_ps[s], n)
                    nc.scalar.copy(att_tr[s], ps[s][:, 2, :].rearrange("p (b n) -> p b n", b=BLK)).then_inc(att_t[s], 1)

                with act.Fori(1, ROUNDS + 1) as n:
                    def each(stage, *args):
                        for s in range(STREAMS):
                            stage(s, n, *args)
                    each(norm_y)
                    each(ln_apply, LN_L0, xa)
                    each(high, XP)
                    each(ln_apply, LN_G1, t)
                    each(high, X1T)
                    each(take_qk)
                    each(exps)
                    each(take_probs)
                    each(high, OT)
                    each(ln_apply, LN_G2, t)
                    each(high, X2T)
                    each(gelus)
                    each(ln_apply, LN_G3, t)
                    each(ln_apply, LN_L1, xb)
                    each(high, XBT)
                    each(high, H0)
                    each(high, H1)
                    for c in range(NCELL):
                        each(cell, c)
                    each(ln_apply, LN_L2, xc)
                    each(high, XCT)
                    each(take_wh)
                    each(gat_exps)
                    each(take_att)
                    each(ln_apply, LN_L3, xb)

            @block.gpsimd
            def _(pool):
                def ln_root(s, n, j):
                    pool.wait_ge(ln_ve[s], at(n, NORMS, j))
                    nc.gpsimd.tensor_tensor(rstd[s][:, :], ve[s][:, :], nhalf[:, 0:BLK], ALU.pow).then_inc(ln_rstd[s], 1)

                def scale(s, n, j, name):
                    pool.wait_ge(ln_out[s], at(n, NORMS, j))
                    nc.gpsimd.tensor_tensor(t[s][:, :, :], t[s][:, :, :], row_of(name), ALU.mult).then_inc(scaled_ok[s], 1)

                def x1_bias(s, n):
                    pool.wait_ge(x1_ok[s], n)
                    pool.wait_ge(out_stored[s], n * 16 - 15)
                    nc.gpsimd.tensor_tensor(xb[s][:, :, :], x1[s][:, :, :], row_of("bo"), ALU.add).then_inc(pre_ok[s], 1)

                def probs(s, n):
                    for b in range(BLK):
                        pool.wait_ge(inv_ok[s], at(n, BLK, b))
                        nc.gpsimd.tensor_tensor(prob[s][:, b, :, :], prob[s][:, b, :, :],
                                                ssum[s][:, b * HEADS:(b + 1) * HEADS].unsqueeze(2)
                                                .broadcast_to([P, HEADS, P]), ALU.mult).then_inc(prob_ok[s], 1)

                def x2_bias(s, n):
                    pool.wait_ge(x2_ok[s], n)
                    nc.gpsimd.tensor_tensor(xb[s][:, :, :], x1[s][:, :, :], row_of("b2"), ALU.add).then_inc(pre_ok[s], 1)

                def gelu_high(s, n):
                    for m in range(HT):
                        pool.wait_ge(gelu_ok[s], at(n, HT, m))
                        nc.gpsimd.tensor_tensor(gelu_hl[s][:, 0, m, :], gelu[s][:, m, :],
                                                zero[:, 0:1].broadcast_to([P, TILE]), ALU.add)\
                            .then_inc(gelu_hi[s], 1)

                def xa_bias(s, n):
                    pool.wait_ge(t_ok[s], at(n, NORMS, LN_G3))
                    nc.gpsimd.tensor_tensor(xb[s][:, :, :], xa[s][:, :, :], row_of("be3"), ALU.add).then_inc(pre_ok[s], 1)

                def cell(s, n, c):
                    pool.wait_ge(h_ok[s], at(n, NCELL, c))
                    w = cell_width(c)
                    if is_last_step(c):
                        h = cell_tokens(state[s], c)
                        nc.gpsimd.tensor_tensor(cell_tokens(state_hl[s][:, 0, :, :], c), h, zeros_like(h), ALU.add)\
                            .then_inc(h_hi[s], 1)
                    else:
                        h = cell_h[s][:, 0:KT * w]
                        nc.gpsimd.tensor_tensor(cell_hl[s][:, 0, 0:KT * w], h, zeros_like(h), ALU.add).then_inc(h_hi[s], 1)

                with pool.Fori(1, ROUNDS + 1) as n:
                    def each(stage, *args):
                        for s in range(STREAMS):
                            stage(s, n, *args)
                    each(ln_root, LN_L0)
                    each(ln_root, LN_G1)
                    each(scale, LN_G1, "g1")
                    each(x1_bias)
                    each(probs)
                    each(ln_root, LN_G2)
                    each(scale, LN_G2, "g2")
                    each(x2_bias)
                    each(gelu_high)
                    each(xa_bias)
                    each(ln_root, LN_G3)
                    each(scale, LN_G3, "g3")
                    each(ln_root, LN_L1)
                    for c in range(NCELL):
                        each(cell, c)
                    each(ln_root, LN_L2)
                    each(ln_root, LN_L3)

            @block.vector
            def _(dve):
                for s in range(STREAMS):
                    nc.vector.memset(small[:, 42 + s:43 + s], 0.0).then_inc(banks_free[s], 1)
                    nc.vector.memset(small[:, 44 + s:45 + s], 0.0).then_inc(out_stored[s], 1)

                held = [0]

                def wait_apart(semaphore, value):
                    dve.wait_ge(semaphore, value)
                    nc.vector.memset(hold[:, held[0]:held[0] + 1], 0.0)
                    held[0] += 1

                def ln(s, n, j):
                    dve.wait_ge(t_ok[s], at(n, NORMS, j))
                    for b in range(BLK):
                        op = nc.vector.bn_stats(stats[s][:, b, :], t[s][:, b, :])
                    op.then_inc(ln_stats[s], 1)
                    wait_apart(ln_stats[s], at(n, NORMS, j))
                    for b in range(BLK):
                        op = nc.vector.bn_aggr(mv[s][:, b, :], stats[s][:, b, :])
                    op.then_inc(ln_mv[s], 1)
                    dve.wait_ge(ln_mv[s], at(n, NORMS, j))
                    nc.vector.tensor_scalar(ve[s][:, :], mv[s][:, :, 1], EPS, None, ALU.add).then_inc(ln_ve[s], 1)

                def ln_shift(s, n, j):
                    dve.wait_ge(ln_rstd[s], at(n, NORMS, j))
                    nc.vector.scalar_tensor_tensor(nmr[s][:, :], mv[s][:, :, 0], -1.0, rstd[s][:, :], ALU.mult, ALU.mult)\
                        .then_inc(ln_nmr[s], 1)

                def add_y(s, n):
                    dve.wait_ge(x_in[s], n * 16)
                    dve.wait_ge(y_ps[s], n)
                    nc.vector.tensor_tensor(t[s][:, :, :], by_token(s, 0), xa[s][:, :, :], ALU.add).then_inc(t_ok[s], 1)
                    ln(s, n, LN_L0)

                def low(s, n, j):
                    dve.wait_ge(feat_hi[s], at(n, FEATS, j))
                    hi, lo = feat_dst[j][s][:, 0, :, :], feat_dst[j][s][:, 1, :, :]
                    src = by_feature(s, feat_bank[j])
                    if j in feat_relu:
                        nc.vector.scalar_tensor_tensor(lo, src, 0.0, hi, ALU.max, ALU.subtract).then_inc(feat_lo[s], 1)
                    else:
                        nc.vector.tensor_tensor(lo, src, hi, ALU.subtract).then_inc(feat_lo[s], 1)

                def conv_bias(s, n):
                    dve.wait_ge(hc_ps[s], n)
                    nc.vector.scalar_tensor_tensor(t[s][:, :, :], by_token(s, 0), UNSCALE, row_of("bc"), ALU.mult, ALU.add)\
                        .then_inc(t_ok[s], 1)
                    ln(s, n, LN_G1)

                def make_x1(s, n):
                    dve.wait_ge(scaled_ok[s], at(n, 3, 0))
                    nc.vector.tensor_tensor(t[s][:, :, :], t[s][:, :, :], row_of("be1"), ALU.add).then_inc(shifted_ok[s], 1)
                    dve.wait_ge(shifted_ok[s], n)
                    nc.vector.scalar_tensor_tensor(x1[s][:, :, :], t[s][:, :, :], 0.0, xa[s][:, :, :], ALU.max, ALU.add)\
                        .then_inc(x1_ok[s], 1)

                def take_v(s, n):
                    dve.wait_ge(v_ps[s], n)
                    nc.vector.tensor_scalar(vv[s], by_token(s, 0), UNSCALE, None, ALU.mult).then_inc(v_ok[s], 1)

                def mask_scores(s, n):
                    for b in range(BLK):
                        if b % 2 == 0:
                            wait_apart(score_ps[s], at(n, BLK, b + 1))
                        for h in range(HEADS):
                            i = b * HEADS + h
                            op = nc.vector.tensor_tensor_reduce(prob[s][:, b, h, :],
                                                                score(s, b, h), mask1[:, :],
                                                                1.0, -3.0e38, ALU.add, ALU.max, smax[s][:, i:i + 1])
                        op.then_inc(masked_ok[s], 1)
                        dve.wait_ge(masked_ok[s], at(n, BLK, b))
                        part = smax[s][:, b * HEADS:(b + 1) * HEADS]
                        nc.vector.tensor_scalar(part, part, -1.0, None, ALU.mult).then_inc(nmax_ok[s], 1)

                def invert_sums(s, n):
                    for b in range(BLK):
                        dve.wait_ge(exp_ok[s], at(n, BLK, b))
                        part = ssum[s][:, b * HEADS:(b + 1) * HEADS]
                        nc.vector.reciprocal(part, part).then_inc(inv_ok[s], 1)

                def add_attn(s, n):
                    dve.wait_ge(pre_ok[s], at(n, 3, 0))
                    dve.wait_ge(wo_ps[s], n)
                    nc.vector.scalar_tensor_tensor(t[s][:, :, :], by_token(s, 2), UNSCALE, xb[s][:, :, :], ALU.mult, ALU.add)\
                        .then_inc(t_ok[s], 1)
                    ln(s, n, LN_G2)

                def make_x2(s, n):
                    dve.wait_ge(scaled_ok[s], at(n, 3, 1))
                    nc.vector.tensor_tensor(x1[s][:, :, :], t[s][:, :, :], row_of("be2"), ALU.add).then_inc(x2_ok[s], 1)

                def gelu_low(s, n):
                    for m in range(HT):
                        dve.wait_ge(gelu_hi[s], at(n, HT, m))
                        nc.vector.tensor_tensor(gelu_hl[s][:, 1, m, :], gelu[s][:, m, :], gelu_hl[s][:, 0, m, :],
                                                ALU.subtract).then_inc(gelu_lo[s], 1)

                def add_mlp(s, n):
                    dve.wait_ge(pre_ok[s], at(n, 3, 1))
                    dve.wait_ge(w2_ps[s], n)
                    nc.vector.scalar_tensor_tensor(t[s][:, :, :], by_token(s, 2), UNSCALE, xb[s][:, :, :], ALU.mult, ALU.add)\
                        .then_inc(t_ok[s], 1)
                    ln(s, n, LN_G3)

                def add_xa(s, n):
                    dve.wait_ge(pre_ok[s], at(n, 3, 2))
                    dve.wait_ge(scaled_ok[s], at(n, 3, 2))
                    nc.vector.tensor_tensor(t[s][:, :, :], t[s][:, :, :], xb[s][:, :, :], ALU.add).then_inc(t_ok[s], 1)
                    ln(s, n, LN_L1)

                def gcn_bias(s, n, j):
                    dve.wait_ge(wg_ps[s], at(n, 2, j))
                    nc.vector.scalar_tensor_tensor(wg[s], by_token(s, 2), UNSCALE, row_of(("bg0", "bg1")[j]), ALU.mult,
                                                   ALU.add).then_inc(wg_ok[s], 1)

                def cell(s, n, c):
                    w = cell_width(c)
                    g = [gates[s][:, j, 0:KT * w] for j in range(4)]
                    cc, tc = cell_c[s][:, 0:KT * w], cell_t[s][:, 0:KT * w]
                    if CELLS[c][1] == 0:
                        dve.wait_ge(gate_ok[s], gate_at(n, c, 1))
                        nc.vector.tensor_tensor(cc, g[GATE_I], g[GATE_G], ALU.mult).then_inc(c_ok[s], 1)
                    else:
                        i = STEPPED.index(c)
                        dve.wait_ge(gate_ok[s], gate_at(n, c, 1))
                        nc.vector.tensor_tensor(g[GATE_I], g[GATE_I], g[GATE_G], ALU.mult).then_inc(ig_ok[s], 1)
                        dve.wait_ge(gate_ok[s], gate_at(n, c, 2))
                        nc.vector.tensor_tensor(cc, cc, g[GATE_F], ALU.mult).then_inc(fc_ok[s], 1)
                        dve.wait_ge(fc_ok[s], at(n, len(STEPPED), i))
                        nc.vector.tensor_tensor(cc, cc, g[GATE_I], ALU.add).then_inc(c_ok[s], 1)
                    dve.wait_ge(tanh_ok[s], at(n, NCELL, c))
                    if is_last_step(c):
                        h, hi, lo = (cell_tokens(x, c) for x in
                                     (state[s], state_hl[s][:, 0, :, :], state_hl[s][:, 1, :, :]))
                        o, th = (like_cell(x.rearrange("q (k w) -> q k w", k=KT), c) for x in (g[GATE_O], tc))
                    else:
                        h, hi, lo = cell_h[s][:, 0:KT * w], cell_hl[s][:, 0, 0:KT * w], cell_hl[s][:, 1, 0:KT * w]
                        o, th = g[GATE_O], tc
                    nc.vector.tensor_tensor(h, o, th, ALU.mult).then_inc(h_ok[s], 1)
                    dve.wait_ge(h_hi[s], at(n, NCELL, c))
                    nc.vector.tensor_tensor(lo, h, hi, ALU.subtract).then_inc(h_lo[s], 1)

                def add_state(s, n):
                    dve.wait_ge(hf_ps[s], n)
                    nc.vector.tensor_tensor(t[s][:, :, :], by_token(s, 0), xb[s][:, :, :], ALU.add).then_inc(t_ok[s], 1)
                    ln(s, n, LN_L2)

                def gat_logits(s, n):
                    dve.wait_ge(s_ps[s], n)
                    nc.vector.tensor_scalar(s1[s], ps[s][:, 3, 0:BLK], UNSCALE, None, ALU.mult).then_inc(s1_ok[s], 1)
                    dve.wait_ge(s1_ok[s], n)
                    for b in range(BLK):
                        op = nc.vector.tensor_scalar(logit[s][:, b, :], ps[s][:, 2, b * P:(b + 1) * P], UNSCALE,
                                                     s1[s][:, b:b + 1], ALU.mult, ALU.add)
                    op.then_inc(e_ok[s], 1)
                    dve.wait_ge(e_ok[s], n)
                    nc.vector.scalar_tensor_tensor(logit[s], logit[s], 0.2, logit[s], ALU.mult, ALU.max)\
                        .then_inc(lrelu_ok[s], 1)
                    wait_apart(lrelu_ok[s], n)
                    for b in range(BLK):
                        op = nc.vector.tensor_tensor_reduce(att[s][:, b, :], logit[s][:, b, :], mask3[:, :], 1.0, -3.0e38,
                                                            ALU.add, ALU.max, smax[s][:, b:b + 1])
                    op.then_inc(emask_ok[s], 1)
                    dve.wait_ge(emask_ok[s], n)
                    nc.vector.tensor_scalar(smax[s][:, 0:BLK], smax[s][:, 0:BLK], -1.0, None, ALU.mult)\
                        .then_inc(enmax_ok[s], 1)

                def gat_sums(s, n):
                    dve.wait_ge(eexp_ok[s], n)
                    nc.vector.reciprocal(ssum[s][:, 0:BLK], ssum[s][:, 0:BLK]).then_inc(einv_ok[s], 1)

                def add_gat(s, n):
                    dve.wait_ge(einv_ok[s], n)
                    dve.wait_ge(av_ps[s], n)
                    for b in range(BLK):
                        op = nc.vector.scalar_tensor_tensor(t[s][:, b, :], by_token(s, 0)[:, b, :], ssum[s][:, b:b + 1],
                                                            xc[s][:, b, :], ALU.mult, ALU.add)
                    op.then_inc(t_ok[s], 1)
                    ln(s, n, LN_L3)

                def end_tile(s, n):
                    ln_shift(s, n, LN_L3)
                    nc.vector.memset(small[:, 42 + s:43 + s], 0.0).then_inc(banks_free[s], 1)

                with dve.Fori(1, ROUNDS + 1) as n:
                    def each(stage, *args):
                        for s in range(STREAMS):
                            stage(s, n, *args)
                    each(add_y)
                    each(ln_shift, LN_L0)
                    each(low, XP)
                    each(conv_bias)
                    each(ln_shift, LN_G1)
                    each(make_x1)
                    each(low, X1T)
                    each(take_v)
                    each(mask_scores)
                    each(invert_sums)
                    each(low, OT)
                    each(add_attn)
                    each(ln_shift, LN_G2)
                    each(make_x2)
                    each(low, X2T)
                    each(gelu_low)
                    each(add_mlp)
                    each(ln_shift, LN_G3)
                    each(add_xa)
                    each(ln_shift, LN_L1)
                    each(low, XBT)
                    each(gcn_bias, 0)
                    each(low, H0)
                    each(gcn_bias, 1)
                    each(low, H1)
                    for c in range(NCELL):
                        each(cell, c)
                    each(add_state)
                    each(ln_shift, LN_L2)
                    each(low, XCT)
                    each(gat_logits)
                    each(gat_sums)
                    each(add_gat)
                    each(end_tile)


def kernel(**inputs):
    import numpy as np
    import concourse.bacc as bacc
    from concourse.bass_utils import run_bass_kernel_spmd

    given = {k: np.asarray(v) for k, v in inputs.items()}

    def turned(a):
        return np.swapaxes(a, -1, -2)

    mats = {"l0_w1": turned(given["L0_gnn_W1"]), "l0_w2": turned(given["L0_gnn_W2"]), "wc": given["L1_gnn_Wc"],
            "wq": given["L1_gnn_Wq"], "wk": given["L1_gnn_Wk"], "wv": given["L1_gnn_Wv"], "wo": given["L1_gnn_Wo"],
            "w1": given["L1_gnn_W1"], "w2": given["L1_gnn_W2"], "wg0": given["L2_gnn_Wg0"], "wg1": given["L2_gnn_Wg1"],
            "w3": given["L3_gnn_W"]}
    for p in range(1, SKIPS + 1):
        mats[f"wih{p}"] = turned(given["L2_gnn_Wih"][p - 1])
        mats[f"whh{p}"] = turned(given["L2_gnn_Whh"][p - 1])

    def tiled(w):
        return w.reshape(-1, P, w.shape[1]).transpose(1, 0, 2).reshape(P, -1)

    vectors = {"b1": given["L0_gnn_b1"], "g1": given["L0_gnn_g1"], "be1": given["L0_gnn_be1"], "b2": given["L0_gnn_b2"],
               "g2": given["L0_gnn_g2"], "be2": given["L0_gnn_be2"], "l1_b1": given["L1_gnn_b1"],
               "bih": given["L2_gnn_bih"], "bhh": given["L2_gnn_bhh"], "a": given["L3_gnn_a"]}
    lines = {r: given[f"L1_gnn_{r}"] for r in ROWS if not r.startswith("bg")}
    lines |= {r: given[f"L2_gnn_{r}"] for r in ROWS if r.startswith("bg")}
    arrays = {
        "in_x": given["x"],
        "in_adj": given["adj"],
        "in_adj_t": turned(given["adj"]),
        "in_wpack": np.concatenate([tiled(mats[name]) for name, _, _ in WEIGHTS], axis=1),
        "in_w3t": tiled(turned(given["L3_gnn_W"])).reshape(P, KT, DIM),
        "in_cols": np.concatenate([vectors[name].reshape(-1, P).T for name, _ in COLS], axis=1),
        "in_rows": np.stack([lines[r] for r in ROWS]),
    }
    arrays = {k: np.ascontiguousarray(v) for k, v in arrays.items()}
    nc = bacc.Bacc("TRN2", target_bir_lowering=False, num_devices=1)
    args = [nc.dram_tensor(k, v.shape, mybir.dt.from_np(v.dtype), kind="ExternalInput").ap() for k, v in arrays.items()]
    out = nc.dram_tensor("out", (BATCH, NODES, DIM), F32, kind="ExternalOutput").ap()
    build(nc, *args, out)
    result = run_bass_kernel_spmd(nc, [arrays], core_ids=[0])
    return result.results[0]["out"]
```

```python
from contextlib import ExitStack

import concourse.bass as bass
from concourse import mybir

F32 = mybir.dt.float32
F16 = mybir.dt.float16
ALU = mybir.AluOpType
ACT = mybir.ActivationFunctionType
AX = mybir.AxisListType

P = 128
BATCH, NODES, DIM = 128, 64, 256
HID = 2 * DIM
HEADS = 4
HEAD_DIM = DIM // HEADS
GATES = 4 * DIM
SKIPS = 4
KT = DIM // P
HT = HID // P
TILE = 512
BLK = TILE // P
TILE_BATCHES = TILE // NODES
TILES = BATCH * NODES // TILE
STREAMS = 2
ROUNDS = TILES // STREAMS
BANKS = 4
EPS = 1e-5
WSCALE = 256.0
UNSCALE = 1.0 / WSCALE
SQUARINGS = 28
NEG_L1, NEG_OFF, NEG_L3 = -1.0e9, -2.0e9, -1.0e30

WEIGHTS = [("l0_w1", DIM, HID), ("l0_w2", HID, DIM), ("wc", DIM, DIM), ("wq", DIM, DIM), ("wk", DIM, DIM),
           ("wv", DIM, DIM), ("wo", DIM, DIM), ("w1", DIM, HID), ("w2", HID, DIM), ("wg0", DIM, DIM),
           ("wg1", DIM, DIM), ("w3", DIM, DIM)]
WEIGHTS += [(f"wih{p}", DIM, GATES) for p in range(1, SKIPS + 1)]
WEIGHTS += [(f"whh{p}", DIM, GATES) for p in range(2, SKIPS + 1)]
UNIT = 1408
STAGES = 4


def weight_places():
    at, place = 0, {}
    for name, rows, width in WEIGHTS:
        place[name] = (at, width)
        at += rows // P * width
    return place, at


W_AT, W_COLS = weight_places()
UNITS = W_COLS // UNIT
assert UNITS * UNIT == W_COLS and UNITS % STAGES == 0 and SQUARINGS % (UNITS // STAGES) == 0

COLS = [("b1", HT), ("g1", HT), ("be1", HT), ("b2", KT), ("g2", KT), ("be2", KT), ("l1_b1", HT),
        ("bih", SKIPS * GATES // P), ("bhh", SKIPS * GATES // P), ("a", 2 * KT)]
ROWS = ["bc", "g1", "be1", "bo", "g2", "be2", "b2", "g3", "be3", "bg0", "bg1"]


def col_places():
    at, place = 0, {}
    for name, n in COLS:
        place[name] = (at, n)
        at += n
    return place, at


C_AT, C_COLS = col_places()

PARTS = 6
SECOND, FIRST = "second", "first"
FIRST_HALF = """
norm_y turn_y norm_l0 cheb conv norm_g1 turn_x1 q x1_bias k v scores exps turn_probs attend attn_out norm_g2
turn_x2 x2_bias mlp_up gelu_split xa_bias mlp_down norm_g3 norm_l1 turn_xb gcn0 mix0
""".split()
ORDER = """
norm_y gcn1 mix1 turn_y inp0 norm_l0 cell0 hid0 cheb inp1 cell1 hid1 conv norm_g1 inp2 cell2 hid2 inp3 turn_x1
cell3 hid3 q x1_bias k inp4 cell4 hid4 v scores exps inp5 cell5 hid5 turn_probs inp6 cell6 hid6 attend inp7
cell7 hid7 attn_out norm_g2 inp8 cell8 hid8 inp9 turn_x2 x2_bias cell9 hid9 mlp_up inp10 gelu_split cell10
hid10 turn_state norm_l2 xa_bias mlp_down norm_g3 norm_l1 turn_xc turn_xb gat gcn0 gat_exps turn_att mix0
gat_mix norm_l3
""".split()
SCHEDULE = [(FIRST if step in FIRST_HALF else SECOND, step) for step in ORDER]


def beside(second, first):
    given = {SECOND: second, FIRST: first}
    return [(name, *given[half]) for half, name in SCHEDULE if given[half] is not None]


def opening():
    return beside(None, (0, 1))


def rounds(n):
    return beside((0, n), (1, n)) + beside((1, n), (0, n + 1))


def parts(n):
    steps = rounds(n)
    part = -(-len(steps) // PARTS)
    return [steps[i:i + part] for i in range(0, len(steps), part)]


def closing():
    return beside((0, ROUNDS), (1, ROUNDS)) + beside((1, ROUNDS), None)


CELLS = [(1, 0, 0), (1, 0, TILE // 2)]
CELLS += [(p, step, None) for p in range(2, SKIPS + 1) for step in range(p)]
NCELL = len(CELLS)
GATE_I, GATE_F, GATE_G, GATE_O = range(4)
NORMS = 7
LN_L0, LN_G1, LN_G2, LN_G3, LN_L1, LN_L2, LN_L3 = range(NORMS)


def cell_width(c):
    p = CELLS[c][0]
    return TILE // 2 if p == 1 else TILE_BATCHES * (NODES // p)


def cell_tokens(buf, c):
    p, step, first = CELLS[c]
    if first is not None:
        return buf[:, :, first:first + TILE // 2]
    windows = NODES // p
    return buf.rearrange("q k (b t) -> q k b t", t=NODES)[:, :, :, step:step + (windows - 1) * p + 1:p]


def like_cell(ap, c):
    p, _, first = CELLS[c]
    return ap if first is not None else ap.rearrange("q k (b w) -> q k b w", b=TILE_BATCHES)


def is_last_step(c):
    return CELLS[c][1] == CELLS[c][0] - 1


def build(nc, x, adj, adj_t, wpack, w3t, cols, rows, out):
    ctx = ExitStack()
    with ctx:
        def sb(name, shape, dt=F32):
            return ctx.enter_context(nc.sbuf_tensor(name, shape, dt))

        def sem(name):
            return ctx.enter_context(nc.semaphore(name))

        def sems(name):
            return [sem(f"{name}_{s}") for s in range(STREAMS)]

        w_hi = sb("w_hi", [P, W_COLS], F16)
        w_lo = sb("w_lo", [P, W_COLS], F16)
        col = sb("col", [P, C_COLS])
        row = sb("row", [P, len(ROWS), DIM])
        ident = sb("ident", [P, P])
        a_bd = sb("a_bd", [P, P])
        at_bd = sb("at_bd", [P, P])
        gcn_t = sb("gcn_t", [P, P])
        cheb_t = sb("cheb_t", [P, P])
        mask1 = sb("mask1", [P, P])
        mask3 = sb("mask3", [P, P])
        lstm_b = sb("lstm_b", [P, SKIPS * GATES // P])
        wa1 = sb("wa1", [P, 2, KT], F16)
        wa2 = sb("wa2", [P, 2, KT, P], F16)
        bn1 = sb("bn1", [P, 2, HT])
        bn2 = sb("bn2", [P, 2, KT])
        small = sb("small", [P, 64])
        act_in = [sb(f"act_in_{s}", [P, KT, TILE]) for s in range(STREAMS)]
        xa = [sb(f"xa_{s}", [P, BLK, DIM]) for s in range(STREAMS)]
        t = [sb(f"t_{s}", [P, BLK, DIM]) for s in range(STREAMS)]
        x1 = [sb(f"x1_{s}", [P, BLK, DIM]) for s in range(STREAMS)]
        xb = [sb(f"xb_{s}", [P, BLK, DIM]) for s in range(STREAMS)]
        hl_a = [sb(f"hl_a_{s}", [P, 2, KT, TILE], F16) for s in range(STREAMS)]
        hl_b = [sb(f"hl_b_{s}", [P, 2, KT, TILE], F16) for s in range(STREAMS)]
        pool_mem = [sb(f"pool_mem_{s}", [P, 5 * KT * TILE]) for s in range(STREAMS)]
        stats = [sb(f"stats_{s}", [P, BLK, 6]) for s in range(STREAMS)]
        mv = [sb(f"mv_{s}", [P, BLK, 2]) for s in range(STREAMS)]
        ve = [sb(f"ve_{s}", [P, BLK]) for s in range(STREAMS)]
        rstd = [sb(f"rstd_{s}", [P, BLK]) for s in range(STREAMS)]
        nmr = [sb(f"nmr_{s}", [P, BLK]) for s in range(STREAMS)]
        zero = sb("zero", [P, 1])
        hold = sb("hold", [P, 128])
        nhalf = sb("nhalf", [P, 2 * BLK])
        smax = [sb(f"smax_{s}", [P, BLK * HEADS]) for s in range(STREAMS)]
        ssum = [sb(f"ssum_{s}", [P, BLK * HEADS]) for s in range(STREAMS)]
        bnst1 = sb("bnst1", [P, HT, TILES, 6])
        bnst2 = sb("bnst2", [P, KT, TILES, 6])
        ps = [ctx.enter_context(nc.psum_tensor(f"ps_{s}", [P, BANKS, 512], F32)) for s in range(STREAMS)]

        h_dram = nc.dram_tensor("h_scratch", [TILES, P, HT, TILE], F32, kind="Internal").ap()
        o_dram = nc.dram_tensor("o_scratch", [TILES, P, KT, TILE], F32, kind="Internal").ap()
        x_tiles = x.rearrange("(r s b2 b) n d -> r s (b n) b2 d", r=ROUNDS, s=STREAMS, b=P // NODES)
        out_tiles = out.rearrange("(r s b2 b) n d -> r s (b n) b2 d", r=ROUNDS, s=STREAMS, b=P // NODES)
        h_tiles = h_dram.rearrange("(r s) p m n -> r s p m n", s=STREAMS)
        o_tiles = o_dram.rearrange("(r s) p m n -> r s p m n", s=STREAMS)

        def weight(name, k, c0, n):
            at, width = W_AT[name]
            a = at + k * width + c0
            return w_hi[:, a:a + n], w_lo[:, a:a + n]

        def vec(name, m):
            return col[:, C_AT[name][0] + m:C_AT[name][0] + m + 1]

        def vecs(name):
            a, n = C_AT[name]
            return col[:, a:a + n]

        def row_of(name):
            return row[:, ROWS.index(name), :].unsqueeze(1).broadcast_to([P, BLK, DIM])

        def product(o, l, r, first, last):
            nc.tensor.matmul(o, l[0], r[0], start=first, stop=False, skip_group_check=True)
            nc.tensor.matmul(o, l[0], r[1], start=False, stop=False, skip_group_check=True)
            return nc.tensor.matmul(o, l[1], r[0], start=False, stop=last, skip_group_check=True)

        def zeros_like(ap):
            z = zero[:, 0:1]
            while len(z.shape) < len(ap.shape):
                z = z.unsqueeze(1)
            return z.broadcast_to(list(ap.shape))

        def by_token(s, b):
            return ps[s][:, b:b + 2, :].rearrange("p b (c f) -> p (b c) f", f=DIM)

        def by_feature(s, b):
            return ps[s][:, b:b + KT, :]

        used = []

        with ExitStack() as pctx:
            def psem(name):
                used.append(pctx.enter_context(nc.semaphore(name)))
                return used[-1]

            zeroed = psem("zeroed")
            adj_in = psem("adj_in")
            vec_in = psem("vec_in")
            w_in = [psem(f"w_in_{b}") for b in range(STAGES)]
            unit_hi = psem("unit_hi")
            unit_lo = psem("unit_lo")
            ident_ok = psem("ident_ok")
            step = psem("step")
            pow_ok = psem("pow_ok")
            gcn_ps = psem("gcn_ps")
            sq_ps = psem("sq_ps")
            sq_ready = psem("sq_ready")
            lam_ps = psem("lam_ps")
            wa_ps = psem("wa_ps")
            stage = [pool_mem[b // 2][:, b % 2 * UNIT:(b % 2 + 1) * UNIT] for b in range(STAGES)]
            w3t_sb = xa[0]
            ones = x1[0][:, 0, 0:P]
            scaled = x1[0][:, 1, 0:P]
            sym = x1[0][0:NODES, 2, 0:NODES]
            powr = x1[0][0:NODES, 3, 0:NODES]
            junk = x1[1][0:NODES, 0, 0:NODES]
            junk_full = x1[1][:, 1, 0:P]
            tr_part = small[0:NODES, 0:1]
            inv_tr = small[0:NODES, 1:2]
            lam_part = small[0:NODES, 2:4]
            rsum, csum, diag, deg, dinv = (small[:, 8 + j:9 + j] for j in range(5))
            lam_r, lam_c = small[:, 13:14], small[:, 14:15]
            lam_v = small[:, 16:18]
            wa_f = small[:, 20:20 + 2 * KT]
            SQ = ps[0][0:NODES, 0, 0:NODES]
            TR = ps[0][:, 1, 0:1]
            LAM = ps[0][:, 2, 0:2]
            GCN = ps[0][:, 3, 0:P]
            WA = ps[1][:, 0, 0:2 * KT]

            block = pctx.enter_context(nc.Block())

            @block.sync
            def _(sp):
                sp.wait_ge(zeroed, 2)
                for b in range(2):
                    d = slice(b * NODES, (b + 1) * NODES)
                    sp.dma_start(a_bd[d, d], adj).then_inc(adj_in, 16)
                    sp.dma_start(at_bd[d, d], adj_t).then_inc(adj_in, 16)
                sp.dma_start(col[:, :], cols).then_inc(vec_in, 16)
                sp.dma_start(w3t_sb[:, 0:KT, :], w3t).then_inc(vec_in, 16)
                sp.dma_start(row[:, :, :], rows.partition_broadcast(P)).then_inc(vec_in, 16)
                for b in range(STAGES):
                    sp.dma_start(stage[b], wpack[:, bass.ts(b, UNIT)]).then_inc(w_in[b], 16)
                with sp.Fori(1, UNITS // STAGES) as u:
                    for b in range(STAGES):
                        sp.wait_ge(unit_lo, u * STAGES + b - (STAGES - 1))
                        sp.dma_start(stage[b], wpack[:, bass.ds(u * (STAGES * UNIT) + b * UNIT, UNIT)])\
                            .then_inc(w_in[b], 16)

            @block.gpsimd
            def _(pool):
                nc.gpsimd.memset(a_bd[:, :], 0.0).then_inc(zeroed, 1)
                nc.gpsimd.memset(at_bd[:, :], 0.0).then_inc(zeroed, 1)
                nc.gpsimd.memset(ident[:, :], 0.0).then_inc(ident_ok, 1)
                nc.gpsimd.memset(ones, 1.0).then_inc(ident_ok, 1)
                nc.gpsimd.memset(nhalf[:, :], -0.5).then_inc(ident_ok, 1)
                nc.gpsimd.memset(zero[:, :], 0.0).then_inc(ident_ok, 1)
                pool.wait_ge(ident_ok, 4)
                nc.gpsimd.affine_select(out=ident[:, :], in_=ident[:, :], compare_op=ALU.not_equal, fill=1.0, base=0,
                                        pattern=[[-1, P]], channel_multiplier=1).then_inc(ident_ok, 1)
                pool.wait_ge(step, 5)
                nc.gpsimd.tensor_tensor(dinv, deg, nhalf[:, 0:1], ALU.pow).then_inc(pow_ok, 1)

            @block.scalar
            def _(act):
                with act.Fori(0, UNITS // STAGES) as u:
                    for b in range(STAGES):
                        act.wait_ge(w_in[b], u * 16 + 16)
                        nc.scalar.activation(w_hi[:, bass.ds(u * (STAGES * UNIT) + b * UNIT, UNIT)], stage[b], ACT.Copy,
                                             scale=WSCALE).then_inc(unit_hi, 1)

            @block.tensor
            def _(pe):
                pe.wait_ge(step, 6)
                pe.wait_ge(ident_ok, 5)
                nc.tensor.transpose(GCN, scaled, ident[:, :]).then_inc(gcn_ps, 1)
                pe.wait_ge(vec_in, 48)
                for half in range(2):
                    for kt in range(KT):
                        for ot in range(KT):
                            mm = nc.tensor.matmul(WA[:, half * KT + kt:half * KT + kt + 1],
                                                  w3t_sb[:, ot, kt * P:(kt + 1) * P],
                                                  vec("a", half * KT + ot), start=(ot == 0), stop=(ot == KT - 1))
                mm.then_inc(wa_ps, 1)
                with pe.Fori(0, SQUARINGS) as k:
                    pe.wait_ge(sq_ready, k * 2 + 2)
                    nc.tensor.matmul(TR, ones[0:NODES, :], tr_part, start=True, stop=True)
                    nc.tensor.matmul(SQ, powr, powr, start=True, stop=True).then_inc(sq_ps, 1)
                pe.wait_ge(sq_ready, 2 * SQUARINGS + 3)
                nc.tensor.matmul(LAM, ones[0:NODES, :], lam_part, start=True, stop=True).then_inc(lam_ps, 1)

            @block.vector
            def _(dve):
                dve.wait_ge(adj_in, 64)
                dve.wait_ge(ident_ok, 5)
                nc.vector.reduce_sum(rsum, a_bd[:, :], axis=AX.X).then_inc(step, 1)
                nc.vector.reduce_sum(csum, at_bd[:, :], axis=AX.X).then_inc(step, 1)
                nc.vector.tensor_tensor_reduce(junk_full, a_bd[:, :], ident[:, :], 1.0, 0.0, ALU.mult, ALU.add,
                                               diag).then_inc(step, 1)
                dve.wait_ge(step, 3)
                nc.vector.scalar_tensor_tensor(deg, rsum, 1.0, csum, ALU.add, ALU.add).then_inc(step, 1)
                dve.wait_ge(step, 4)
                nc.vector.tensor_tensor(deg, deg, diag, ALU.subtract).then_inc(step, 1)
                dve.wait_ge(pow_ok, 1)
                nc.vector.tensor_tensor(junk_full, a_bd[:, :], ident[:, :], ALU.add).then_inc(sq_ready, 1)
                dve.wait_ge(sq_ready, 1)
                nc.vector.tensor_scalar(scaled, junk_full, dinv, None, ALU.mult).then_inc(step, 1)
                dve.wait_ge(gcn_ps, 1)
                nc.vector.tensor_scalar(gcn_t[:, :], GCN, dinv, None, ALU.mult).then_inc(step, 1)
                nc.vector.tensor_scalar(mask1[:, :], a_bd[:, :], 0.0, NEG_L1, ALU.is_le, ALU.mult).then_inc(step, 1)
                nc.vector.tensor_scalar(mask3[:, :], a_bd[:, :], 0.0, NEG_L3, ALU.is_equal, ALU.mult).then_inc(step, 1)
                dve.wait_ge(step, 9)
                nc.vector.memset(mask1[0:NODES, NODES:P], NEG_OFF).then_inc(step, 1)
                nc.vector.memset(mask1[NODES:P, 0:NODES], NEG_OFF).then_inc(step, 1)
                dve.wait_ge(vec_in, 48)
                nc.vector.tensor_tensor(lstm_b[:, :], vecs("bih"), vecs("bhh"), ALU.add).then_inc(step, 1)
                dve.wait_ge(step, 12)
                for g in (GATE_I, GATE_F, GATE_O):
                    part = lstm_b[:, :].rearrange("p (w g k) -> p w g k", g=4, k=KT)[:, :, g, :]
                    half = nc.vector.tensor_scalar(part, part, 0.5, None, ALU.mult)
                half.then_inc(step, 1)
                twice = row[:, ROWS.index("bg1"), :]
                nc.vector.tensor_scalar(twice, twice, 2.0, None, ALU.mult).then_inc(step, 1)
                dve.wait_ge(wa_ps, 1)
                nc.vector.tensor_scalar(wa_f, WA, WSCALE, None, ALU.mult).then_inc(step, 1)
                dve.wait_ge(step, 15)
                nc.vector.tensor_copy(wa1[:, 0, :], wa_f[:, 0:KT]).then_inc(step, 1)
                nc.vector.tensor_copy(wa2[:, 0, :, :], wa_f[:, KT:2 * KT].unsqueeze(2).broadcast_to([P, KT, P]))\
                    .then_inc(step, 1)
                dve.wait_ge(step, 17)
                nc.vector.tensor_tensor(wa1[:, 1, :], wa_f[:, 0:KT], wa1[:, 0, :], ALU.subtract).then_inc(step, 1)
                nc.vector.tensor_tensor(wa2[:, 1, :, :], wa_f[:, KT:2 * KT].unsqueeze(2).broadcast_to([P, KT, P]),
                                        wa2[:, 0, :, :], ALU.subtract).then_inc(step, 1)
                nc.vector.tensor_tensor(sym, a_bd[0:NODES, 0:NODES], at_bd[0:NODES, 0:NODES], ALU.add).then_inc(step, 1)
                dve.wait_ge(step, 20)
                nc.vector.tensor_scalar(sym, sym, 0.5, None, ALU.mult).then_inc(step, 1)
                dve.wait_ge(step, 21)
                nc.vector.tensor_copy(powr, sym).then_inc(step, 1)
                dve.wait_ge(step, 22)
                nc.vector.tensor_tensor_reduce(junk, powr, powr, 1.0, 0.0, ALU.mult, ALU.add, tr_part)\
                    .then_inc(sq_ready, 1)

                def square(k):
                    dve.wait_ge(sq_ps, k + 1)
                    nc.vector.reciprocal(inv_tr, TR[0:NODES, :]).then_inc(step, 1)
                    dve.wait_ge(step, k + 23)
                    nc.vector.tensor_scalar(powr, SQ, inv_tr, None, ALU.mult).then_inc(sq_ready, 1)
                    dve.wait_ge(sq_ready, k * 2 + 3)
                    nc.vector.tensor_tensor_reduce(junk, powr, powr, 1.0, 0.0, ALU.mult, ALU.add, tr_part)\
                        .then_inc(sq_ready, 1)

                group = SQUARINGS // (UNITS // STAGES)
                with dve.Fori(0, UNITS // STAGES) as u:
                    for b in range(STAGES):
                        for k in range(b * group // STAGES, (b + 1) * group // STAGES):
                            square(u * group + k)
                        part = bass.ds(u * (STAGES * UNIT) + b * UNIT, UNIT)
                        dve.wait_ge(unit_hi, u * STAGES + b + 1)
                        nc.vector.scalar_tensor_tensor(w_lo[:, part], stage[b], WSCALE, w_hi[:, part], ALU.mult,
                                                       ALU.subtract).then_inc(unit_lo, 1)
                dve.wait_ge(sq_ready, 2 * SQUARINGS + 2)
                nc.vector.tensor_tensor_reduce(junk, sym, powr, 1.0, 0.0, ALU.mult, ALU.add, lam_part[:, 0:1])\
                    .then_inc(pow_ok, 1)
                dve.wait_ge(pow_ok, 2)
                nc.vector.tensor_tensor_reduce(junk, ident[0:NODES, 0:NODES], powr, 1.0, 0.0, ALU.mult, ALU.add,
                                               lam_part[:, 1:2]).then_inc(sq_ready, 1)
                dve.wait_ge(lam_ps, 1)
                nc.vector.tensor_copy(lam_v, LAM).then_inc(pow_ok, 1)
                dve.wait_ge(pow_ok, 3)
                nc.vector.reciprocal(lam_r, lam_v[:, 1:2]).then_inc(pow_ok, 1)
                dve.wait_ge(pow_ok, 4)
                nc.vector.tensor_scalar(lam_c, lam_v[:, 0:1], lam_r, 1e-8, ALU.mult, ALU.add).then_inc(pow_ok, 1)
                dve.wait_ge(pow_ok, 5)
                nc.vector.reciprocal(lam_r, lam_c).then_inc(pow_ok, 1)
                dve.wait_ge(pow_ok, 6)
                nc.vector.tensor_scalar(lam_c, lam_r, 2.0, None, ALU.mult).then_inc(pow_ok, 1)
                dve.wait_ge(pow_ok, 7)
                nc.vector.scalar_tensor_tensor(cheb_t[:, :], at_bd[:, :], lam_c, ident[:, :], ALU.mult, ALU.subtract)\
                    .then_inc(pow_ok, 1)

        with ExitStack() as pctx:
            def psems(name):
                used.extend(pctx.enter_context(nc.semaphore(f"{name}_{s}")) for s in range(STREAMS))
                return used[-STREAMS:]

            x_in, agg_ps, agg_hi, agg_lo, hid_ps, hid_out, hid_stats, hid_stored = (
                psems(n) for n in ("p1_x_in", "agg_ps", "agg_hi", "agg_lo", "hid_ps", "hid_out", "hid_stats", "hid_stored"))
            hid = [pool_mem[s][:, 0:HT * TILE].rearrange("p (m n) -> p m n", m=HT) for s in range(STREAMS)]
            bn_step, bn_pow = psems("bn1")
            block = pctx.enter_context(nc.Block())

            @block.sync
            def _(sp):
                def store(s, n):
                    sp.wait_ge(hid_out[s], n * HT + 1)
                    sp.dma_start(h_tiles[bass.ds(n - 1, 1), s].rearrange("o p m n -> (o p) m n"), hid[s])\
                        .then_inc(hid_stored[s], 16)

                for s in range(STREAMS):
                    sp.dma_start(xa[s][:, :, :], x_tiles[0, s]).then_inc(x_in[s], 16)
                with sp.Fori(1, ROUNDS) as r:
                    for s in range(STREAMS):
                        sp.wait_ge(agg_ps[s], r)
                        sp.dma_start(xa[s][:, :, :], x_tiles[bass.ds(r, 1), s].rearrange("o p b d -> (o p) b d"))\
                            .then_inc(x_in[s], 16)
                    for s in range(STREAMS):
                        store(s, r)
                for s in range(STREAMS):
                    store(s, ROUNDS)
                for s in range(STREAMS):
                    sp.wait_ge(hid_stored[s], 16 * ROUNDS + 1)

            @block.tensor
            def _(pe):
                def aggregate(s, n):
                    pe.wait_ge(x_in[s], n * 16)
                    pe.wait_ge(hid_out[s], n * HT - HT + 1)
                    for f in range(KT):
                        for b in range(BLK):
                            mm = nc.tensor.matmul(ps[s][:, f, b * P:(b + 1) * P], xa[s][:, b, f * P:(f + 1) * P],
                                                  gcn_t[:, :], start=True, stop=True)
                    mm.then_inc(agg_ps[s], 1)

                def hidden(s, n):
                    pe.wait_ge(agg_lo[s], n)
                    agg = hl_a[s]
                    for m in range(HT):
                        bank = (m + 2) % BANKS
                        for k in range(KT):
                            mm = product(ps[s][:, bank, :], weight("l0_w1", k, m * P, P),
                                         (agg[:, 0, k, :], agg[:, 1, k, :]), k == 0, k == KT - 1)
                        mm.then_inc(hid_ps[s], 1)

                with pe.Fori(0, ROUNDS) as r:
                    for s in range(STREAMS):
                        aggregate(s, r + 1)
                    for s in range(STREAMS):
                        hidden(s, r + 1)

            @block.scalar
            def _(act):
                for s in range(STREAMS):
                    nc.scalar.activation(small[:, 40 + s:41 + s], ident[:, 0:1], ACT.Copy).then_inc(hid_out[s], 1)

                def agg_high(s, n):
                    act.wait_ge(agg_ps[s], n)
                    nc.scalar.copy(hl_a[s][:, 0, :, :], by_feature(s, 0)).then_inc(agg_hi[s], 1)

                def hid_bias(s, n):
                    act.wait_ge(hid_stored[s], n * 16 - 15)
                    act.wait_ge(hid_stats[s], n)
                    for m in range(HT):
                        act.wait_ge(hid_ps[s], n * HT - (HT - 1 - m))
                        nc.scalar.activation(hid[s][:, m, :], ps[s][:, (m + 2) % BANKS, :], ACT.Identity,
                                             bias=vec("b1", m), scale=UNSCALE).then_inc(hid_out[s], 1)

                with act.Fori(0, ROUNDS) as r:
                    for s in range(STREAMS):
                        agg_high(s, r + 1)
                    for s in range(STREAMS):
                        hid_bias(s, r + 1)

            @block.vector
            def _(dve):
                for s in range(STREAMS):
                    nc.vector.memset(small[:, 42 + s:43 + s], 0.0).then_inc(hid_stats[s], 1)
                    nc.vector.memset(small[:, 44 + s:45 + s], 0.0).then_inc(hid_stored[s], 1)

                def agg_low(s, n):
                    dve.wait_ge(agg_hi[s], n)
                    nc.vector.tensor_tensor(hl_a[s][:, 1, :, :], by_feature(s, 0), hl_a[s][:, 0, :, :], ALU.subtract)\
                        .then_inc(agg_lo[s], 1)

                def hid_stat(s, r):
                    for m in range(HT):
                        dve.wait_ge(hid_out[s], r * HT + m + 2)
                        st = nc.vector.bn_stats(bnst1[:, m, bass.ds(r * STREAMS + s, 1), :]
                                                .rearrange("p o c -> p (o c)"), hid[s][:, m, :])
                    st.then_inc(hid_stats[s], 1)

                with dve.Fori(0, ROUNDS) as r:
                    for s in range(STREAMS):
                        agg_low(s, r + 1)
                    for s in range(STREAMS):
                        hid_stat(s, r)
                for s in range(STREAMS):
                    dve.wait_ge(hid_stats[s], ROUNDS + 1)
                for m in range(HT):
                    nc.vector.bn_aggr(small[:, 2 * m:2 * m + 2], bnst1[:, m, :, :].rearrange("p t c -> p (t c)"))\
                        .then_inc(bn_step, 1)
                m_v = small[:, 0:2 * HT].rearrange("p (m c) -> p m c", c=2)
                dve.wait_ge(bn_step, HT)
                nc.vector.tensor_scalar(small[:, 16:16 + HT], m_v[:, :, 1], EPS, None, ALU.add).then_inc(bn_step, 1)
                dve.wait_ge(bn_pow, 1)
                nc.vector.tensor_tensor(bn1[:, 0, :], vecs("g1"), small[:, 24:24 + HT], ALU.mult).then_inc(bn_step, 1)
                dve.wait_ge(bn_step, HT + 2)
                nc.vector.tensor_tensor(small[:, 32:32 + HT], m_v[:, :, 0], bn1[:, 0, :], ALU.mult).then_inc(bn_step, 1)
                dve.wait_ge(bn_step, HT + 3)
                nc.vector.tensor_tensor(bn1[:, 1, :], vecs("be1"), small[:, 32:32 + HT], ALU.subtract).then_inc(bn_step, 1)

            @block.gpsimd
            def _(pool):
                pool.wait_ge(bn_step, HT + 1)
                nc.gpsimd.tensor_tensor(small[:, 24:24 + HT], small[:, 16:16 + HT], nhalf[:, 0:HT], ALU.pow)\
                    .then_inc(bn_pow, 1)

        with ExitStack() as pctx:
            def psems(name):
                return [pctx.enter_context(nc.semaphore(f"{name}_{s}")) for s in range(STREAMS)]

            rel, rel_hi, rel_lo, o_ps, o_out, o_stats, o_stored = (
                psems(n) for n in ("rel", "rel_hi", "rel_lo", "o_ps", "o_out", "o_stats", "o_stored"))
            h_in = [psems(f"h_in_{i}") for i in range(2)]
            hid = [[pool_mem[s][:, i * HT * TILE:(i + 1) * HT * TILE].rearrange("p (m n) -> p m n", m=HT)
                    for s in range(STREAMS)] for i in range(2)]
            hl = [[hl_a[s], hl_b[s]] for s in range(STREAMS)]
            bn_step = pctx.enter_context(nc.semaphore("bn2_step"))
            bn_pow = pctx.enter_context(nc.semaphore("bn2_pow"))
            block = pctx.enter_context(nc.Block())

            @block.sync
            def _(sp):
                for done in used:
                    sp.sem_clear(done)

                def store(s, n):
                    sp.wait_ge(o_out[s], n * KT + 1)
                    sp.dma_start(o_tiles[bass.ds(n - 1, 1), s].rearrange("o p m n -> (o p) m n"), act_in[s][:, :, :])\
                        .then_inc(o_stored[s], 16)

                for i in range(2):
                    for s in range(STREAMS):
                        sp.dma_start(hid[i][s], h_tiles[i, s]).then_inc(h_in[i][s], 16)
                with sp.Fori(1, ROUNDS // 2) as r:
                    for i in range(2):
                        for s in range(STREAMS):
                            sp.wait_ge(rel_lo[s], (r * 2 + i - 1) * HT)
                            sp.dma_start(hid[i][s], h_tiles[bass.ds(r * 2 + i, 1), s].rearrange("o p m n -> (o p) m n"))\
                                .then_inc(h_in[i][s], 16)
                        for s in range(STREAMS):
                            store(s, r * 2 + i - 1)
                for i in range(2):
                    for s in range(STREAMS):
                        store(s, ROUNDS - 1 + i)
                for s in range(STREAMS):
                    sp.wait_ge(o_stored[s], 16 * ROUNDS + 1)

            @block.scalar
            def _(act):
                def relu(s, r, i):
                    act.wait_ge(h_in[i][s], r * 16 + 16)
                    for m in range(HT):
                        nc.scalar.activation(hid[i][s][:, m, :], hid[i][s][:, m, :], ACT.Relu, bias=bn1[:, 1, m:m + 1],
                                             scale=bn1[:, 0, m:m + 1]).then_inc(rel[s], 1)

                def out_bias(s, n):
                    act.wait_ge(o_ps[s], n + 1)
                    act.wait_ge(o_stored[s], n * 16 - 15)
                    act.wait_ge(o_stats[s], n)
                    for m in range(KT):
                        nc.scalar.activation(act_in[s][:, m, :], ps[s][:, m, :], ACT.Identity, bias=vec("b2", m),
                                             scale=UNSCALE).then_inc(o_out[s], 1)

                for s in range(STREAMS):
                    nc.scalar.activation(small[:, 40 + s:41 + s], ident[:, 0:1], ACT.Copy).then_inc(o_out[s], 1)
                for s in range(STREAMS):
                    relu(s, 0, 0)
                with act.Fori(0, ROUNDS // 2 - 1) as r:
                    for s in range(STREAMS):
                        relu(s, r, 1)
                        out_bias(s, r * 2 + 1)
                    for s in range(STREAMS):
                        relu(s, r + 1, 0)
                        out_bias(s, r * 2 + 2)
                for s in range(STREAMS):
                    relu(s, ROUNDS // 2 - 1, 1)
                    out_bias(s, ROUNDS - 1)
                for s in range(STREAMS):
                    out_bias(s, ROUNDS)

            @block.gpsimd
            def _(pool):
                def high(s, n, i):
                    pool.wait_ge(o_ps[s], n)
                    for m in range(HT):
                        pool.wait_ge(rel[s], n * HT - (HT - 1 - m))
                        nc.gpsimd.tensor_tensor(hl[s][m // KT][:, 0, m % KT, :], hid[i][s][:, m, :],
                                                zero[:, 0:1].broadcast_to([P, TILE]), ALU.add).then_inc(rel_hi[s], 1)

                with pool.Fori(0, ROUNDS // 2) as r:
                    for i in range(2):
                        for s in range(STREAMS):
                            high(s, r * 2 + i + 1, i)
                pool.wait_ge(bn_step, KT + 1)
                nc.gpsimd.tensor_tensor(small[:, 24:24 + KT], small[:, 16:16 + KT], nhalf[:, 0:KT], ALU.pow)\
                    .then_inc(bn_pow, 1)

            @block.vector
            def _(dve):
                for s in range(STREAMS):
                    nc.vector.memset(small[:, 42 + s:43 + s], 0.0).then_inc(o_stats[s], 1)
                    nc.vector.memset(small[:, 44 + s:45 + s], 0.0).then_inc(o_stored[s], 1)
                    nc.vector.memset(small[:, 46 + s:47 + s], 0.0).then_inc(o_ps[s], 1)

                def low(s, n, i):
                    for m in range(HT):
                        dve.wait_ge(rel_hi[s], n * HT - (HT - 1 - m))
                        nc.vector.tensor_tensor(hl[s][m // KT][:, 1, m % KT, :], hid[i][s][:, m, :],
                                                hl[s][m // KT][:, 0, m % KT, :], ALU.subtract).then_inc(rel_lo[s], 1)

                def out_stat(s, r):
                    for m in range(KT):
                        dve.wait_ge(o_out[s], r * KT + m + 2)
                        st = nc.vector.bn_stats(bnst2[:, m, bass.ds(r * STREAMS + s, 1), :]
                                                .rearrange("p o c -> p (o c)"), act_in[s][:, m, :])
                    st.then_inc(o_stats[s], 1)

                for s in range(STREAMS):
                    low(s, 1, 0)
                with dve.Fori(0, ROUNDS // 2 - 1) as r:
                    for s in range(STREAMS):
                        low(s, r * 2 + 2, 1)
                        out_stat(s, r * 2)
                    for s in range(STREAMS):
                        low(s, r * 2 + 3, 0)
                        out_stat(s, r * 2 + 1)
                for s in range(STREAMS):
                    low(s, ROUNDS, 1)
                    out_stat(s, ROUNDS - 2)
                for s in range(STREAMS):
                    out_stat(s, ROUNDS - 1)
                for s in range(STREAMS):
                    dve.wait_ge(o_stats[s], ROUNDS + 1)
                for m in range(KT):
                    nc.vector.bn_aggr(small[:, 2 * m:2 * m + 2], bnst2[:, m, :, :].rearrange("p t c -> p (t c)"))\
                        .then_inc(bn_step, 1)
                m_v = small[:, 0:2 * KT].rearrange("p (m c) -> p m c", c=2)
                dve.wait_ge(bn_step, KT)
                nc.vector.tensor_scalar(small[:, 16:16 + KT], m_v[:, :, 1], EPS, None, ALU.add).then_inc(bn_step, 1)
                dve.wait_ge(bn_pow, 1)
                nc.vector.tensor_tensor(bn2[:, 0, :], vecs("g2"), small[:, 24:24 + KT], ALU.mult).then_inc(bn_step, 1)
                dve.wait_ge(bn_step, KT + 2)
                nc.vector.tensor_tensor(small[:, 32:32 + KT], m_v[:, :, 0], bn2[:, 0, :], ALU.mult).then_inc(bn_step, 1)
                dve.wait_ge(bn_step, KT + 3)
                nc.vector.tensor_tensor(bn2[:, 1, :], vecs("be2"), small[:, 32:32 + KT], ALU.subtract).then_inc(bn_step, 1)

            @block.tensor
            def _(pe):
                def second(s, n):
                    pe.wait_ge(o_out[s], n * KT - KT + 1)
                    for k in range(HT):
                        pe.wait_ge(rel_lo[s], n * HT - (HT - 1 - k))
                        half = hl[s][k // KT]
                        for m in range(KT):
                            mm = product(ps[s][:, m, :], weight("l0_w2", k, m * P, P),
                                         (half[:, 0, k % KT, :], half[:, 1, k % KT, :]), k == 0, k == HT - 1)
                    mm.then_inc(o_ps[s], 1)

                with pe.Fori(0, ROUNDS) as r:
                    for s in range(STREAMS):
                        second(s, r + 1)

        with ExitStack() as pctx:
            def psems(name):
                return [pctx.enter_context(nc.semaphore(f"{name}_{s}")) for s in range(STREAMS)]

            x_in, o_in, out_stored, banks_free = (psems(n) for n in ("x_in", "o_in", "out_stored", "banks_free"))
            y_ok, y_ps = psems("y_ok"), psems("y_ps")
            t_ok, ln_stats, ln_mv, ln_ve, ln_rstd, ln_nmr, ln_out, centred = (
                psems(n) for n in ("t_ok", "ln_stats", "ln_mv", "ln_ve", "ln_rstd", "ln_nmr", "ln_out", "centred"))
            feat_ps, feat_hi, feat_lo = psems("feat_ps"), psems("feat_hi"), psems("feat_lo")
            hc_ps, wo_ps, w2_ps, wg_ps, wg_ok = (psems(n) for n in ("hc_ps", "wo_ps", "w2_ps", "wg_ps", "wg_ok"))
            affine_ok, pre_ok, x1_ok, x2_ok, o_ok = (psems(n) for n in ("affine_ok", "pre_ok", "x1_ok", "x2_ok", "o_ok"))
            q_ps, k_ps, v_ps, q_ok, k_ok, v_ok = (psems(n) for n in ("q_ps", "k_ps", "v_ps", "q_ok", "k_ok", "v_ok"))
            score_ps, masked_ok, nmax_ok, exp_ok, inv_ok, prob_ok, prob_ps, prob_t = (
                psems(n) for n in ("score_ps", "masked_ok", "nmax_ok", "exp_ok", "inv_ok", "prob_ok", "prob_ps", "prob_t"))
            w1_ps, gelu_ok, gelu_hi, gelu_lo = (psems(n) for n in ("w1_ps", "gelu_ok", "gelu_hi", "gelu_lo"))
            gate_ps, gate_ok, ig_ok, fc_ok, c_ok, tanh_ok, h_ok, h_hi, h_lo = (
                psems(n) for n in ("gate_ps", "gate_ok", "ig_ok", "fc_ok", "c_ok", "tanh_ok", "h_ok", "h_hi", "h_lo"))
            hf_ps, wh_ps, wh_ok, s_ps, s1_ok, e_ok, lrelu_ok, emask_ok, enmax_ok, eexp_ok, einv_ok, att_ps, att_t, av_ps = (
                psems(n) for n in ("hf_ps", "wh_ps", "wh_ok", "s_ps", "s1_ok", "e_ok", "lrelu_ok", "emask_ok", "enmax_ok",
                                   "eexp_ok", "einv_ok", "att_ps", "att_t", "av_ps"))

            XP, X1T, OT, X2T, XBT, H0, H1, XCT = range(8)
            FEATS = 8 * KT
            feat_dst = [hl_a, hl_b, hl_a, hl_b, hl_a, hl_b, hl_a, hl_b]
            feat_bank = [2, 2, 0, 0, 0, 0, 0, 2]
            feat_relu = [H0, H1]
            FEAT_OF = {"cheb": XP, "turn_x1": X1T, "attend": OT, "turn_x2": X2T, "turn_xb": XBT, "mix0": H0, "mix1": H1,
                       "turn_xc": XCT}
            NORM_OF = {"norm_l0": LN_L0, "norm_g1": LN_G1, "norm_g2": LN_G2, "norm_g3": LN_G3, "norm_l1": LN_L1,
                       "norm_l2": LN_L2, "norm_l3": LN_L3}
            SCORE_BANK = [2, 3, 0, 1]
            HID_BANK = [2, 3, 0, 1]

            def at(n, each, j):
                return n * each - (each - 1 - j)

            GATE_LIST = [[GATE_I, GATE_G, GATE_O] if CELLS[c][1] == 0 else [GATE_I, GATE_G, GATE_F, GATE_O]
                         for c in range(NCELL)]
            GATE_AT = [sum(len(g) for g in GATE_LIST[:c]) for c in range(NCELL)]
            NGATE = sum(len(g) for g in GATE_LIST)
            STEPPED = [c for c in range(NCELL) if CELLS[c][1] > 0]

            def score(s, b, h):
                c = (b % 2 * 2 + h // 2) * P
                return ps[s][:, SCORE_BANK[b // 2 * 2] + h % 2, c:c + P]

            PLAIN = [LN_L0, LN_L1, LN_L2, LN_L3]
            GAINED = [LN_G1, LN_G2, LN_G3]

            def out_at(n, j):
                return at(n, len(PLAIN), PLAIN.index(j))

            def feat_at(n, j, m=KT - 1):
                return at(n, FEATS, j * KT + m)

            def gate_at(n, c, j):
                return at(n, NGATE, GATE_AT[c] + j)

            mem = pool_mem
            q = [m[:, 0:1024].rearrange("p (k n) -> p k n", k=KT) for m in mem]
            kk = [m[:, 1024:2048].rearrange("p (k n) -> p k n", k=KT) for m in mem]
            prob_tr = [m[:, 0:2048].rearrange("p (b h n) -> p b h n", b=BLK, h=HEADS) for m in mem]
            vv = [m[:, 2048:3072].rearrange("p (b d) -> p b d", b=BLK) for m in mem]
            prob = [m[:, 3072:5120].rearrange("p (b h n) -> p b h n", b=BLK, h=HEADS) for m in mem]
            gelu = [m[:, 0:2048].rearrange("p (m n) -> p m n", m=HT) for m in mem]
            gelu_hl = [m[:, 2048:4096].bitcast(F16).rearrange("p (c m n) -> p c m n", c=2, m=HT) for m in mem]
            wg = [m[:, 0:1024].rearrange("p (b d) -> p b d", b=BLK) for m in mem]
            gates = [m[:, 0:2048].rearrange("p (g n) -> p g n", g=4) for m in mem]
            cell_c = [m[:, 2048:2560] for m in mem]
            cell_t = [m[:, 2560:3072] for m in mem]
            cell_h = [m[:, 3072:3584] for m in mem]
            cell_hl = [m[:, 3584:4096].bitcast(F16).rearrange("p (c n) -> p c n", c=2) for m in mem]
            state = [m[:, 4096:5120].rearrange("p (k n) -> p k n", k=KT) for m in mem]
            state_hl = feat_dst[H1]
            wh = [m[:, 0:1024].rearrange("p (b d) -> p b d", b=BLK) for m in mem]
            logit = [m[:, 1024:1536].rearrange("p (b n) -> p b n", b=BLK) for m in mem]
            att = [m[:, 1536:2048].rearrange("p (b n) -> p b n", b=BLK) for m in mem]
            att_tr = [m[:, 2048:2560].rearrange("p (b n) -> p b n", b=BLK) for m in mem]
            s1 = [small[:, 8 + BLK * s:8 + BLK * s + BLK] for s in range(STREAMS)]
            xc = x1

            block = pctx.enter_context(nc.Block())

            @block.sync
            def _(sp):
                def load_o(s, r):
                    sp.dma_start(act_in[s][:, :, :], o_tiles[bass.ds(r, 1), s].rearrange("o p m n -> (o p) m n"))\
                        .then_inc(o_in[s], 16)

                def load_x(s, r):
                    sp.dma_start(xa[s][:, :, :], x_tiles[bass.ds(r, 1), s].rearrange("o p b d -> (o p) b d"))\
                        .then_inc(x_in[s], 16)

                def store(s, n):
                    sp.wait_ge(ln_out[s], out_at(n, LN_L3))
                    sp.dma_start(out_tiles[bass.ds(n - 1, 1), s].rearrange("o p b d -> (o p) b d"), xb[s][:, :, :])\
                        .then_inc(out_stored[s], 16)

                def load_next(s, n):
                    sp.wait_ge(y_ps[s], n)
                    load_o(s, n)
                    sp.wait_ge(pre_ok[s], n * 3)
                    load_x(s, n)

                for s in range(STREAMS):
                    load_o(s, 0)
                    load_x(s, 0)
                with sp.Fori(1, ROUNDS) as n:
                    for s in range(STREAMS):
                        load_next(s, n)
                        store(s, n)
                for s in range(STREAMS):
                    store(s, ROUNDS)
                for s in range(STREAMS):
                    sp.wait_ge(out_stored[s], 16 * ROUNDS + 1)

            @block.tensor
            def _(pe):
                def turn_y(s, n):
                    pe.wait_ge(banks_free[s], n)
                    pe.wait_ge(y_ok[s], n * KT)
                    for f in range(KT):
                        for b in range(BLK):
                            mm = nc.tensor.transpose(by_token(s, 0)[:, b, f * P:(f + 1) * P],
                                                     act_in[s][:, f, b * P:(b + 1) * P], ident[:, :])
                    mm.then_inc(y_ps[s], 1)

                def chebyshev(s, n):
                    pe.wait_ge(ln_out[s], out_at(n, LN_L0))
                    for f in range(KT):
                        for b in range(BLK):
                            mm = nc.tensor.matmul(by_feature(s, feat_bank[XP])[:, f, b * P:(b + 1) * P],
                                                  xa[s][:, b, f * P:(f + 1) * P], cheb_t[:, :], start=True, stop=True)
                        mm.then_inc(feat_ps[s], 1)

                def dense(s, src, name, bank):
                    kts = src.shape[2]
                    for b in range(BLK):
                        for k in range(kts):
                            mm = product(by_token(s, bank)[:, b, :],
                                         (src[:, 0, k, b * P:(b + 1) * P], src[:, 1, k, b * P:(b + 1) * P]),
                                         weight(name, k, 0, DIM), k == 0, k == kts - 1)
                    return mm

                def conv(s, n):
                    pe.wait_ge(feat_lo[s], feat_at(n, XP))
                    dense(s, hl_a[s][:, :, :, :], "wc", 0).then_inc(hc_ps[s], 1)

                def turn(s, src, j):
                    for f in range(KT):
                        for b in range(BLK):
                            mm = nc.tensor.transpose(by_feature(s, feat_bank[j])[:, f, b * P:(b + 1) * P],
                                                     src[s][:, b, f * P:(f + 1) * P], ident[:, :])
                        mm.then_inc(feat_ps[s], 1)

                def turn_x1(s, n):
                    pe.wait_ge(x1_ok[s], n)
                    turn(s, x1, X1T)

                def query(s, n):
                    pe.wait_ge(feat_lo[s], feat_at(n, X1T))
                    rows_of(s, "wq", 0).then_inc(q_ps[s], 1)

                def key(s, n):
                    rows_of(s, "wk", 2).then_inc(k_ps[s], 1)

                def value(s, n):
                    pe.wait_ge(q_ok[s], n)
                    dense(s, hl_b[s][:, :, :, :], "wv", 0).then_inc(v_ps[s], 1)

                def rows_of(s, name, bank):
                    src = hl_b[s]
                    for m in range(KT):
                        for k in range(KT):
                            mm = product(ps[s][:, bank + m, :], weight(name, k, m * P, P),
                                         (src[:, 0, k, :], src[:, 1, k, :]), k == 0, k == KT - 1)
                    return mm

                def scores(s, n):
                    pe.wait_ge(k_ok[s], n)
                    for b in range(BLK):
                        if b == 2:
                            pe.wait_ge(v_ok[s], n)
                        for h in range(HEADS):
                            d = slice(h % 2 * HEAD_DIM, h % 2 * HEAD_DIM + HEAD_DIM)
                            mm = nc.tensor.matmul(score(s, b, h), q[s][d, h // 2, b * P:(b + 1) * P],
                                                  kk[s][d, h // 2, b * P:(b + 1) * P], start=True, stop=True)
                            if b % 2 == 1 and h >= HEADS - 2:
                                mm.then_inc(score_ps[s], 1)

                def turn_probs(s, n):
                    for b in range(BLK):
                        if b % 2 == 0:
                            pe.wait_ge(masked_ok[s], at(n, BLK, b + 1))
                        pe.wait_ge(prob_ok[s], at(n, BLK, b))
                        for h in range(HEADS):
                            mm = nc.tensor.transpose(ps[s][:, SCORE_BANK[b], h * P:(h + 1) * P], prob[s][:, b, h, :],
                                                     ident[:, :])
                        mm.then_inc(prob_ps[s], 1)

                def attend(s, n):
                    pe.wait_ge(prob_t[s], n * BLK)
                    for pair in range(KT):
                        for b in range(BLK):
                            for h in (2 * pair, 2 * pair + 1):
                                d = slice(h % 2 * HEAD_DIM, h % 2 * HEAD_DIM + HEAD_DIM)
                                mm = nc.tensor.matmul(ps[s][d, feat_bank[OT] + pair, b * P:(b + 1) * P],
                                                      vv[s][:, b, h * HEAD_DIM:(h + 1) * HEAD_DIM], prob_tr[s][:, b, h, :],
                                                      start=True, stop=True)
                        mm.then_inc(feat_ps[s], 1)

                def attn_out(s, n):
                    pe.wait_ge(feat_lo[s], feat_at(n, OT))
                    dense(s, hl_a[s][:, :, :, :], "wo", 2).then_inc(wo_ps[s], 1)

                def turn_x2(s, n):
                    pe.wait_ge(x2_ok[s], n)
                    turn(s, x1, X2T)

                def mlp_up(s, n):
                    pe.wait_ge(feat_lo[s], feat_at(n, X2T))
                    src = hl_b[s]
                    for m in range(HT):
                        for k in range(KT):
                            mm = product(ps[s][:, HID_BANK[m], :], weight("w1", k, m * P, P),
                                         (src[:, 0, k, :], src[:, 1, k, :]), k == 0, k == KT - 1)
                        mm.then_inc(w1_ps[s], 1)

                def mlp_down(s, n):
                    pe.wait_ge(gelu_lo[s], n * HT)
                    dense(s, gelu_hl[s], "w2", 2).then_inc(w2_ps[s], 1)

                def turn_xb(s, n):
                    pe.wait_ge(ln_out[s], out_at(n, LN_L1))
                    turn(s, xb, XBT)

                def gcn_dense(s, n, j):
                    pe.wait_ge(feat_lo[s], feat_at(n, (XBT, H0)[j]))
                    dense(s, (hl_a, hl_b)[j][s][:, :, :, :], ("wg0", "wg1")[j], 2).then_inc(wg_ps[s], 1)

                def gcn_mix(s, n, j):
                    pe.wait_ge(wg_ok[s], at(n, 2, j))
                    for f in range(KT):
                        for b in range(BLK):
                            mm = nc.tensor.matmul(by_feature(s, 0)[:, f, b * P:(b + 1) * P],
                                                  wg[s][:, b, f * P:(f + 1) * P], at_bd[:, :], start=True, stop=True)
                        mm.then_inc(feat_ps[s], 1)

                def cell_input(s, n, c):
                    p, step, _ = CELLS[c]
                    w = cell_width(c)
                    if c == 0:
                        pe.wait_ge(feat_lo[s], feat_at(n, H1))
                    elif step == 0 and p > 1:
                        pe.wait_ge(h_lo[s], at(n, NCELL, c - 1))
                    if c > 0:
                        pe.wait_ge(gate_ok[s], gate_at(n, c, -1))
                    tok = [cell_tokens(state_hl[s][:, half, :, :], c) for half in range(2)]
                    for g in GATE_LIST[c]:
                        for m in range(KT):
                            o = ps[s][:, g, m * w:(m + 1) * w]
                            o = o if p == 1 else o.rearrange("q (b w) -> q b w", b=TILE_BATCHES)
                            for k in range(KT):
                                mm = product(o, weight(f"wih{p}", k, (g * KT + m) * P, P), (tok[0][:, k], tok[1][:, k]),
                                             m == 0 and k == 0, step == 0 and m == KT - 1 and k == KT - 1)
                        if step == 0:
                            mm.then_inc(gate_ps[s], 1)

                def cell_state(s, n, c):
                    p, step, _ = CELLS[c]
                    w = cell_width(c)
                    if step == 0:
                        return
                    pe.wait_ge(h_lo[s], at(n, NCELL, c - 1))
                    for g in GATE_LIST[c]:
                        for m in range(KT):
                            for k in range(KT):
                                mm = product(ps[s][:, g, m * w:(m + 1) * w], weight(f"whh{p}", k, (g * KT + m) * P, P),
                                             (cell_hl[s][:, 0, k * w:(k + 1) * w], cell_hl[s][:, 1, k * w:(k + 1) * w]),
                                             False, m == KT - 1 and k == KT - 1)
                        mm.then_inc(gate_ps[s], 1)

                def turn_state(s, n):
                    pe.wait_ge(h_ok[s], n * NCELL)
                    pe.wait_ge(gate_ok[s], n * NGATE)
                    for f in range(KT):
                        for b in range(BLK):
                            mm = nc.tensor.transpose(by_token(s, 0)[:, b, f * P:(f + 1) * P],
                                                     state[s][:, f, b * P:(b + 1) * P], ident[:, :])
                    mm.then_inc(hf_ps[s], 1)

                def turn_xc(s, n):
                    pe.wait_ge(ln_out[s], out_at(n, LN_L2))
                    turn(s, xc, XCT)

                def gat_dense(s, n):
                    pe.wait_ge(feat_lo[s], feat_at(n, XCT))
                    src = hl_b[s]
                    for k in range(KT):
                        product(ps[s][:, 2, :], (wa2[:, 0, k, :], wa2[:, 1, k, :]), (src[:, 0, k, :], src[:, 1, k, :]),
                                k == 0, k == KT - 1)
                    for b in range(BLK):
                        for k in range(KT):
                            mm = product(ps[s][:, 3, b:b + 1],
                                         (src[:, 0, k, b * P:(b + 1) * P], src[:, 1, k, b * P:(b + 1) * P]),
                                         (wa1[:, 0, k:k + 1], wa1[:, 1, k:k + 1]), k == 0, k == KT - 1)
                    mm.then_inc(s_ps[s], 1)
                    dense(s, src[:, :, :, :], "w3", 0).then_inc(wh_ps[s], 1)

                def turn_att(s, n):
                    pe.wait_ge(eexp_ok[s], n)
                    for b in range(BLK):
                        mm = nc.tensor.transpose(ps[s][:, 2, b * P:(b + 1) * P], att[s][:, b, :], ident[:, :])
                    mm.then_inc(att_ps[s], 1)

                def gat_mix(s, n):
                    pe.wait_ge(wh_ok[s], n)
                    pe.wait_ge(att_t[s], n)
                    for b in range(BLK):
                        mm = nc.tensor.matmul(by_token(s, 0)[:, b, :], att_tr[s][:, b, :], wh[s][:, b, :],
                                              start=True, stop=True)
                    mm.then_inc(av_ps[s], 1)

                steps = {"turn_y": turn_y, "cheb": chebyshev, "conv": conv, "turn_x1": turn_x1, "q": query, "k": key,
                         "v": value, "scores": scores, "turn_probs": turn_probs, "attend": attend, "attn_out": attn_out,
                         "turn_x2": turn_x2, "mlp_up": mlp_up, "mlp_down": mlp_down, "turn_xb": turn_xb,
                         "turn_state": turn_state, "turn_xc": turn_xc, "gat": gat_dense, "turn_att": turn_att,
                         "gat_mix": gat_mix}

                def run(name, s, n):
                    if name.startswith("cell"):
                        cell_state(s, n, int(name[4:]))
                    elif name.startswith("inp"):
                        cell_input(s, n, int(name[3:]))
                    elif name[:3] in ("gcn", "mix"):
                        (gcn_dense if name[:3] == "gcn" else gcn_mix)(s, n, int(name[3:]))
                    elif name in steps:
                        steps[name](s, n)

                for name, s, n in opening():
                    run(name, s, n)
                with pe.Fori(1, ROUNDS) as r:
                    for part in parts(r):
                        with pe.Fori(0, 1):
                            for name, s, n in part:
                                run(name, s, n)
                for name, s, n in closing():
                    run(name, s, n)

            @block.scalar
            def _(act):
                def norm_y(s, n):
                    act.wait_ge(o_in[s], n * 16)
                    for m in range(KT):
                        nc.scalar.activation(act_in[s][:, m, :], act_in[s][:, m, :], ACT.Identity,
                                             bias=bn2[:, 1, m:m + 1], scale=bn2[:, 0, m:m + 1]).then_inc(y_ok[s], 1)

                def ln_apply(s, n):
                    act.wait_ge(ln_nmr[s], n)
                    for b in range(BLK):
                        op = nc.scalar.activation(xb[s][:, b, :], t[s][:, b, :], ACT.Identity, bias=nmr[s][:, b:b + 1],
                                                  scale=rstd[s][:, b:b + 1])
                    op.then_inc(ln_out[s], 1)

                def high(s, n, j):
                    for m in range(KT):
                        act.wait_ge(feat_ps[s], feat_at(n, j, m))
                        nc.scalar.activation(feat_dst[j][s][:, 0, m, :], by_feature(s, feat_bank[j])[:, m, :],
                                             ACT.Relu if j in feat_relu else ACT.Copy).then_inc(feat_hi[s], 1)

                def take_q(s, n):
                    act.wait_ge(q_ps[s], n)
                    nc.scalar.activation(q[s], by_feature(s, 0), ACT.Copy, scale=UNSCALE * HEAD_DIM ** -0.5)\
                        .then_inc(q_ok[s], 1)

                def take_k(s, n):
                    act.wait_ge(k_ps[s], n)
                    nc.scalar.activation(kk[s], by_feature(s, 2), ACT.Copy, scale=UNSCALE).then_inc(k_ok[s], 1)

                def exps(s, n):
                    for b in range(BLK):
                        act.wait_ge(nmax_ok[s], at(n, BLK, b))
                        for h in range(HEADS):
                            i = b * HEADS + h
                            op = nc.scalar.activation(prob[s][:, b, h, :], prob[s][:, b, h, :], ACT.Exp,
                                                      bias=smax[s][:, i:i + 1], accum_out=ssum[s][:, i:i + 1])
                        op.then_inc(exp_ok[s], 1)

                def take_probs(s, n):
                    for b in range(BLK):
                        act.wait_ge(prob_ps[s], at(n, BLK, b))
                        nc.scalar.copy(prob_tr[s][:, b, :, :], ps[s][:, SCORE_BANK[b], :]
                                       .rearrange("p (h n) -> p h n", h=HEADS)).then_inc(prob_t[s], 1)

                def gelus(s, n):
                    for m in range(HT):
                        act.wait_ge(w1_ps[s], at(n, HT, m))
                        nc.scalar.activation(gelu[s][:, m, :], ps[s][:, HID_BANK[m], :], ACT.Gelu, bias=vec("l1_b1", m),
                                             scale=UNSCALE).then_inc(gelu_ok[s], 1)

                def gates_of(s, n, c):
                    p = CELLS[c][0]
                    w = cell_width(c)
                    if c == 1:
                        act.wait_ge(h_ok[s], at(n, NCELL, 0))
                        act.wait_ge(h_hi[s], at(n, NCELL, 0))
                    for j, g in enumerate(GATE_LIST[c]):
                        act.wait_ge(gate_ps[s], gate_at(n, c, j))
                        for m in range(KT):
                            bias = ((p - 1) * 4 + g) * KT + m
                            op = nc.scalar.activation(gates[s][:, g, m * w:(m + 1) * w], ps[s][:, g, m * w:(m + 1) * w],
                                                      ACT.Tanh, bias=lstm_b[:, bias:bias + 1],
                                                      scale=UNSCALE * (0.5 if g == GATE_G else 0.25))
                        op.then_inc(gate_ok[s], 1)

                def tanh_c(s, n, c):
                    w = cell_width(c)
                    act.wait_ge(c_ok[s], at(n, NCELL, c))
                    nc.scalar.activation(cell_t[s][:, 0:KT * w], cell_c[s][:, 0:KT * w], ACT.Tanh, scale=0.5)\
                        .then_inc(tanh_ok[s], 1)

                def take_wh(s, n):
                    act.wait_ge(wh_ps[s], n)
                    nc.scalar.activation(wh[s], by_token(s, 0), ACT.Copy, scale=UNSCALE).then_inc(wh_ok[s], 1)

                def gat_exps(s, n):
                    act.wait_ge(enmax_ok[s], n)
                    for b in range(BLK):
                        op = nc.scalar.activation(att[s][:, b, :], att[s][:, b, :], ACT.Exp, bias=smax[s][:, b:b + 1],
                                                  accum_out=ssum[s][:, b:b + 1])
                    op.then_inc(eexp_ok[s], 1)

                def take_att(s, n):
                    act.wait_ge(att_ps[s], n)
                    nc.scalar.copy(att_tr[s], ps[s][:, 2, :].rearrange("p (b n) -> p b n", b=BLK)).then_inc(att_t[s], 1)

                def run(name, s, n):
                    if name == "norm_y":
                        norm_y(s, n)
                    elif name == "q":
                        take_q(s, n)
                    elif name == "k":
                        take_k(s, n)
                    elif name == "exps":
                        exps(s, n)
                    elif name == "turn_probs":
                        take_probs(s, n)
                    elif name == "mlp_up":
                        gelus(s, n)
                    elif name.startswith("cell"):
                        gates_of(s, n, int(name[4:]))
                    elif name.startswith("hid"):
                        tanh_c(s, n, int(name[3:]))
                    elif name == "gat":
                        take_wh(s, n)
                    elif name == "gat_exps":
                        gat_exps(s, n)
                    elif name == "turn_att":
                        take_att(s, n)
                    elif name == "norm_l3":
                        ln_apply(s, n)
                    elif name in FEAT_OF:
                        high(s, n, FEAT_OF[name])

                for name, s, n in opening():
                    run(name, s, n)
                with act.Fori(1, ROUNDS) as r:
                    for part in parts(r):
                        with act.Fori(0, 1):
                            for name, s, n in part:
                                run(name, s, n)
                for name, s, n in closing():
                    run(name, s, n)

            @block.gpsimd
            def _(pool):
                def ln_root(s, n, j):
                    pool.wait_ge(ln_ve[s], at(n, NORMS, j))
                    nc.gpsimd.tensor_tensor(rstd[s][:, :], ve[s][:, :], nhalf[:, 0:BLK], ALU.pow).then_inc(ln_rstd[s], 1)

                def x1_bias(s, n):
                    pool.wait_ge(x1_ok[s], n)
                    pool.wait_ge(out_stored[s], n * 16 - 15)
                    nc.gpsimd.tensor_tensor(xb[s][:, :, :], x1[s][:, :, :], row_of("bo"), ALU.add).then_inc(pre_ok[s], 1)

                def probs(s, n):
                    for b in range(BLK):
                        pool.wait_ge(inv_ok[s], at(n, BLK, b))
                        nc.gpsimd.tensor_tensor(prob[s][:, b, :, :], prob[s][:, b, :, :],
                                                ssum[s][:, b * HEADS:(b + 1) * HEADS].unsqueeze(2)
                                                .broadcast_to([P, HEADS, P]), ALU.mult).then_inc(prob_ok[s], 1)

                def x2_bias(s, n):
                    pool.wait_ge(x2_ok[s], n)
                    nc.gpsimd.tensor_tensor(xb[s][:, :, :], x1[s][:, :, :], row_of("b2"), ALU.add).then_inc(pre_ok[s], 1)

                def gelu_high(s, n):
                    for m in range(HT):
                        pool.wait_ge(gelu_ok[s], at(n, HT, m))
                        nc.gpsimd.tensor_tensor(gelu_hl[s][:, 0, m, :], gelu[s][:, m, :],
                                                zero[:, 0:1].broadcast_to([P, TILE]), ALU.add)\
                            .then_inc(gelu_hi[s], 1)

                def xa_bias(s, n):
                    pool.wait_ge(pre_ok[s], at(n, 3, 1))
                    pool.wait_ge(feat_ps[s], feat_at(n, X2T))
                    nc.gpsimd.tensor_tensor(x1[s][:, :, :], xa[s][:, :, :], row_of("be3"), ALU.add).then_inc(pre_ok[s], 1)

                def cell(s, n, c):
                    w = cell_width(c)
                    o, th, hi = gates[s][:, GATE_O, 0:KT * w], cell_t[s][:, 0:KT * w], cell_hl[s][:, 0, 0:KT * w]
                    if is_last_step(c):
                        o, th = (like_cell(x.rearrange("q (k w) -> q k w", k=KT), c) for x in (o, th))
                        hi = cell_tokens(state_hl[s][:, 0, :, :], c)
                    pool.wait_ge(o_ok[s], at(n, NCELL, c))
                    pool.wait_ge(tanh_ok[s], at(n, NCELL, c))
                    nc.gpsimd.tensor_tensor(hi, o, th, ALU.mult).then_inc(h_hi[s], 1)

                def run(name, s, n):
                    if name in NORM_OF:
                        ln_root(s, n, NORM_OF[name])
                    elif name == "x1_bias":
                        x1_bias(s, n)
                    elif name == "exps":
                        probs(s, n)
                    elif name == "x2_bias":
                        x2_bias(s, n)
                    elif name == "gelu_split":
                        gelu_high(s, n)
                    elif name == "xa_bias":
                        xa_bias(s, n)
                    elif name.startswith("hid"):
                        cell(s, n, int(name[3:]))

                for name, s, n in opening():
                    run(name, s, n)
                with pool.Fori(1, ROUNDS) as r:
                    for part in parts(r):
                        with pool.Fori(0, 1):
                            for name, s, n in part:
                                run(name, s, n)
                for name, s, n in closing():
                    run(name, s, n)

            @block.vector
            def _(dve):
                for s in range(STREAMS):
                    nc.vector.memset(small[:, 42 + s:43 + s], 0.0).then_inc(banks_free[s], 1)
                    nc.vector.memset(small[:, 44 + s:45 + s], 0.0).then_inc(out_stored[s], 1)

                held = [0]

                def wait_apart(semaphore, value):
                    dve.wait_ge(semaphore, value)
                    nc.vector.memset(hold[:, held[0]:held[0] + 1], 0.0)
                    held[0] += 1

                def ln(s, n, j):
                    dve.wait_ge(t_ok[s], at(n, NORMS, j))
                    for b in range(BLK):
                        op = nc.vector.bn_stats(stats[s][:, b, :], t[s][:, b, :])
                    op.then_inc(ln_stats[s], 1)
                    wait_apart(ln_stats[s], at(n, NORMS, j))
                    for b in range(BLK):
                        op = nc.vector.bn_aggr(mv[s][:, b, :], stats[s][:, b, :])
                    op.then_inc(ln_mv[s], 1)
                    dve.wait_ge(ln_mv[s], at(n, NORMS, j))
                    nc.vector.tensor_scalar(ve[s][:, :], mv[s][:, :, 1], EPS, None, ALU.add).then_inc(ln_ve[s], 1)

                def ln_apply(s, n, j, dst):
                    dve.wait_ge(ln_rstd[s], at(n, NORMS, j))
                    for b in range(BLK):
                        op = nc.vector.tensor_scalar(dst[s][:, b, :], t[s][:, b, :], mv[s][:, b, 0:1], rstd[s][:, b:b + 1],
                                                     ALU.subtract, ALU.mult)
                    op.then_inc(ln_out[s], 1)

                def ln_affine(s, n, j, gain, shift, dst):
                    dve.wait_ge(ln_mv[s], at(n, NORMS, j))
                    for b in range(BLK):
                        op = nc.vector.scalar_tensor_tensor(t[s][:, b, :], t[s][:, b, :], mv[s][:, b, 0:1],
                                                            row_of(gain)[:, b, :], ALU.subtract, ALU.mult)
                    op.then_inc(centred[s], 1)
                    dve.wait_ge(centred[s], at(n, len(GAINED), GAINED.index(j)))
                    dve.wait_ge(ln_rstd[s], at(n, NORMS, j))
                    for b in range(BLK):
                        op = nc.vector.scalar_tensor_tensor(dst[s][:, b, :], t[s][:, b, :], rstd[s][:, b:b + 1],
                                                            shift[:, b, :], ALU.mult, ALU.add)
                    return op

                def ln_shift(s, n):
                    dve.wait_ge(ln_rstd[s], at(n, NORMS, LN_L3))
                    nc.vector.scalar_tensor_tensor(nmr[s][:, :], mv[s][:, :, 0], -1.0, rstd[s][:, :], ALU.mult, ALU.mult)\
                        .then_inc(ln_nmr[s], 1)

                def add_y(s, n):
                    dve.wait_ge(x_in[s], n * 16)
                    dve.wait_ge(y_ps[s], n)
                    nc.vector.tensor_tensor(t[s][:, :, :], by_token(s, 0), xa[s][:, :, :], ALU.add).then_inc(t_ok[s], 1)
                    ln(s, n, LN_L0)

                def low(s, n, j):
                    for m in range(KT):
                        dve.wait_ge(feat_hi[s], feat_at(n, j, m))
                        hi, lo = feat_dst[j][s][:, 0, m, :], feat_dst[j][s][:, 1, m, :]
                        src = by_feature(s, feat_bank[j])[:, m, :]
                        if j in feat_relu:
                            nc.vector.scalar_tensor_tensor(lo, src, 0.0, hi, ALU.max, ALU.subtract).then_inc(feat_lo[s], 1)
                        else:
                            nc.vector.tensor_tensor(lo, src, hi, ALU.subtract).then_inc(feat_lo[s], 1)

                def conv_bias(s, n):
                    dve.wait_ge(hc_ps[s], n)
                    nc.vector.scalar_tensor_tensor(t[s][:, :, :], by_token(s, 0), UNSCALE, row_of("bc"), ALU.mult, ALU.add)\
                        .then_inc(t_ok[s], 1)
                    ln(s, n, LN_G1)

                def make_x1(s, n):
                    ln_affine(s, n, LN_G1, "g1", row_of("be1"), t).then_inc(affine_ok[s], 1)
                    dve.wait_ge(affine_ok[s], n)
                    nc.vector.scalar_tensor_tensor(x1[s][:, :, :], t[s][:, :, :], 0.0, xa[s][:, :, :], ALU.max, ALU.add)\
                        .then_inc(x1_ok[s], 1)

                def take_v(s, n):
                    dve.wait_ge(v_ps[s], n)
                    nc.vector.tensor_scalar(vv[s], by_token(s, 0), UNSCALE, None, ALU.mult).then_inc(v_ok[s], 1)

                def mask_scores(s, n):
                    for b in range(BLK):
                        if b % 2 == 0:
                            wait_apart(score_ps[s], at(n, BLK, b + 1))
                        for h in range(HEADS):
                            i = b * HEADS + h
                            op = nc.vector.tensor_tensor_reduce(prob[s][:, b, h, :],
                                                                score(s, b, h), mask1[:, :],
                                                                1.0, -3.0e38, ALU.add, ALU.max, smax[s][:, i:i + 1])
                        op.then_inc(masked_ok[s], 1)
                        dve.wait_ge(masked_ok[s], at(n, BLK, b))
                        part = smax[s][:, b * HEADS:(b + 1) * HEADS]
                        nc.vector.tensor_scalar(part, part, -1.0, None, ALU.mult).then_inc(nmax_ok[s], 1)

                def invert_sums(s, n):
                    for b in range(BLK):
                        dve.wait_ge(exp_ok[s], at(n, BLK, b))
                        part = ssum[s][:, b * HEADS:(b + 1) * HEADS]
                        nc.vector.reciprocal(part, part).then_inc(inv_ok[s], 1)

                def add_attn(s, n):
                    dve.wait_ge(pre_ok[s], at(n, 3, 0))
                    dve.wait_ge(wo_ps[s], n)
                    nc.vector.scalar_tensor_tensor(t[s][:, :, :], by_token(s, 2), UNSCALE, xb[s][:, :, :], ALU.mult, ALU.add)\
                        .then_inc(t_ok[s], 1)
                    ln(s, n, LN_G2)

                def make_x2(s, n):
                    ln_affine(s, n, LN_G2, "g2", row_of("be2"), x1).then_inc(x2_ok[s], 1)

                def gelu_low(s, n):
                    for m in range(HT):
                        dve.wait_ge(gelu_hi[s], at(n, HT, m))
                        nc.vector.tensor_tensor(gelu_hl[s][:, 1, m, :], gelu[s][:, m, :], gelu_hl[s][:, 0, m, :],
                                                ALU.subtract).then_inc(gelu_lo[s], 1)

                def add_mlp(s, n):
                    dve.wait_ge(pre_ok[s], at(n, 3, 1))
                    dve.wait_ge(w2_ps[s], n)
                    nc.vector.scalar_tensor_tensor(t[s][:, :, :], by_token(s, 2), UNSCALE, xb[s][:, :, :], ALU.mult, ALU.add)\
                        .then_inc(t_ok[s], 1)
                    ln(s, n, LN_G3)

                def add_xa(s, n):
                    dve.wait_ge(pre_ok[s], at(n, 3, 2))
                    ln_affine(s, n, LN_G3, "g3", x1[s][:, :, :], t).then_inc(t_ok[s], 1)
                    ln(s, n, LN_L1)

                def gcn_bias(s, n, j):
                    dve.wait_ge(wg_ps[s], at(n, 2, j))
                    nc.vector.scalar_tensor_tensor(wg[s], by_token(s, 2), UNSCALE * (j + 1), row_of(("bg0", "bg1")[j]),
                                                   ALU.mult, ALU.add).then_inc(wg_ok[s], 1)

                def cell_sum(s, n, c):
                    w = cell_width(c)
                    g = [gates[s][:, j, 0:KT * w] for j in range(4)]
                    cc = cell_c[s][:, 0:KT * w]
                    first = CELLS[c][1] == 0
                    dve.wait_ge(gate_ok[s], gate_at(n, c, 1))
                    nc.vector.scalar_tensor_tensor(cc if first else g[GATE_I], g[GATE_I], 1.0, g[GATE_G], ALU.add,
                                                   ALU.mult).then_inc(c_ok[s] if first else ig_ok[s], 1)
                    if not first:
                        i = STEPPED.index(c)
                        dve.wait_ge(gate_ok[s], gate_at(n, c, 2))
                        nc.vector.scalar_tensor_tensor(cc, g[GATE_F], 1.0, cc, ALU.add, ALU.mult).then_inc(fc_ok[s], 1)
                        dve.wait_ge(fc_ok[s], at(n, len(STEPPED), i))
                        nc.vector.scalar_tensor_tensor(cc, cc, 0.5, g[GATE_I], ALU.mult, ALU.add).then_inc(c_ok[s], 1)
                    dve.wait_ge(gate_ok[s], gate_at(n, c, len(GATE_LIST[c]) - 1))
                    nc.vector.tensor_scalar(g[GATE_O], g[GATE_O], 1.0, None, ALU.add).then_inc(o_ok[s], 1)

                def cell_out(s, n, c):
                    w = cell_width(c)
                    o, th = gates[s][:, GATE_O, 0:KT * w], cell_t[s][:, 0:KT * w]
                    if is_last_step(c):
                        h, hi, lo = (cell_tokens(x, c) for x in
                                     (state[s], state_hl[s][:, 0, :, :], state_hl[s][:, 1, :, :]))
                        o, th = (like_cell(x.rearrange("q (k w) -> q k w", k=KT), c) for x in (o, th))
                    else:
                        h, hi, lo = cell_h[s][:, 0:KT * w], cell_hl[s][:, 0, 0:KT * w], cell_hl[s][:, 1, 0:KT * w]
                    dve.wait_ge(o_ok[s], at(n, NCELL, c))
                    dve.wait_ge(tanh_ok[s], at(n, NCELL, c))
                    nc.vector.tensor_tensor(h, o, th, ALU.mult).then_inc(h_ok[s], 1)
                    dve.wait_ge(h_ok[s], at(n, NCELL, c))
                    dve.wait_ge(h_hi[s], at(n, NCELL, c))
                    nc.vector.tensor_tensor(lo, h, hi, ALU.subtract).then_inc(h_lo[s], 1)

                def add_state(s, n):
                    dve.wait_ge(hf_ps[s], n)
                    nc.vector.scalar_tensor_tensor(t[s][:, :, :], by_token(s, 0), 0.5, xb[s][:, :, :], ALU.mult, ALU.add)\
                        .then_inc(t_ok[s], 1)
                    ln(s, n, LN_L2)

                def gat_logits(s, n):
                    dve.wait_ge(s_ps[s], n)
                    nc.vector.tensor_scalar(s1[s], ps[s][:, 3, 0:BLK], UNSCALE, None, ALU.mult).then_inc(s1_ok[s], 1)
                    dve.wait_ge(s1_ok[s], n)
                    for b in range(BLK):
                        op = nc.vector.tensor_scalar(logit[s][:, b, :], ps[s][:, 2, b * P:(b + 1) * P], UNSCALE,
                                                     s1[s][:, b:b + 1], ALU.mult, ALU.add)
                    op.then_inc(e_ok[s], 1)
                    dve.wait_ge(e_ok[s], n)
                    nc.vector.scalar_tensor_tensor(logit[s], logit[s], 0.2, logit[s], ALU.mult, ALU.max)\
                        .then_inc(lrelu_ok[s], 1)
                    wait_apart(lrelu_ok[s], n)
                    for b in range(BLK):
                        op = nc.vector.tensor_tensor_reduce(att[s][:, b, :], logit[s][:, b, :], mask3[:, :], 1.0, -3.0e38,
                                                            ALU.add, ALU.max, smax[s][:, b:b + 1])
                    op.then_inc(emask_ok[s], 1)
                    dve.wait_ge(emask_ok[s], n)
                    nc.vector.tensor_scalar(smax[s][:, 0:BLK], smax[s][:, 0:BLK], -1.0, None, ALU.mult)\
                        .then_inc(enmax_ok[s], 1)

                def gat_sums(s, n):
                    dve.wait_ge(eexp_ok[s], n)
                    nc.vector.reciprocal(ssum[s][:, 0:BLK], ssum[s][:, 0:BLK]).then_inc(einv_ok[s], 1)

                def add_gat(s, n):
                    dve.wait_ge(einv_ok[s], n)
                    dve.wait_ge(av_ps[s], n)
                    for b in range(BLK):
                        op = nc.vector.scalar_tensor_tensor(t[s][:, b, :], by_token(s, 0)[:, b, :], ssum[s][:, b:b + 1],
                                                            xc[s][:, b, :], ALU.mult, ALU.add)
                    op.then_inc(t_ok[s], 1)
                    ln(s, n, LN_L3)
                    nc.vector.memset(small[:, 42 + s:43 + s], 0.0).then_inc(banks_free[s], 1)

                def run(name, s, n):
                    if name == "turn_y":
                        add_y(s, n)
                    elif name == "norm_l0":
                        ln_apply(s, n, LN_L0, xa)
                    elif name == "conv":
                        conv_bias(s, n)
                    elif name == "norm_g1":
                        make_x1(s, n)
                    elif name == "v":
                        take_v(s, n)
                    elif name == "scores":
                        mask_scores(s, n)
                    elif name == "exps":
                        invert_sums(s, n)
                    elif name == "attn_out":
                        add_attn(s, n)
                    elif name == "norm_g2":
                        make_x2(s, n)
                    elif name == "gelu_split":
                        gelu_low(s, n)
                    elif name == "mlp_down":
                        add_mlp(s, n)
                    elif name == "norm_g3":
                        add_xa(s, n)
                    elif name == "norm_l1":
                        ln_apply(s, n, LN_L1, xb)
                    elif name.startswith("gcn"):
                        gcn_bias(s, n, int(name[3:]))
                    elif name.startswith("cell"):
                        cell_sum(s, n, int(name[4:]))
                    elif name.startswith("hid"):
                        cell_out(s, n, int(name[3:]))
                    elif name == "turn_state":
                        add_state(s, n)
                    elif name == "norm_l2":
                        ln_apply(s, n, LN_L2, xc)
                    elif name == "gat":
                        gat_logits(s, n)
                    elif name == "gat_exps":
                        gat_sums(s, n)
                    elif name == "gat_mix":
                        add_gat(s, n)
                    elif name == "norm_l3":
                        ln_shift(s, n)
                    elif name in FEAT_OF:
                        low(s, n, FEAT_OF[name])

                for name, s, n in opening():
                    run(name, s, n)
                with dve.Fori(1, ROUNDS) as r:
                    for part in parts(r):
                        with dve.Fori(0, 1):
                            for name, s, n in part:
                                run(name, s, n)
                for name, s, n in closing():
                    run(name, s, n)


def kernel(**inputs):
    import numpy as np
    import concourse.bacc as bacc
    from concourse.bass_utils import run_bass_kernel_spmd

    given = {k: np.asarray(v) for k, v in inputs.items()}

    def turned(a):
        return np.swapaxes(a, -1, -2)

    mats = {"l0_w1": turned(given["L0_gnn_W1"]), "l0_w2": turned(given["L0_gnn_W2"]), "wc": given["L1_gnn_Wc"],
            "wq": given["L1_gnn_Wq"], "wk": given["L1_gnn_Wk"], "wv": given["L1_gnn_Wv"], "wo": given["L1_gnn_Wo"],
            "w1": given["L1_gnn_W1"], "w2": given["L1_gnn_W2"], "wg0": given["L2_gnn_Wg0"], "wg1": given["L2_gnn_Wg1"],
            "w3": given["L3_gnn_W"]}
    for p in range(1, SKIPS + 1):
        mats[f"wih{p}"] = turned(given["L2_gnn_Wih"][p - 1])
        mats[f"whh{p}"] = turned(given["L2_gnn_Whh"][p - 1])

    def tiled(w):
        return w.reshape(-1, P, w.shape[1]).transpose(1, 0, 2).reshape(P, -1)

    vectors = {"b1": given["L0_gnn_b1"], "g1": given["L0_gnn_g1"], "be1": given["L0_gnn_be1"], "b2": given["L0_gnn_b2"],
               "g2": given["L0_gnn_g2"], "be2": given["L0_gnn_be2"], "l1_b1": given["L1_gnn_b1"],
               "bih": given["L2_gnn_bih"], "bhh": given["L2_gnn_bhh"], "a": given["L3_gnn_a"]}
    lines = {r: given[f"L1_gnn_{r}"] for r in ROWS if not r.startswith("bg")}
    lines |= {r: given[f"L2_gnn_{r}"] for r in ROWS if r.startswith("bg")}
    arrays = {
        "in_x": given["x"],
        "in_adj": given["adj"],
        "in_adj_t": turned(given["adj"]),
        "in_wpack": np.concatenate([tiled(mats[name]) for name, _, _ in WEIGHTS], axis=1),
        "in_w3t": tiled(turned(given["L3_gnn_W"])).reshape(P, KT, DIM),
        "in_cols": np.concatenate([vectors[name].reshape(-1, P).T for name, _ in COLS], axis=1),
        "in_rows": np.stack([lines[r] for r in ROWS]),
    }
    arrays = {k: np.ascontiguousarray(v) for k, v in arrays.items()}
    nc = bacc.Bacc("TRN2", target_bir_lowering=False, num_devices=1)
    args = [nc.dram_tensor(k, v.shape, mybir.dt.from_np(v.dtype), kind="ExternalInput").ap() for k, v in arrays.items()]
    out = nc.dram_tensor("out", (BATCH, NODES, DIM), F32, kind="ExternalOutput").ap()
    build(nc, *args, out)
    result = run_bass_kernel_spmd(nc, [arrays], core_ids=[0])
    return result.results[0]["out"]
```

```python
from contextlib import ExitStack

import concourse.bass as bass
from concourse import mybir

F32 = mybir.dt.float32
F16 = mybir.dt.float16
ALU = mybir.AluOpType
ACT = mybir.ActivationFunctionType
AX = mybir.AxisListType

P = 128
BATCH, NODES, DIM = 128, 64, 256
HID = 2 * DIM
HEADS = 4
HEAD_DIM = DIM // HEADS
GATES = 4 * DIM
SKIPS = 4
KT = DIM // P
HT = HID // P
TILE = 512
BLK = TILE // P
TILE_BATCHES = TILE // NODES
TILES = BATCH * NODES // TILE
STREAMS = 2
ROUNDS = TILES // STREAMS
BANKS = 4
EPS = 1e-5
WSCALE = 256.0
UNSCALE = 1.0 / WSCALE
SQUARES = 4
SQUARINGS = SQUARES * (ROUNDS - 1)
MASK_L1, MASK_OFF, MASK_L3 = 1.0e9, 2.0e9, 1.0e30

WEIGHTS = [("l0_w1", DIM, HID), ("l0_w2", HID, DIM), ("wc", DIM, DIM), ("wq", DIM, DIM), ("wk", DIM, DIM),
           ("wv", DIM, DIM), ("wo", DIM, DIM), ("w1", DIM, HID), ("w2", HID, DIM), ("wg0", DIM, DIM),
           ("wg1", DIM, DIM), ("w3", DIM, DIM)]
WEIGHTS += [(f"wih{p}", DIM, GATES) for p in range(1, SKIPS + 1)]
WEIGHTS += [(f"whh{p}", DIM, GATES) for p in range(2, SKIPS + 1)]
UNIT = 1408
STAGES = 2


def weight_places():
    at, place = 0, {}
    for name, rows, width in WEIGHTS:
        place[name] = (at, width)
        at += rows // P * width
    return place, at


W_AT, W_COLS = weight_places()
assert W_AT["l0_w1"][0] == 0 and DIM // P * HID <= UNIT
UNITS = W_COLS // UNIT
assert UNITS * UNIT == W_COLS

COLS = [("b1", HT), ("g1", HT), ("be1", HT), ("b2", KT), ("g2", KT), ("be2", KT), ("l1_b1", HT),
        ("bih", SKIPS * GATES // P), ("bhh", SKIPS * GATES // P), ("a", 2 * KT)]
ROWS = ["bc", "g1", "be1", "bo", "g2", "be2", "b2", "g3", "be3", "bg0", "bg1"]


def col_places():
    at, place = 0, {}
    for name, n in COLS:
        place[name] = (at, n)
        at += n
    return place, at


C_AT, C_COLS = col_places()

PARTS = 2
SECOND, FIRST = "second", "first"
FIRST_HALF = """
norm_y turn_y norm_l0 cheb conv norm_g1 turn_x1 q x1_bias k v scores exps turn_probs attend attn_out norm_g2
turn_x2 x2_bias mlp_up gelu_split xa_bias mlp_down norm_g3 norm_l1 turn_xb gcn0 mix0
""".split()
ORDER = """
gcn1 norm_y mix1 turn_y inp0 cell0 norm_l0 hid0 inp1 cell1 cheb hid1 conv norm_g1 inp2 cell2 hid2 inp3 turn_x1
cell3 hid3 q x1_bias k inp4 cell4 hid4 v scores exps inp5 cell5 hid5 turn_probs inp6 cell6 hid6 attend inp7
cell7 hid7 inp8 cell8 hid8 inp9 attn_out cell9 hid9 inp10 norm_g2 cell10 hid10 turn_x2 turn_state norm_l2
x2_bias mlp_up gelu_split xa_bias turn_xc mlp_down norm_g3 gat norm_l1 gat_exps turn_xb turn_att gcn0 gat_mix
mix0 norm_l3
""".split()
SCHEDULE = [(FIRST if step in FIRST_HALF else SECOND, step) for step in ORDER]


def beside(second, first):
    given = {SECOND: second, FIRST: first}
    return [(name, *given[half]) for half, name in SCHEDULE if given[half] is not None]


def opening():
    return beside(None, (0, 1))


def rounds(n):
    return beside((0, n), (1, n)) + beside((1, n), (0, n + 1))


def parts(n):
    steps = rounds(n)
    part = -(-len(steps) // PARTS)
    return [steps[i:i + part] for i in range(0, len(steps), part)]


def closing():
    return beside((0, ROUNDS), (1, ROUNDS)) + beside((1, ROUNDS), None)


CELLS = [(1, 0, 0), (1, 0, TILE // 2)]
CELLS += [(p, step, None) for p in range(2, SKIPS + 1) for step in range(p)]
NCELL = len(CELLS)
GATE_I, GATE_F, GATE_G, GATE_O = range(4)
NORMS = 7
LN_L0, LN_G1, LN_G2, LN_G3, LN_L1, LN_L2, LN_L3 = range(NORMS)


def cell_width(c):
    p = CELLS[c][0]
    return TILE // 2 if p == 1 else TILE_BATCHES * (NODES // p)


def cell_tokens(buf, c):
    p, step, first = CELLS[c]
    if first is not None:
        return buf[:, :, first:first + TILE // 2]
    windows = NODES // p
    return buf.rearrange("q k (b t) -> q k b t", t=NODES)[:, :, :, step:step + (windows - 1) * p + 1:p]


def like_cell(ap, c):
    p, _, first = CELLS[c]
    return ap if first is not None else ap.rearrange("q k (b w) -> q k b w", b=TILE_BATCHES)


def is_last_step(c):
    return CELLS[c][1] == CELLS[c][0] - 1


def build(nc, x, adj, adj_t, wpack, w3t, cols, rows, out):
    ctx = ExitStack()
    with ctx:
        def sb(name, shape, dt=F32):
            return ctx.enter_context(nc.sbuf_tensor(name, shape, dt))

        def sem(name):
            return ctx.enter_context(nc.semaphore(name))

        def sems(name):
            return [sem(f"{name}_{s}") for s in range(STREAMS)]

        w_hi = sb("w_hi", [P, W_COLS], F16)
        w_lo = sb("w_lo", [P, W_COLS], F16)
        col = sb("col", [P, C_COLS])
        row = sb("row", [P, len(ROWS), DIM])
        ident = sb("ident", [P, P])
        a_bd = sb("a_bd", [P, P])
        at_bd = sb("at_bd", [P, P])
        gcn_t = sb("gcn_t", [P, P])
        cheb_t = sb("cheb_t", [P, P])
        mask1 = sb("mask1", [P, P])
        mask3 = sb("mask3", [P, P])
        lstm_b = sb("lstm_b", [P, SKIPS * GATES // P])
        wa1 = sb("wa1", [P, 2, KT], F16)
        wa2 = sb("wa2", [P, 2, KT, P], F16)
        bn1 = sb("bn1", [P, 2, HT])
        bn2 = sb("bn2", [P, 2, KT])
        small = sb("small", [P, 64])
        setup = sb("setup", [P, 32])
        act_in = [sb(f"act_in_{s}", [P, KT, TILE]) for s in range(STREAMS)]
        xa = [sb(f"xa_{s}", [P, BLK, DIM]) for s in range(STREAMS)]
        t = [sb(f"t_{s}", [P, BLK, DIM]) for s in range(STREAMS)]
        x1 = [sb(f"x1_{s}", [P, BLK, DIM]) for s in range(STREAMS)]
        xb = [sb(f"xb_{s}", [P, BLK, DIM]) for s in range(STREAMS)]
        hl_a = [sb(f"hl_a_{s}", [P, 2, KT, TILE], F16) for s in range(STREAMS)]
        hl_b = [sb(f"hl_b_{s}", [P, 2, KT, TILE], F16) for s in range(STREAMS)]
        pool_mem = [sb(f"pool_mem_{s}", [P, 5 * KT * TILE]) for s in range(STREAMS)]
        stats = [sb(f"stats_{s}", [P, BLK, 6]) for s in range(STREAMS)]
        mv = [sb(f"mv_{s}", [P, BLK, 2]) for s in range(STREAMS)]
        ve = [sb(f"ve_{s}", [P, BLK]) for s in range(STREAMS)]
        rstd = [sb(f"rstd_{s}", [P, BLK]) for s in range(STREAMS)]
        nmr = [sb(f"nmr_{s}", [P, BLK]) for s in range(STREAMS)]
        zero = sb("zero", [P, 1])
        hold = sb("hold", [P, 128])
        nhalf = sb("nhalf", [P, 2 * BLK])
        smin = [sb(f"smin_{s}", [P, BLK * HEADS]) for s in range(STREAMS)]
        ssum = [sb(f"ssum_{s}", [P, BLK * HEADS]) for s in range(STREAMS)]
        bnst1 = sb("bnst1", [P, HT, TILES, 6])
        bnst2 = sb("bnst2", [P, KT, TILES, 6])
        ps = [ctx.enter_context(nc.psum_tensor(f"ps_{s}", [P, BANKS, 512], F32)) for s in range(STREAMS)]

        h_dram = nc.dram_tensor("h_scratch", [TILES, P, HT, TILE], F32, kind="Internal").ap()
        o_dram = nc.dram_tensor("o_scratch", [TILES, P, KT, TILE], F32, kind="Internal").ap()
        x_tiles = x.rearrange("(r s b2 b) n d -> r s (b n) b2 d", r=ROUNDS, s=STREAMS, b=P // NODES)
        out_tiles = out.rearrange("(r s b2 b) n d -> r s (b n) b2 d", r=ROUNDS, s=STREAMS, b=P // NODES)
        h_tiles = h_dram.rearrange("(r s) p m n -> r s p m n", s=STREAMS)
        o_tiles = o_dram.rearrange("(r s) p m n -> r s p m n", s=STREAMS)

        def weight(name, k, c0, n):
            at, width = W_AT[name]
            a = at + k * width + c0
            return w_hi[:, a:a + n], w_lo[:, a:a + n]

        def vec(name, m):
            return col[:, C_AT[name][0] + m:C_AT[name][0] + m + 1]

        def vecs(name):
            a, n = C_AT[name]
            return col[:, a:a + n]

        def row_of(name):
            return row[:, ROWS.index(name), :].unsqueeze(1).broadcast_to([P, BLK, DIM])

        def product(o, l, r, first, last):
            nc.tensor.matmul(o, l[0], r[0], start=first, stop=False, skip_group_check=True)
            nc.tensor.matmul(o, l[0], r[1], start=False, stop=False, skip_group_check=True)
            return nc.tensor.matmul(o, l[1], r[0], start=False, stop=last, skip_group_check=True)

        def zeros_like(ap):
            z = zero[:, 0:1]
            while len(z.shape) < len(ap.shape):
                z = z.unsqueeze(1)
            return z.broadcast_to(list(ap.shape))

        def by_token(s, b):
            return ps[s][:, b:b + 2, :].rearrange("p b (c f) -> p (b c) f", f=DIM)

        def by_feature(s, b):
            return ps[s][:, b:b + KT, :]

        h_in = [sems(f"h_in_{i}") for i in range(2)]
        x3_in = sems("x3_in")

        used = []

        with ExitStack() as pctx:
            def psem(name):
                used.append(pctx.enter_context(nc.semaphore(name)))
                return used[-1]

            def psems(name):
                return [psem(f"{name}_{s}") for s in range(STREAMS)]

            zeroed = psem("zeroed")
            adj_in = psem("adj_in")
            vec_in = psem("vec_in")
            row_in = psem("row_in")
            w_in = [psem(f"w_in_{b}") for b in range(STAGES)]
            unit_hi = psem("unit_hi")
            unit_lo = psem("unit_lo")
            ident_ok = psem("ident_ok")
            step = psem("step")
            pow_ok = psem("pow_ok")
            gcn_ps = psem("gcn_ps")
            sq_ps = psem("sq_ps")
            sq_ready = psem("sq_ready")
            lam_ps = psem("lam_ps")
            wa_ps = psem("wa_ps")
            x_in, agg_ps, agg_hi, agg_lo, hid_ps, hid_out, hid_stats, hid_stored = (
                psems(n) for n in ("p1_x_in", "agg_ps", "agg_hi", "agg_lo", "hid_ps", "hid_out", "hid_stats", "hid_stored"))
            bn_step, bn_pow = psem("bn1_step"), psem("bn1_pow")
            hid = [pool_mem[s][:, 0:HT * TILE].rearrange("p (m n) -> p m n", m=HT) for s in range(STREAMS)]
            stage = [pool_mem[b][:, HT * TILE:HT * TILE + UNIT] for b in range(STAGES)]
            first_hid = [pool_mem[s][:, HT * TILE:2 * HT * TILE].rearrange("p (m n) -> p m n", m=HT)
                         for s in range(STREAMS)]
            w3t_sb = t[0]
            ones = x1[0][:, 0, 0:P]
            scaled = x1[0][:, 1, 0:P]
            sym = x1[0][0:NODES, 2, 0:NODES]
            powr = x1[0][0:NODES, 3, 0:NODES]
            junk = x1[1][0:NODES, 0, 0:NODES]
            junk_full = x1[1][:, 1, 0:P]
            tr_part = setup[0:NODES, 0:1]
            inv_tr = setup[0:NODES, 1:2]
            lam_part = setup[0:NODES, 2:4]
            rsum, csum, diag, deg, dinv = (setup[:, 8 + j:9 + j] for j in range(5))
            lam_r, lam_c = setup[:, 13:14], setup[:, 14:15]
            lam_v = setup[:, 16:18]
            wa_f = setup[:, 20:20 + 2 * KT]
            spare = ps[1][:, BANKS - 1, :]
            SQ, TR, LAM, WA, GCN = (spare[0:NODES, 0:NODES], spare[:, 64:65], spare[:, 66:68], spare[:, 72:72 + 2 * KT],
                                    spare[:, P:2 * P])
            hid_bank = [[2, 3, 0, 1], [2, 0, 1, 2]]

            block = pctx.enter_context(nc.Block())

            @block.sync
            def _(sp):
                sp.wait_ge(zeroed, 2)
                for b in range(2):
                    d = slice(b * NODES, (b + 1) * NODES)
                    sp.dma_start(a_bd[d, d], adj).then_inc(adj_in, 16)
                    sp.dma_start(at_bd[d, d], adj_t).then_inc(adj_in, 16)
                sp.dma_start(col[:, :], cols).then_inc(vec_in, 16)
                sp.dma_start(w3t_sb[:, 0:KT, :], w3t).then_inc(vec_in, 16)
                sp.dma_start(stage[0], wpack[:, 0:UNIT]).then_inc(w_in[0], 16)
                for s in range(STREAMS):
                    sp.dma_start(xa[s][:, :, :], x_tiles[0, s]).then_inc(x_in[s], 16)
                sp.dma_start(stage[1], wpack[:, UNIT:2 * UNIT]).then_inc(w_in[1], 16)
                sp.dma_start(row[:, :, :], rows.partition_broadcast(P)).then_inc(row_in, 16)

                def store(s, n):
                    sp.wait_ge(hid_out[s], n * HT + 1)
                    sp.dma_start(h_tiles[bass.ds(n - 1, 1), s].rearrange("o p m n -> (o p) m n"), hid[s])\
                        .then_inc(hid_stored[s], 16)

                def load_unit(r, b):
                    sp.wait_ge(unit_lo, r * STAGES + b - (STAGES - 1))
                    sp.dma_start(stage[b], wpack[:, bass.ds(r * (STAGES * UNIT) + b * UNIT, UNIT)]).then_inc(w_in[b], 16)

                def load_x(s, r):
                    sp.wait_ge(agg_ps[s], r)
                    sp.dma_start(xa[s][:, :, :], x_tiles[bass.ds(r, 1), s].rearrange("o p b d -> (o p) b d"))\
                        .then_inc(x_in[s], 16)

                for b in range(STAGES):
                    load_unit(1, b)
                with sp.Fori(1, ROUNDS - 1) as r:
                    for s in range(STREAMS):
                        load_x(s, r)
                    for s in range(STREAMS):
                        load_unit(r + 1, s)
                        store(s, r)
                for s in range(STREAMS):
                    load_x(s, ROUNDS - 1)
                for n in (ROUNDS - 1, ROUNDS):
                    for s in range(STREAMS):
                        store(s, n)
                for s in range(STREAMS):
                    sp.wait_ge(unit_lo, UNITS)
                    sp.wait_ge(hid_stored[s], 17)
                    sp.dma_start(first_hid[s], h_tiles[0, s]).then_inc(h_in[0][s], 16)
                for s in range(STREAMS):
                    sp.wait_ge(hid_stored[s], 16 * ROUNDS + 1)

            @block.gpsimd
            def _(pool):
                nc.gpsimd.memset(a_bd[:, :], 0.0).then_inc(zeroed, 1)
                nc.gpsimd.memset(at_bd[:, :], 0.0).then_inc(zeroed, 1)
                nc.gpsimd.memset(ident[:, :], 0.0).then_inc(ident_ok, 1)
                nc.gpsimd.memset(ones, 1.0).then_inc(ident_ok, 1)
                nc.gpsimd.memset(nhalf[:, :], -0.5).then_inc(ident_ok, 1)
                nc.gpsimd.memset(zero[:, :], 0.0).then_inc(ident_ok, 1)
                pool.wait_ge(ident_ok, 4)
                nc.gpsimd.affine_select(out=ident[:, :], in_=ident[:, :], compare_op=ALU.not_equal, fill=1.0, base=0,
                                        pattern=[[-1, P]], channel_multiplier=1).then_inc(ident_ok, 1)
                pool.wait_ge(step, 5)
                nc.gpsimd.tensor_tensor(dinv, deg, nhalf[:, 0:1], ALU.pow).then_inc(pow_ok, 1)
                pool.wait_ge(bn_step, HT + 1)
                nc.gpsimd.tensor_tensor(small[:, 24:24 + HT], small[:, 16:16 + HT], nhalf[:, 0:HT], ALU.pow)\
                    .then_inc(bn_pow, 1)

            @block.scalar
            def _(act):
                act.wait_ge(vec_in, 32)
                act.wait_ge(ident_ok, 5)
                for s in range(STREAMS):
                    nc.scalar.activation(small[:, 40 + s:41 + s], ident[:, 0:1], ACT.Copy).then_inc(hid_out[s], 1)

                def unit_high(r, b):
                    act.wait_ge(w_in[b], r * 16 + 16)
                    nc.scalar.activation(w_hi[:, bass.ds(r * (STAGES * UNIT) + b * UNIT, UNIT)], stage[b], ACT.Copy,
                                         scale=WSCALE).then_inc(unit_hi, 1)

                def agg_high(s, n):
                    act.wait_ge(agg_ps[s], n)
                    nc.scalar.copy(hl_a[s][:, 0, :, :], by_feature(s, 0)).then_inc(agg_hi[s], 1)

                def hid_bias(s, n):
                    act.wait_ge(hid_stored[s], n * 16 - 15)
                    act.wait_ge(hid_stats[s], n)
                    for m in range(HT):
                        act.wait_ge(hid_ps[s], n * HT - (HT - 1 - m))
                        nc.scalar.activation(hid[s][:, m, :], ps[s][:, hid_bank[s][m], :], ACT.Identity,
                                             bias=vec("b1", m), scale=UNSCALE).then_inc(hid_out[s], 1)

                for b in range(STAGES):
                    unit_high(0, b)
                with act.Fori(0, ROUNDS - 1) as r:
                    for s in range(STREAMS):
                        agg_high(s, r + 1)
                    for s in range(STREAMS):
                        unit_high(r + 1, s)
                        hid_bias(s, r + 1)
                for s in range(STREAMS):
                    agg_high(s, ROUNDS)
                for s in range(STREAMS):
                    hid_bias(s, ROUNDS)

            @block.tensor
            def _(pe):
                pe.wait_ge(step, 6)
                pe.wait_ge(ident_ok, 5)
                nc.tensor.transpose(GCN, scaled, ident[:, :]).then_inc(gcn_ps, 1)
                pe.wait_ge(vec_in, 32)
                pe.wait_ge(unit_lo, 1)
                for half in range(2):
                    for kt in range(KT):
                        for ot in range(KT):
                            mm = nc.tensor.matmul(WA[:, half * KT + kt:half * KT + kt + 1],
                                                  w3t_sb[:, ot, kt * P:(kt + 1) * P],
                                                  vec("a", half * KT + ot), start=(ot == 0), stop=(ot == KT - 1))
                mm.then_inc(wa_ps, 1)

                def square(k):
                    pe.wait_ge(sq_ready, k * 2 + 2)
                    nc.tensor.matmul(TR, ones[0:NODES, :], tr_part, start=True, stop=True)
                    nc.tensor.matmul(SQ, powr, powr, start=True, stop=True).then_inc(sq_ps, 1)

                def aggregate(s, n):
                    pe.wait_ge(x_in[s], n * 16)
                    pe.wait_ge(hid_out[s], n * HT - HT + 1)
                    for f in range(KT):
                        for b in range(BLK):
                            mm = nc.tensor.matmul(ps[s][:, f, b * P:(b + 1) * P], xa[s][:, b, f * P:(f + 1) * P],
                                                  gcn_t[:, :], start=True, stop=True)
                    mm.then_inc(agg_ps[s], 1)

                def hidden(s, n, ms):
                    agg = hl_a[s]
                    for m in ms:
                        if m == 0:
                            pe.wait_ge(agg_lo[s], n)
                        if hid_bank[s][m] in hid_bank[s][:m]:
                            pe.wait_ge(hid_out[s], n * HT - HT + 2)
                        for k in range(KT):
                            mm = product(ps[s][:, hid_bank[s][m], :], weight("l0_w1", k, m * P, P),
                                         (agg[:, 0, k, :], agg[:, 1, k, :]), k == 0, k == KT - 1)
                        mm.then_inc(hid_ps[s], 1)

                pe.wait_ge(step, 7)
                with pe.Fori(0, ROUNDS - 1) as r:
                    for s in range(STREAMS):
                        aggregate(s, r + 1)
                    for s in range(STREAMS):
                        square(r * SQUARES + 2 * s)
                        hidden(s, r + 1, range(HT // 2))
                        square(r * SQUARES + 2 * s + 1)
                        hidden(s, r + 1, range(HT // 2, HT))
                for s in range(STREAMS):
                    aggregate(s, ROUNDS)
                hidden(0, ROUNDS, range(HT))
                pe.wait_ge(sq_ready, 2 * SQUARINGS + 3)
                nc.tensor.matmul(LAM, ones[0:NODES, :], lam_part, start=True, stop=True).then_inc(lam_ps, 1)
                hidden(1, ROUNDS, range(HT))

            @block.vector
            def _(dve):
                for s in range(STREAMS):
                    nc.vector.memset(small[:, 42 + s:43 + s], 0.0).then_inc(hid_stats[s], 1)
                    nc.vector.memset(small[:, 44 + s:45 + s], 0.0).then_inc(hid_stored[s], 1)

                def unit_low(r, b):
                    part = bass.ds(r * (STAGES * UNIT) + b * UNIT, UNIT)
                    dve.wait_ge(unit_hi, r * STAGES + b + 1)
                    nc.vector.scalar_tensor_tensor(w_lo[:, part], stage[b], WSCALE, w_hi[:, part], ALU.mult,
                                                   ALU.subtract).then_inc(unit_lo, 1)

                dve.wait_ge(adj_in, 64)
                dve.wait_ge(ident_ok, 5)
                nc.vector.reduce_sum(rsum, a_bd[:, :], axis=AX.X).then_inc(step, 1)
                nc.vector.reduce_sum(csum, at_bd[:, :], axis=AX.X).then_inc(step, 1)
                nc.vector.tensor_tensor_reduce(junk_full, a_bd[:, :], ident[:, :], 1.0, 0.0, ALU.mult, ALU.add,
                                               diag).then_inc(step, 1)
                dve.wait_ge(step, 3)
                nc.vector.scalar_tensor_tensor(deg, rsum, 1.0, csum, ALU.add, ALU.add).then_inc(step, 1)
                dve.wait_ge(step, 4)
                nc.vector.tensor_tensor(deg, deg, diag, ALU.subtract).then_inc(step, 1)
                dve.wait_ge(pow_ok, 1)
                nc.vector.tensor_tensor(junk_full, a_bd[:, :], ident[:, :], ALU.add).then_inc(sq_ready, 1)
                dve.wait_ge(sq_ready, 1)
                nc.vector.tensor_scalar(scaled, junk_full, dinv, None, ALU.mult).then_inc(step, 1)
                dve.wait_ge(gcn_ps, 1)
                nc.vector.tensor_scalar(gcn_t[:, :], GCN, dinv, None, ALU.mult).then_inc(step, 1)
                for b in range(STAGES):
                    unit_low(0, b)
                nc.vector.tensor_scalar(mask1[:, :], a_bd[:, :], 0.0, MASK_L1, ALU.is_le, ALU.mult).then_inc(step, 1)
                nc.vector.tensor_scalar(mask3[:, :], a_bd[:, :], 0.0, MASK_L3, ALU.is_equal, ALU.mult).then_inc(step, 1)
                dve.wait_ge(step, 9)
                nc.vector.memset(mask1[0:NODES, NODES:P], MASK_OFF).then_inc(step, 1)
                nc.vector.memset(mask1[NODES:P, 0:NODES], MASK_OFF).then_inc(step, 1)
                dve.wait_ge(vec_in, 32)
                nc.vector.tensor_tensor(lstm_b[:, :], vecs("bih"), vecs("bhh"), ALU.add).then_inc(step, 1)
                dve.wait_ge(step, 12)
                for g in (GATE_I, GATE_F, GATE_O):
                    part = lstm_b[:, :].rearrange("p (w g k) -> p w g k", g=4, k=KT)[:, :, g, :]
                    half = nc.vector.tensor_scalar(part, part, 0.5, None, ALU.mult)
                half.then_inc(step, 1)
                dve.wait_ge(wa_ps, 1)
                nc.vector.tensor_scalar(wa_f, WA, WSCALE, None, ALU.mult).then_inc(step, 1)
                dve.wait_ge(step, 14)
                nc.vector.tensor_copy(wa1[:, 0, :], wa_f[:, 0:KT]).then_inc(step, 1)
                nc.vector.tensor_copy(wa2[:, 0, :, :], wa_f[:, KT:2 * KT].unsqueeze(2).broadcast_to([P, KT, P]))\
                    .then_inc(step, 1)
                dve.wait_ge(step, 16)
                nc.vector.tensor_tensor(wa1[:, 1, :], wa_f[:, 0:KT], wa1[:, 0, :], ALU.subtract).then_inc(step, 1)
                nc.vector.tensor_tensor(wa2[:, 1, :, :], wa_f[:, KT:2 * KT].unsqueeze(2).broadcast_to([P, KT, P]),
                                        wa2[:, 0, :, :], ALU.subtract).then_inc(step, 1)
                nc.vector.tensor_tensor(sym, a_bd[0:NODES, 0:NODES], at_bd[0:NODES, 0:NODES], ALU.add).then_inc(step, 1)
                dve.wait_ge(step, 19)
                nc.vector.tensor_scalar(sym, sym, 0.5, None, ALU.mult).then_inc(step, 1)
                dve.wait_ge(step, 20)
                nc.vector.tensor_copy(powr, sym).then_inc(step, 1)
                dve.wait_ge(step, 21)
                nc.vector.tensor_tensor_reduce(junk, powr, powr, 1.0, 0.0, ALU.mult, ALU.add, tr_part)\
                    .then_inc(sq_ready, 1)

                def square(k):
                    dve.wait_ge(sq_ps, k + 1)
                    nc.vector.reciprocal(inv_tr, TR[0:NODES, :]).then_inc(step, 1)
                    dve.wait_ge(step, k + 22)
                    nc.vector.tensor_scalar(powr, SQ, inv_tr, None, ALU.mult).then_inc(sq_ready, 1)
                    dve.wait_ge(sq_ready, k * 2 + 3)
                    nc.vector.tensor_tensor_reduce(junk, powr, powr, 1.0, 0.0, ALU.mult, ALU.add, tr_part)\
                        .then_inc(sq_ready, 1)

                def agg_low(s, n):
                    dve.wait_ge(agg_hi[s], n)
                    nc.vector.tensor_tensor(hl_a[s][:, 1, :, :], by_feature(s, 0), hl_a[s][:, 0, :, :], ALU.subtract)\
                        .then_inc(agg_lo[s], 1)

                def hid_stat(s, r, ms):
                    for m in ms:
                        dve.wait_ge(hid_out[s], r * HT + m + 2)
                        st = nc.vector.bn_stats(bnst1[:, m, bass.ds(r * STREAMS + s, 1), :]
                                                .rearrange("p o c -> p (o c)"), hid[s][:, m, :])
                    if HT - 1 in ms:
                        st.then_inc(hid_stats[s], 1)

                with dve.Fori(0, ROUNDS - 1) as r:
                    for s in range(STREAMS):
                        agg_low(s, r + 1)
                    for s in range(STREAMS):
                        square(r * SQUARES + 2 * s)
                        unit_low(r + 1, s)
                        hid_stat(s, r, range(HT // 2))
                        square(r * SQUARES + 2 * s + 1)
                        hid_stat(s, r, range(HT // 2, HT))
                for s in range(STREAMS):
                    agg_low(s, ROUNDS)
                dve.wait_ge(row_in, 16)
                twice = row[:, ROWS.index("bg1"), :]
                nc.vector.tensor_scalar(twice, twice, 2.0, None, ALU.mult).then_inc(step, 1)
                dve.wait_ge(sq_ready, 2 * SQUARINGS + 2)
                nc.vector.tensor_tensor_reduce(junk, sym, powr, 1.0, 0.0, ALU.mult, ALU.add, lam_part[:, 0:1])\
                    .then_inc(pow_ok, 1)
                dve.wait_ge(pow_ok, 2)
                nc.vector.tensor_tensor_reduce(junk, ident[0:NODES, 0:NODES], powr, 1.0, 0.0, ALU.mult, ALU.add,
                                               lam_part[:, 1:2]).then_inc(sq_ready, 1)
                hid_stat(0, ROUNDS - 1, range(HT))
                dve.wait_ge(lam_ps, 1)
                nc.vector.tensor_copy(lam_v, LAM).then_inc(pow_ok, 1)
                dve.wait_ge(pow_ok, 3)
                nc.vector.reciprocal(lam_r, lam_v[:, 1:2]).then_inc(pow_ok, 1)
                dve.wait_ge(pow_ok, 4)
                nc.vector.tensor_scalar(lam_c, lam_v[:, 0:1], lam_r, 1e-8, ALU.mult, ALU.add).then_inc(pow_ok, 1)
                dve.wait_ge(pow_ok, 5)
                nc.vector.reciprocal(lam_r, lam_c).then_inc(pow_ok, 1)
                dve.wait_ge(pow_ok, 6)
                nc.vector.tensor_scalar(lam_c, lam_r, 2.0, None, ALU.mult).then_inc(pow_ok, 1)
                dve.wait_ge(pow_ok, 7)
                nc.vector.scalar_tensor_tensor(cheb_t[:, :], at_bd[:, :], lam_c, ident[:, :], ALU.mult, ALU.subtract)\
                    .then_inc(pow_ok, 1)
                hid_stat(1, ROUNDS - 1, range(HT))
                for s in range(STREAMS):
                    dve.wait_ge(hid_stats[s], ROUNDS + 1)
                for m in range(HT):
                    nc.vector.bn_aggr(small[:, 2 * m:2 * m + 2], bnst1[:, m, :, :].rearrange("p t c -> p (t c)"))\
                        .then_inc(bn_step, 1)
                m_v = small[:, 0:2 * HT].rearrange("p (m c) -> p m c", c=2)
                dve.wait_ge(bn_step, HT)
                nc.vector.tensor_scalar(small[:, 16:16 + HT], m_v[:, :, 1], EPS, None, ALU.add).then_inc(bn_step, 1)
                dve.wait_ge(bn_pow, 1)
                nc.vector.tensor_tensor(bn1[:, 0, :], vecs("g1"), small[:, 24:24 + HT], ALU.mult).then_inc(bn_step, 1)
                dve.wait_ge(bn_step, HT + 2)
                nc.vector.tensor_tensor(small[:, 32:32 + HT], m_v[:, :, 0], bn1[:, 0, :], ALU.mult).then_inc(bn_step, 1)
                dve.wait_ge(bn_step, HT + 3)
                nc.vector.tensor_tensor(bn1[:, 1, :], vecs("be1"), small[:, 32:32 + HT], ALU.subtract).then_inc(bn_step, 1)

        with ExitStack() as pctx:
            def psems(name):
                return [pctx.enter_context(nc.semaphore(f"{name}_{s}")) for s in range(STREAMS)]

            rel, rel_hi, rel_lo, o_ps, o_out, o_stats, o_stored = (
                psems(n) for n in ("rel", "rel_hi", "rel_lo", "o_ps", "o_out", "o_stats", "o_stored"))
            hid = [first_hid, [pool_mem[s][:, 0:HT * TILE].rearrange("p (m n) -> p m n", m=HT) for s in range(STREAMS)]]
            hl = [[hl_a[s], hl_b[s]] for s in range(STREAMS)]
            bn_step = pctx.enter_context(nc.semaphore("bn2_step"))
            bn_pow = pctx.enter_context(nc.semaphore("bn2_pow"))
            block = pctx.enter_context(nc.Block())

            @block.sync
            def _(sp):
                for done in used:
                    sp.sem_clear(done)

                def store(s, n):
                    sp.wait_ge(o_out[s], n * KT + 1)
                    sp.dma_start(o_tiles[bass.ds(n - 1, 1), s].rearrange("o p m n -> (o p) m n"), act_in[s][:, :, :])\
                        .then_inc(o_stored[s], 16)

                for s in range(STREAMS):
                    sp.dma_start(hid[1][s], h_tiles[1, s]).then_inc(h_in[1][s], 16)
                for s in range(STREAMS):
                    sp.dma_start(xa[s][:, :, :], x_tiles[0, s]).then_inc(x3_in[s], 16)
                with sp.Fori(1, ROUNDS // 2) as r:
                    for i in range(2):
                        for s in range(STREAMS):
                            sp.wait_ge(rel_lo[s], (r * 2 + i - 1) * HT)
                            sp.dma_start(hid[i][s], h_tiles[bass.ds(r * 2 + i, 1), s].rearrange("o p m n -> (o p) m n"))\
                                .then_inc(h_in[i][s], 16)
                        for s in range(STREAMS):
                            store(s, r * 2 + i - 1)
                for i in range(2):
                    for s in range(STREAMS):
                        store(s, ROUNDS - 1 + i)
                for s in range(STREAMS):
                    sp.wait_ge(o_stored[s], 16 * ROUNDS + 1)

            @block.scalar
            def _(act):
                def relu(s, r, i):
                    act.wait_ge(h_in[i][s], r * 16 + 16)
                    for m in range(HT):
                        nc.scalar.activation(hid[i][s][:, m, :], hid[i][s][:, m, :], ACT.Relu, bias=bn1[:, 1, m:m + 1],
                                             scale=bn1[:, 0, m:m + 1]).then_inc(rel[s], 1)

                def out_bias(s, n):
                    act.wait_ge(o_ps[s], n + 1)
                    act.wait_ge(o_stored[s], n * 16 - 15)
                    act.wait_ge(o_stats[s], n)
                    for m in range(KT):
                        nc.scalar.activation(act_in[s][:, m, :], ps[s][:, m, :], ACT.Identity, bias=vec("b2", m),
                                             scale=UNSCALE).then_inc(o_out[s], 1)

                for s in range(STREAMS):
                    nc.scalar.activation(small[:, 40 + s:41 + s], ident[:, 0:1], ACT.Copy).then_inc(o_out[s], 1)
                for s in range(STREAMS):
                    relu(s, 0, 0)
                with act.Fori(0, ROUNDS // 2 - 1) as r:
                    for s in range(STREAMS):
                        relu(s, r, 1)
                        out_bias(s, r * 2 + 1)
                    for s in range(STREAMS):
                        relu(s, r + 1, 0)
                        out_bias(s, r * 2 + 2)
                for s in range(STREAMS):
                    relu(s, ROUNDS // 2 - 1, 1)
                    out_bias(s, ROUNDS - 1)
                for s in range(STREAMS):
                    out_bias(s, ROUNDS)

            @block.gpsimd
            def _(pool):
                def high(s, n, i):
                    pool.wait_ge(o_ps[s], n)
                    for m in range(HT):
                        pool.wait_ge(rel[s], n * HT - (HT - 1 - m))
                        nc.gpsimd.tensor_tensor(hl[s][m // KT][:, 0, m % KT, :], hid[i][s][:, m, :],
                                                zero[:, 0:1].broadcast_to([P, TILE]), ALU.add).then_inc(rel_hi[s], 1)

                with pool.Fori(0, ROUNDS // 2) as r:
                    for i in range(2):
                        for s in range(STREAMS):
                            high(s, r * 2 + i + 1, i)
                pool.wait_ge(bn_step, KT + 1)
                nc.gpsimd.tensor_tensor(small[:, 24:24 + KT], small[:, 16:16 + KT], nhalf[:, 0:KT], ALU.pow)\
                    .then_inc(bn_pow, 1)

            @block.vector
            def _(dve):
                for s in range(STREAMS):
                    nc.vector.memset(small[:, 42 + s:43 + s], 0.0).then_inc(o_stats[s], 1)
                    nc.vector.memset(small[:, 44 + s:45 + s], 0.0).then_inc(o_stored[s], 1)
                    nc.vector.memset(small[:, 46 + s:47 + s], 0.0).then_inc(o_ps[s], 1)

                def low(s, n, i):
                    for m in range(HT):
                        dve.wait_ge(rel_hi[s], n * HT - (HT - 1 - m))
                        nc.vector.tensor_tensor(hl[s][m // KT][:, 1, m % KT, :], hid[i][s][:, m, :],
                                                hl[s][m // KT][:, 0, m % KT, :], ALU.subtract).then_inc(rel_lo[s], 1)

                def out_stat(s, r):
                    for m in range(KT):
                        dve.wait_ge(o_out[s], r * KT + m + 2)
                        st = nc.vector.bn_stats(bnst2[:, m, bass.ds(r * STREAMS + s, 1), :]
                                                .rearrange("p o c -> p (o c)"), act_in[s][:, m, :])
                    st.then_inc(o_stats[s], 1)

                for s in range(STREAMS):
                    low(s, 1, 0)
                with dve.Fori(0, ROUNDS // 2 - 1) as r:
                    for s in range(STREAMS):
                        low(s, r * 2 + 2, 1)
                        out_stat(s, r * 2)
                    for s in range(STREAMS):
                        low(s, r * 2 + 3, 0)
                        out_stat(s, r * 2 + 1)
                for s in range(STREAMS):
                    low(s, ROUNDS, 1)
                    out_stat(s, ROUNDS - 2)
                for s in range(STREAMS):
                    out_stat(s, ROUNDS - 1)
                for s in range(STREAMS):
                    dve.wait_ge(o_stats[s], ROUNDS + 1)
                for m in range(KT):
                    nc.vector.bn_aggr(small[:, 2 * m:2 * m + 2], bnst2[:, m, :, :].rearrange("p t c -> p (t c)"))\
                        .then_inc(bn_step, 1)
                m_v = small[:, 0:2 * KT].rearrange("p (m c) -> p m c", c=2)
                dve.wait_ge(bn_step, KT)
                nc.vector.tensor_scalar(small[:, 16:16 + KT], m_v[:, :, 1], EPS, None, ALU.add).then_inc(bn_step, 1)
                dve.wait_ge(bn_pow, 1)
                nc.vector.tensor_tensor(bn2[:, 0, :], vecs("g2"), small[:, 24:24 + KT], ALU.mult).then_inc(bn_step, 1)
                dve.wait_ge(bn_step, KT + 2)
                nc.vector.tensor_tensor(small[:, 32:32 + KT], m_v[:, :, 0], bn2[:, 0, :], ALU.mult).then_inc(bn_step, 1)
                dve.wait_ge(bn_step, KT + 3)
                nc.vector.tensor_tensor(bn2[:, 1, :], vecs("be2"), small[:, 32:32 + KT], ALU.subtract).then_inc(bn_step, 1)

            @block.tensor
            def _(pe):
                def second(s, n):
                    pe.wait_ge(o_out[s], n * KT - KT + 1)
                    for k in range(HT):
                        pe.wait_ge(rel_lo[s], n * HT - (HT - 1 - k))
                        half = hl[s][k // KT]
                        for m in range(KT):
                            mm = product(ps[s][:, m, :], weight("l0_w2", k, m * P, P),
                                         (half[:, 0, k % KT, :], half[:, 1, k % KT, :]), k == 0, k == HT - 1)
                    mm.then_inc(o_ps[s], 1)

                with pe.Fori(0, ROUNDS) as r:
                    for s in range(STREAMS):
                        second(s, r + 1)

        with ExitStack() as pctx:
            def psems(name):
                return [pctx.enter_context(nc.semaphore(f"{name}_{s}")) for s in range(STREAMS)]

            x_in = x3_in
            o_in, out_stored, banks_free = (psems(n) for n in ("o_in", "out_stored", "banks_free"))
            y_ok, y_ps = psems("y_ok"), psems("y_ps")
            t_ok, ln_stats, ln_mv, ln_ve, ln_rstd, ln_nmr, ln_out, centred = (
                psems(n) for n in ("t_ok", "ln_stats", "ln_mv", "ln_ve", "ln_rstd", "ln_nmr", "ln_out", "centred"))
            feat_ps, feat_hi, feat_lo = psems("feat_ps"), psems("feat_hi"), psems("feat_lo")
            hc_ps, wo_ps, w2_ps, wg_ps, wg_ok = (psems(n) for n in ("hc_ps", "wo_ps", "w2_ps", "wg_ps", "wg_ok"))
            affine_ok, pre_ok, x1_ok, x2_ok, o_ok = (psems(n) for n in ("affine_ok", "pre_ok", "x1_ok", "x2_ok", "o_ok"))
            q_ps, k_ps, v_ps, q_ok, k_ok, v_ok = (psems(n) for n in ("q_ps", "k_ps", "v_ps", "q_ok", "k_ok", "v_ok"))
            score_ps, masked_ok, exp_ok, inv_ok, prob_ok, prob_ps, prob_t = (
                psems(n) for n in ("score_ps", "masked_ok", "exp_ok", "inv_ok", "prob_ok", "prob_ps", "prob_t"))
            w1_ps, gelu_ok, gelu_hi, gelu_lo = (psems(n) for n in ("w1_ps", "gelu_ok", "gelu_hi", "gelu_lo"))
            gate_ps, gate_ok, ig_ok, fc_ok, c_ok, tanh_ok, h_ok, h_hi, h_lo = (
                psems(n) for n in ("gate_ps", "gate_ok", "ig_ok", "fc_ok", "c_ok", "tanh_ok", "h_ok", "h_hi", "h_lo"))
            hf_ps, wh_ps, wh_ok, s_ps, s1_ok, e_ok, lrelu_ok, emask_ok, eexp_ok, einv_ok, att_ps, att_t, av_ps = (
                psems(n) for n in ("hf_ps", "wh_ps", "wh_ok", "s_ps", "s1_ok", "e_ok", "lrelu_ok", "emask_ok",
                                   "eexp_ok", "einv_ok", "att_ps", "att_t", "av_ps"))

            XP, X1T, OT, X2T, XBT, H0, H1, XCT = range(8)
            FEATS = 8 * KT
            feat_dst = [hl_a, hl_b, hl_a, hl_b, hl_a, hl_b, hl_a, hl_b]
            feat_bank = [2, 2, 0, 0, 0, 0, 0, 2]
            feat_relu = [H0, H1]
            FEAT_OF = {"cheb": XP, "turn_x1": X1T, "attend": OT, "turn_x2": X2T, "turn_xb": XBT, "mix0": H0, "mix1": H1,
                       "turn_xc": XCT}
            NORM_OF = {"norm_l0": LN_L0, "norm_g1": LN_G1, "norm_g2": LN_G2, "norm_g3": LN_G3, "norm_l1": LN_L1,
                       "norm_l2": LN_L2, "norm_l3": LN_L3}
            SCORE_BANK = [2, 3, 0, 1]
            HID_BANK = [2, 3, 0, 1]

            def at(n, each, j):
                return n * each - (each - 1 - j)

            GATE_LIST = [[GATE_I, GATE_G, GATE_O] if CELLS[c][1] == 0 else [GATE_I, GATE_G, GATE_F, GATE_O]
                         for c in range(NCELL)]
            GATE_AT = [sum(len(g) for g in GATE_LIST[:c]) for c in range(NCELL)]
            NGATE = sum(len(g) for g in GATE_LIST)
            STEPPED = [c for c in range(NCELL) if CELLS[c][1] > 0]

            def score(s, b, h):
                c = (b % 2 * 2 + h // 2) * P
                return ps[s][:, SCORE_BANK[b // 2 * 2] + h % 2, c:c + P]

            PLAIN = [LN_L0, LN_L1, LN_L2, LN_L3]
            GAINED = [LN_G1, LN_G2, LN_G3]

            HALVES = 2
            HALF = BLK // HALVES
            FIRST_OF_HALF = range(0, BLK, HALF)

            def t_at(n, j, half):
                return at(n, HALVES * NORMS, HALVES * j + half)

            def out_at(n, j, half=HALVES - 1):
                return at(n, HALVES * len(PLAIN), HALVES * PLAIN.index(j) + half)

            def feat_at(n, j, m=KT - 1):
                return at(n, FEATS, j * KT + m)

            def gate_at(n, c, j):
                return at(n, NGATE, GATE_AT[c] + j)

            mem = pool_mem
            q = [m[:, 0:1024].rearrange("p (k n) -> p k n", k=KT) for m in mem]
            kk = [m[:, 1024:2048].rearrange("p (k n) -> p k n", k=KT) for m in mem]
            prob_tr = [m[:, 0:2048].rearrange("p (b h n) -> p b h n", b=BLK, h=HEADS) for m in mem]
            vv = [m[:, 2048:3072].rearrange("p (b d) -> p b d", b=BLK) for m in mem]
            prob = [m[:, 3072:5120].rearrange("p (b h n) -> p b h n", b=BLK, h=HEADS) for m in mem]
            gelu = [m[:, 0:2048].rearrange("p (m n) -> p m n", m=HT) for m in mem]
            gelu_hl = [m[:, 2048:4096].bitcast(F16).rearrange("p (c m n) -> p c m n", c=2, m=HT) for m in mem]
            wg = [m[:, 0:1024].rearrange("p (b d) -> p b d", b=BLK) for m in mem]
            gates = [m[:, 0:2048].rearrange("p (g n) -> p g n", g=4) for m in mem]
            cell_c = [m[:, 2048:2560] for m in mem]
            cell_t = [m[:, 2560:3072] for m in mem]
            cell_h = [m[:, 3072:3584] for m in mem]
            cell_hl = [m[:, 3584:4096].bitcast(F16).rearrange("p (c n) -> p c n", c=2) for m in mem]
            state = [m[:, 4096:5120].rearrange("p (k n) -> p k n", k=KT) for m in mem]
            state_hl = feat_dst[H1]
            wh = [m[:, 0:1024].rearrange("p (b d) -> p b d", b=BLK) for m in mem]
            logit = [m[:, 1024:1536].rearrange("p (b n) -> p b n", b=BLK) for m in mem]
            att = [m[:, 1536:2048].rearrange("p (b n) -> p b n", b=BLK) for m in mem]
            att_tr = [m[:, 2048:2560].rearrange("p (b n) -> p b n", b=BLK) for m in mem]
            s1 = [small[:, 8 + BLK * s:8 + BLK * s + BLK] for s in range(STREAMS)]
            xc = x1

            block = pctx.enter_context(nc.Block())

            @block.sync
            def _(sp):
                def load_o(s, r):
                    sp.dma_start(act_in[s][:, :, :], o_tiles[bass.ds(r, 1), s].rearrange("o p m n -> (o p) m n"))\
                        .then_inc(o_in[s], 16)

                def load_x(s, r):
                    sp.dma_start(xa[s][:, :, :], x_tiles[bass.ds(r, 1), s].rearrange("o p b d -> (o p) b d"))\
                        .then_inc(x_in[s], 16)

                def store(s, n):
                    sp.wait_ge(ln_out[s], out_at(n, LN_L3))
                    sp.dma_start(out_tiles[bass.ds(n - 1, 1), s].rearrange("o p b d -> (o p) b d"), xb[s][:, :, :])\
                        .then_inc(out_stored[s], 16)

                def load_next(s, n):
                    sp.wait_ge(y_ps[s], n * HALVES)
                    load_o(s, n)
                    sp.wait_ge(pre_ok[s], n * 3)
                    load_x(s, n)

                for s in range(STREAMS):
                    load_o(s, 0)
                with sp.Fori(1, ROUNDS) as n:
                    for s in range(STREAMS):
                        load_next(s, n)
                        store(s, n)
                for s in range(STREAMS):
                    store(s, ROUNDS)
                for s in range(STREAMS):
                    sp.wait_ge(out_stored[s], 16 * ROUNDS + 1)

            @block.tensor
            def _(pe):
                def turn_y(s, n):
                    pe.wait_ge(banks_free[s], n)
                    pe.wait_ge(y_ok[s], n * KT)
                    turn_back(s, act_in[s], y_ps)

                def turn_back(s, src, done):
                    for b in range(BLK):
                        for f in range(KT):
                            mm = nc.tensor.transpose(by_token(s, 0)[:, b, f * P:(f + 1) * P],
                                                     src[:, f, b * P:(b + 1) * P], ident[:, :])
                        if b % HALF == HALF - 1:
                            mm.then_inc(done[s], 1)

                def chebyshev(s, n):
                    for f in range(KT):
                        for b in range(BLK):
                            if f == 0 and b in FIRST_OF_HALF:
                                pe.wait_ge(ln_out[s], out_at(n, LN_L0, b // HALF))
                            mm = nc.tensor.matmul(by_feature(s, feat_bank[XP])[:, f, b * P:(b + 1) * P],
                                                  xa[s][:, b, f * P:(f + 1) * P], cheb_t[:, :], start=True, stop=True)
                        mm.then_inc(feat_ps[s], 1)

                def wait_rows(s, n, j, k):
                    pe.wait_ge(feat_lo[s], feat_at(n, j, k))

                def dense(s, src, name, bank, done, halves, wait_k=None):
                    kts = src.shape[2]
                    for b in range(BLK):
                        for k in range(kts):
                            if b == 0 and wait_k:
                                wait_k(k)
                            mm = product(by_token(s, bank)[:, b, :],
                                         (src[:, 0, k, b * P:(b + 1) * P], src[:, 1, k, b * P:(b + 1) * P]),
                                         weight(name, k, 0, DIM), k == 0, k == kts - 1)
                        if (b + 1) % (BLK // halves) == 0:
                            mm.then_inc(done[s], 1)

                def conv(s, n):
                    dense(s, hl_a[s][:, :, :, :], "wc", 0, hc_ps, HALVES, lambda k: wait_rows(s, n, XP, k))

                def turn(s, src, j, ready, value):
                    for f in range(KT):
                        for b in range(BLK):
                            if f == 0 and b in FIRST_OF_HALF:
                                pe.wait_ge(ready[s], value(b // HALF))
                            mm = nc.tensor.transpose(by_feature(s, feat_bank[j])[:, f, b * P:(b + 1) * P],
                                                     src[s][:, b, f * P:(f + 1) * P], ident[:, :])
                        mm.then_inc(feat_ps[s], 1)

                def turn_x1(s, n):
                    turn(s, x1, X1T, x1_ok, lambda half: at(n, HALVES, half))

                def query(s, n):
                    rows_of(s, "wq", 0, lambda k: wait_rows(s, n, X1T, k)).then_inc(q_ps[s], 1)

                def key(s, n):
                    rows_of(s, "wk", 2).then_inc(k_ps[s], 1)

                def value(s, n):
                    pe.wait_ge(q_ok[s], n)
                    dense(s, hl_b[s][:, :, :, :], "wv", 0, v_ps, 1)

                def rows_of(s, name, bank, wait_k=None):
                    src = hl_b[s]
                    for m in range(KT):
                        for k in range(KT):
                            if m == 0 and wait_k:
                                wait_k(k)
                            mm = product(ps[s][:, bank + m, :], weight(name, k, m * P, P),
                                         (src[:, 0, k, :], src[:, 1, k, :]), k == 0, k == KT - 1)
                    return mm

                def scores(s, n):
                    pe.wait_ge(k_ok[s], n)
                    for b in range(BLK):
                        if b == 2:
                            pe.wait_ge(v_ok[s], n)
                        for h in range(HEADS):
                            d = slice(h % 2 * HEAD_DIM, h % 2 * HEAD_DIM + HEAD_DIM)
                            mm = nc.tensor.matmul(score(s, b, h), q[s][d, h // 2, b * P:(b + 1) * P],
                                                  kk[s][d, h // 2, b * P:(b + 1) * P], start=True, stop=True)
                            if b % 2 == 1 and h >= HEADS - 2:
                                mm.then_inc(score_ps[s], 1)

                def turn_probs(s, n):
                    for b in range(BLK):
                        if b % 2 == 0:
                            pe.wait_ge(masked_ok[s], at(n, BLK, b + 1))
                        pe.wait_ge(prob_ok[s], at(n, BLK, b))
                        for h in range(HEADS):
                            mm = nc.tensor.transpose(ps[s][:, SCORE_BANK[b], h * P:(h + 1) * P], prob[s][:, b, h, :],
                                                     ident[:, :])
                        mm.then_inc(prob_ps[s], 1)

                def attend(s, n):
                    pe.wait_ge(prob_t[s], n * BLK)
                    for pair in range(KT):
                        for b in range(BLK):
                            for h in (2 * pair, 2 * pair + 1):
                                d = slice(h % 2 * HEAD_DIM, h % 2 * HEAD_DIM + HEAD_DIM)
                                mm = nc.tensor.matmul(ps[s][d, feat_bank[OT] + pair, b * P:(b + 1) * P],
                                                      vv[s][:, b, h * HEAD_DIM:(h + 1) * HEAD_DIM], prob_tr[s][:, b, h, :],
                                                      start=True, stop=True)
                        mm.then_inc(feat_ps[s], 1)

                def attn_out(s, n):
                    dense(s, hl_a[s][:, :, :, :], "wo", 2, wo_ps, HALVES, lambda k: wait_rows(s, n, OT, k))

                def turn_x2(s, n):
                    turn(s, x1, X2T, x2_ok, lambda half: at(n, HALVES, half))

                def mlp_up(s, n):
                    src = hl_b[s]
                    for m in range(HT):
                        for k in range(KT):
                            if m == 0:
                                wait_rows(s, n, X2T, k)
                            mm = product(ps[s][:, HID_BANK[m], :], weight("w1", k, m * P, P),
                                         (src[:, 0, k, :], src[:, 1, k, :]), k == 0, k == KT - 1)
                        mm.then_inc(w1_ps[s], 1)

                def mlp_down(s, n):
                    dense(s, gelu_hl[s], "w2", 2, w2_ps, HALVES, lambda k: pe.wait_ge(gelu_lo[s], at(n, HT, k)))

                def turn_xb(s, n):
                    turn(s, xb, XBT, ln_out, lambda half: out_at(n, LN_L1, half))

                def gcn_dense(s, n, j):
                    dense(s, (hl_a, hl_b)[j][s][:, :, :, :], ("wg0", "wg1")[j], 2, wg_ps, HALVES,
                          lambda k: wait_rows(s, n, (XBT, H0)[j], k))

                def gcn_mix(s, n, j):
                    for f in range(KT):
                        for b in range(BLK):
                            if f == 0 and b in FIRST_OF_HALF:
                                pe.wait_ge(wg_ok[s], at(n, 2 * HALVES, j * HALVES + b // HALF))
                            mm = nc.tensor.matmul(by_feature(s, 0)[:, f, b * P:(b + 1) * P],
                                                  wg[s][:, b, f * P:(f + 1) * P], at_bd[:, :], start=True, stop=True)
                        mm.then_inc(feat_ps[s], 1)

                def cell_input(s, n, c):
                    p, step, _ = CELLS[c]
                    w = cell_width(c)
                    if step == 0 and p > 1:
                        pe.wait_ge(h_lo[s], at(n, NCELL, c - 1))
                    tok = [cell_tokens(state_hl[s][:, half, :, :], c) for half in range(2)]
                    for g in GATE_LIST[c]:
                        if c > 0 and g in GATE_LIST[c - 1]:
                            pe.wait_ge(gate_ok[s], gate_at(n, c - 1, GATE_LIST[c - 1].index(g)))
                        for m in range(KT):
                            o = ps[s][:, g, m * w:(m + 1) * w]
                            o = o if p == 1 else o.rearrange("q (b w) -> q b w", b=TILE_BATCHES)
                            for k in range(KT):
                                if c == 0 and g == GATE_LIST[c][0] and m == 0:
                                    wait_rows(s, n, H1, k)
                                mm = product(o, weight(f"wih{p}", k, (g * KT + m) * P, P), (tok[0][:, k], tok[1][:, k]),
                                             m == 0 and k == 0, step == 0 and m == KT - 1 and k == KT - 1)
                        if step == 0:
                            mm.then_inc(gate_ps[s], 1)

                def cell_state(s, n, c):
                    p, step, _ = CELLS[c]
                    w = cell_width(c)
                    if step == 0:
                        return
                    pe.wait_ge(h_lo[s], at(n, NCELL, c - 1))
                    for g in GATE_LIST[c]:
                        for m in range(KT):
                            for k in range(KT):
                                mm = product(ps[s][:, g, m * w:(m + 1) * w], weight(f"whh{p}", k, (g * KT + m) * P, P),
                                             (cell_hl[s][:, 0, k * w:(k + 1) * w], cell_hl[s][:, 1, k * w:(k + 1) * w]),
                                             False, m == KT - 1 and k == KT - 1)
                        mm.then_inc(gate_ps[s], 1)

                def turn_state(s, n):
                    pe.wait_ge(h_ok[s], n * NCELL)
                    pe.wait_ge(gate_ok[s], n * NGATE)
                    turn_back(s, state[s], hf_ps)

                def turn_xc(s, n):
                    turn(s, xc, XCT, ln_out, lambda half: out_at(n, LN_L2, half))

                def gat_dense(s, n):
                    src = hl_b[s]
                    for k in range(KT):
                        wait_rows(s, n, XCT, k)
                        product(ps[s][:, 2, :], (wa2[:, 0, k, :], wa2[:, 1, k, :]), (src[:, 0, k, :], src[:, 1, k, :]),
                                k == 0, k == KT - 1)
                    for b in range(BLK):
                        for k in range(KT):
                            mm = product(ps[s][:, 3, b:b + 1],
                                         (src[:, 0, k, b * P:(b + 1) * P], src[:, 1, k, b * P:(b + 1) * P]),
                                         (wa1[:, 0, k:k + 1], wa1[:, 1, k:k + 1]), k == 0, k == KT - 1)
                    mm.then_inc(s_ps[s], 1)
                    dense(s, src[:, :, :, :], "w3", 0, wh_ps, 1)

                def turn_att(s, n):
                    pe.wait_ge(eexp_ok[s], n)
                    for b in range(BLK):
                        mm = nc.tensor.transpose(ps[s][:, 2, b * P:(b + 1) * P], att[s][:, b, :], ident[:, :])
                    mm.then_inc(att_ps[s], 1)

                def gat_mix(s, n):
                    pe.wait_ge(wh_ok[s], n)
                    pe.wait_ge(att_t[s], n)
                    for b in range(BLK):
                        mm = nc.tensor.matmul(by_token(s, 0)[:, b, :], att_tr[s][:, b, :], wh[s][:, b, :],
                                              start=True, stop=True)
                        if b % HALF == HALF - 1:
                            mm.then_inc(av_ps[s], 1)

                steps = {"turn_y": turn_y, "cheb": chebyshev, "conv": conv, "turn_x1": turn_x1, "q": query, "k": key,
                         "v": value, "scores": scores, "turn_probs": turn_probs, "attend": attend, "attn_out": attn_out,
                         "turn_x2": turn_x2, "mlp_up": mlp_up, "mlp_down": mlp_down, "turn_xb": turn_xb,
                         "turn_state": turn_state, "turn_xc": turn_xc, "gat": gat_dense, "turn_att": turn_att,
                         "gat_mix": gat_mix}

                def run(name, s, n):
                    if name.startswith("cell"):
                        cell_state(s, n, int(name[4:]))
                    elif name.startswith("inp"):
                        cell_input(s, n, int(name[3:]))
                    elif name[:3] in ("gcn", "mix"):
                        (gcn_dense if name[:3] == "gcn" else gcn_mix)(s, n, int(name[3:]))
                    elif name in steps:
                        steps[name](s, n)

                for name, s, n in opening():
                    run(name, s, n)
                with pe.Fori(1, ROUNDS) as r:
                    for part in parts(r):
                        with pe.Fori(0, 1):
                            for name, s, n in part:
                                run(name, s, n)
                for name, s, n in closing():
                    run(name, s, n)

            @block.scalar
            def _(act):
                def norm_y(s, n):
                    act.wait_ge(o_in[s], n * 16)
                    for m in range(KT):
                        nc.scalar.activation(act_in[s][:, m, :], act_in[s][:, m, :], ACT.Identity,
                                             bias=bn2[:, 1, m:m + 1], scale=bn2[:, 0, m:m + 1]).then_inc(y_ok[s], 1)

                def ln_apply(s, n):
                    act.wait_ge(ln_nmr[s], n)
                    for b in range(BLK):
                        op = nc.scalar.activation(xb[s][:, b, :], t[s][:, b, :], ACT.Identity, bias=nmr[s][:, b:b + 1],
                                                  scale=rstd[s][:, b:b + 1])
                        if b % HALF == HALF - 1:
                            op.then_inc(ln_out[s], 1)

                def high(s, n, j):
                    for m in range(KT):
                        act.wait_ge(feat_ps[s], feat_at(n, j, m))
                        nc.scalar.activation(feat_dst[j][s][:, 0, m, :], by_feature(s, feat_bank[j])[:, m, :],
                                             ACT.Relu if j in feat_relu else ACT.Copy).then_inc(feat_hi[s], 1)

                def take_q(s, n):
                    act.wait_ge(q_ps[s], n)
                    nc.scalar.activation(q[s], by_feature(s, 0), ACT.Copy, scale=-UNSCALE * HEAD_DIM ** -0.5)\
                        .then_inc(q_ok[s], 1)

                def take_k(s, n):
                    act.wait_ge(k_ps[s], n)
                    nc.scalar.activation(kk[s], by_feature(s, 2), ACT.Copy, scale=UNSCALE).then_inc(k_ok[s], 1)

                def exps(s, n):
                    for b in range(BLK):
                        act.wait_ge(masked_ok[s], at(n, BLK, b))
                        for h in range(HEADS):
                            i = b * HEADS + h
                            op = nc.scalar.activation(prob[s][:, b, h, :], prob[s][:, b, h, :], ACT.Exp,
                                                      bias=smin[s][:, i:i + 1], scale=-1.0, accum_out=ssum[s][:, i:i + 1])
                        op.then_inc(exp_ok[s], 1)

                def take_probs(s, n):
                    for b in range(BLK):
                        act.wait_ge(prob_ps[s], at(n, BLK, b))
                        nc.scalar.copy(prob_tr[s][:, b, :, :], ps[s][:, SCORE_BANK[b], :]
                                       .rearrange("p (h n) -> p h n", h=HEADS)).then_inc(prob_t[s], 1)

                def gelus(s, n):
                    for m in range(HT):
                        act.wait_ge(w1_ps[s], at(n, HT, m))
                        for dst, done in ((gelu[s][:, m, :], gelu_ok), (gelu_hl[s][:, 0, m, :], gelu_hi)):
                            nc.scalar.activation(dst, ps[s][:, HID_BANK[m], :], ACT.Gelu, bias=vec("l1_b1", m),
                                                 scale=UNSCALE).then_inc(done[s], 1)

                def gates_of(s, n, c):
                    p = CELLS[c][0]
                    w = cell_width(c)
                    if c == 1:
                        act.wait_ge(h_ok[s], at(n, NCELL, 0))
                        act.wait_ge(h_hi[s], at(n, NCELL, 0))
                    for j, g in enumerate(GATE_LIST[c]):
                        act.wait_ge(gate_ps[s], gate_at(n, c, j))
                        for m in range(KT):
                            bias = ((p - 1) * 4 + g) * KT + m
                            op = nc.scalar.activation(gates[s][:, g, m * w:(m + 1) * w], ps[s][:, g, m * w:(m + 1) * w],
                                                      ACT.Tanh, bias=lstm_b[:, bias:bias + 1],
                                                      scale=UNSCALE * (0.5 if g == GATE_G else 0.25))
                        op.then_inc(gate_ok[s], 1)

                def tanh_c(s, n, c):
                    w = cell_width(c)
                    act.wait_ge(c_ok[s], at(n, NCELL, c))
                    nc.scalar.activation(cell_t[s][:, 0:KT * w], cell_c[s][:, 0:KT * w], ACT.Tanh, scale=0.5)\
                        .then_inc(tanh_ok[s], 1)

                def gat_logits(s, n):
                    act.wait_ge(s1_ok[s], n)
                    for b in range(BLK):
                        op = nc.scalar.activation(logit[s][:, b, :], ps[s][:, 2, b * P:(b + 1) * P], ACT.Identity,
                                                  bias=s1[s][:, b:b + 1], scale=-UNSCALE)
                        if b % HALF == HALF - 1:
                            op.then_inc(e_ok[s], 1)

                def take_wh(s, n):
                    act.wait_ge(wh_ps[s], n)
                    nc.scalar.activation(wh[s], by_token(s, 0), ACT.Copy, scale=UNSCALE).then_inc(wh_ok[s], 1)

                def gat_exps(s, n):
                    for b in range(BLK):
                        if b in FIRST_OF_HALF:
                            act.wait_ge(emask_ok[s], at(n, HALVES, b // HALF))
                        op = nc.scalar.activation(att[s][:, b, :], att[s][:, b, :], ACT.Exp, bias=smin[s][:, b:b + 1],
                                                  scale=-1.0, accum_out=ssum[s][:, b:b + 1])
                    op.then_inc(eexp_ok[s], 1)

                def take_att(s, n):
                    act.wait_ge(att_ps[s], n)
                    nc.scalar.copy(att_tr[s], ps[s][:, 2, :].rearrange("p (b n) -> p b n", b=BLK)).then_inc(att_t[s], 1)

                def run(name, s, n):
                    if name == "norm_y":
                        norm_y(s, n)
                    elif name == "q":
                        take_q(s, n)
                    elif name == "k":
                        take_k(s, n)
                    elif name == "exps":
                        exps(s, n)
                    elif name == "turn_probs":
                        take_probs(s, n)
                    elif name == "mlp_up":
                        gelus(s, n)
                    elif name.startswith("cell"):
                        gates_of(s, n, int(name[4:]))
                    elif name.startswith("hid"):
                        tanh_c(s, n, int(name[3:]))
                    elif name == "gat":
                        gat_logits(s, n)
                        take_wh(s, n)
                    elif name == "gat_exps":
                        gat_exps(s, n)
                    elif name == "turn_att":
                        take_att(s, n)
                    elif name == "norm_l3":
                        ln_apply(s, n)
                    elif name in FEAT_OF:
                        high(s, n, FEAT_OF[name])

                for name, s, n in opening():
                    run(name, s, n)
                with act.Fori(1, ROUNDS) as r:
                    for part in parts(r):
                        with act.Fori(0, 1):
                            for name, s, n in part:
                                run(name, s, n)
                for name, s, n in closing():
                    run(name, s, n)

            @block.gpsimd
            def _(pool):
                def ln_root(s, n, j):
                    pool.wait_ge(ln_ve[s], at(n, NORMS, j))
                    nc.gpsimd.tensor_tensor(rstd[s][:, :], ve[s][:, :], nhalf[:, 0:BLK], ALU.pow).then_inc(ln_rstd[s], 1)

                def x1_bias(s, n):
                    pool.wait_ge(x1_ok[s], n * HALVES)
                    pool.wait_ge(out_stored[s], n * 16 - 15)
                    nc.gpsimd.tensor_tensor(xb[s][:, :, :], x1[s][:, :, :], row_of("bo"), ALU.add).then_inc(pre_ok[s], 1)

                def probs(s, n):
                    for b in range(BLK):
                        pool.wait_ge(inv_ok[s], at(n, BLK, b))
                        nc.gpsimd.tensor_tensor(prob[s][:, b, :, :], prob[s][:, b, :, :],
                                                ssum[s][:, b * HEADS:(b + 1) * HEADS].unsqueeze(2)
                                                .broadcast_to([P, HEADS, P]), ALU.mult).then_inc(prob_ok[s], 1)

                def x2_bias(s, n):
                    pool.wait_ge(x2_ok[s], n * HALVES)
                    nc.gpsimd.tensor_tensor(xb[s][:, :, :], x1[s][:, :, :], row_of("b2"), ALU.add).then_inc(pre_ok[s], 1)

                def xa_bias(s, n):
                    pool.wait_ge(pre_ok[s], at(n, 3, 1))
                    pool.wait_ge(feat_ps[s], feat_at(n, X2T))
                    nc.gpsimd.tensor_tensor(x1[s][:, :, :], xa[s][:, :, :], row_of("be3"), ALU.add).then_inc(pre_ok[s], 1)

                def cell(s, n, c):
                    w = cell_width(c)
                    o, th, hi = gates[s][:, GATE_O, 0:KT * w], cell_t[s][:, 0:KT * w], cell_hl[s][:, 0, 0:KT * w]
                    if is_last_step(c):
                        o, th = (like_cell(x.rearrange("q (k w) -> q k w", k=KT), c) for x in (o, th))
                        hi = cell_tokens(state_hl[s][:, 0, :, :], c)
                    pool.wait_ge(o_ok[s], at(n, NCELL, c))
                    pool.wait_ge(tanh_ok[s], at(n, NCELL, c))
                    nc.gpsimd.tensor_tensor(hi, o, th, ALU.mult).then_inc(h_hi[s], 1)

                def run(name, s, n):
                    if name in NORM_OF:
                        ln_root(s, n, NORM_OF[name])
                    elif name == "x1_bias":
                        x1_bias(s, n)
                    elif name == "exps":
                        probs(s, n)
                    elif name == "x2_bias":
                        x2_bias(s, n)
                    elif name == "xa_bias":
                        xa_bias(s, n)
                    elif name.startswith("hid"):
                        cell(s, n, int(name[3:]))

                for name, s, n in opening():
                    run(name, s, n)
                with pool.Fori(1, ROUNDS) as r:
                    for part in parts(r):
                        with pool.Fori(0, 1):
                            for name, s, n in part:
                                run(name, s, n)
                for name, s, n in closing():
                    run(name, s, n)

            @block.vector
            def _(dve):
                for s in range(STREAMS):
                    nc.vector.memset(small[:, 42 + s:43 + s], 0.0).then_inc(banks_free[s], 1)
                    nc.vector.memset(small[:, 44 + s:45 + s], 0.0).then_inc(out_stored[s], 1)

                held = [0]

                def wait_apart(semaphore, value):
                    dve.wait_ge(semaphore, value)
                    nc.vector.memset(hold[:, held[0]:held[0] + 1], 0.0)
                    held[0] += 1

                def stats_of(s, n, j, half):
                    dve.wait_ge(t_ok[s], t_at(n, j, half))
                    for b in range(half * HALF, (half + 1) * HALF):
                        op = nc.vector.bn_stats(stats[s][:, b, :], t[s][:, b, :])
                    return op

                def ln(s, n, j, make, beside=True):
                    for half in range(HALVES):
                        make(half, slice(half * HALF, (half + 1) * HALF)).then_inc(t_ok[s], 1)
                        if beside:
                            op = stats_of(s, n, j, half)
                    if not beside:
                        for half in range(HALVES):
                            op = stats_of(s, n, j, half)
                    op.then_inc(ln_stats[s], 1)
                    wait_apart(ln_stats[s], at(n, NORMS, j))
                    for b in range(BLK):
                        op = nc.vector.bn_aggr(mv[s][:, b, :], stats[s][:, b, :])
                    op.then_inc(ln_mv[s], 1)
                    dve.wait_ge(ln_mv[s], at(n, NORMS, j))
                    nc.vector.tensor_scalar(ve[s][:, :], mv[s][:, :, 1], EPS, None, ALU.add).then_inc(ln_ve[s], 1)

                def ln_apply(s, n, j, dst):
                    dve.wait_ge(ln_rstd[s], at(n, NORMS, j))
                    for b in range(BLK):
                        op = nc.vector.tensor_scalar(dst[s][:, b, :], t[s][:, b, :], mv[s][:, b, 0:1], rstd[s][:, b:b + 1],
                                                     ALU.subtract, ALU.mult)
                        if b % HALF == HALF - 1:
                            op.then_inc(ln_out[s], 1)

                def ln_centre(s, n, j, gain):
                    dve.wait_ge(ln_mv[s], at(n, NORMS, j))
                    for b in range(BLK):
                        op = nc.vector.scalar_tensor_tensor(t[s][:, b, :], t[s][:, b, :], mv[s][:, b, 0:1],
                                                            row_of(gain)[:, b, :], ALU.subtract, ALU.mult)
                    op.then_inc(centred[s], 1)
                    dve.wait_ge(centred[s], at(n, len(GAINED), GAINED.index(j)))
                    dve.wait_ge(ln_rstd[s], at(n, NORMS, j))

                def ln_scale(s, half, shift, dst):
                    for b in range(half * HALF, (half + 1) * HALF):
                        op = nc.vector.scalar_tensor_tensor(dst[s][:, b, :], t[s][:, b, :], rstd[s][:, b:b + 1],
                                                            shift[:, b, :], ALU.mult, ALU.add)
                    return op

                def ln_shift(s, n):
                    dve.wait_ge(ln_rstd[s], at(n, NORMS, LN_L3))
                    nc.vector.scalar_tensor_tensor(nmr[s][:, :], mv[s][:, :, 0], -1.0, rstd[s][:, :], ALU.mult, ALU.mult)\
                        .then_inc(ln_nmr[s], 1)

                def add_y(s, n):
                    dve.wait_ge(x_in[s], n * 16)

                    def make(half, blocks):
                        dve.wait_ge(y_ps[s], at(n, HALVES, half))
                        return nc.vector.tensor_tensor(t[s][:, blocks, :], by_token(s, 0)[:, blocks, :], xa[s][:, blocks, :],
                                                       ALU.add)
                    ln(s, n, LN_L0, make, beside=False)

                def low(s, n, j):
                    for m in range(KT):
                        dve.wait_ge(feat_hi[s], feat_at(n, j, m))
                        hi, lo = feat_dst[j][s][:, 0, m, :], feat_dst[j][s][:, 1, m, :]
                        src = by_feature(s, feat_bank[j])[:, m, :]
                        if j in feat_relu:
                            nc.vector.scalar_tensor_tensor(lo, src, 0.0, hi, ALU.max, ALU.subtract).then_inc(feat_lo[s], 1)
                        else:
                            nc.vector.tensor_tensor(lo, src, hi, ALU.subtract).then_inc(feat_lo[s], 1)

                def conv_bias(s, n):
                    def make(half, blocks):
                        dve.wait_ge(hc_ps[s], at(n, HALVES, half))
                        return nc.vector.scalar_tensor_tensor(t[s][:, blocks, :], by_token(s, 0)[:, blocks, :], UNSCALE,
                                                              row_of("bc")[:, blocks, :], ALU.mult, ALU.add)
                    ln(s, n, LN_G1, make)

                def make_x1(s, n):
                    ln_centre(s, n, LN_G1, "g1")
                    for half in range(HALVES):
                        ln_scale(s, half, row_of("be1"), t).then_inc(affine_ok[s], 1)
                    for half in range(HALVES):
                        blocks = slice(half * HALF, (half + 1) * HALF)
                        dve.wait_ge(affine_ok[s], at(n, HALVES, half))
                        nc.vector.scalar_tensor_tensor(x1[s][:, blocks, :], t[s][:, blocks, :], 0.0, xa[s][:, blocks, :],
                                                       ALU.max, ALU.add).then_inc(x1_ok[s], 1)

                def take_v(s, n):
                    dve.wait_ge(v_ps[s], n)
                    nc.vector.tensor_scalar(vv[s], by_token(s, 0), UNSCALE, None, ALU.mult).then_inc(v_ok[s], 1)

                def mask_scores(s, n):
                    for b in range(BLK):
                        if b % 2 == 0:
                            wait_apart(score_ps[s], at(n, BLK, b + 1))
                        for h in range(HEADS):
                            i = b * HEADS + h
                            op = nc.vector.tensor_tensor_reduce(prob[s][:, b, h, :],
                                                                score(s, b, h), mask1[:, :],
                                                                1.0, 3.0e38, ALU.add, ALU.min, smin[s][:, i:i + 1])
                        op.then_inc(masked_ok[s], 1)

                def invert_sums(s, n):
                    for b in range(BLK):
                        dve.wait_ge(exp_ok[s], at(n, BLK, b))
                        part = ssum[s][:, b * HEADS:(b + 1) * HEADS]
                        nc.vector.reciprocal(part, part).then_inc(inv_ok[s], 1)

                def add_attn(s, n):
                    dve.wait_ge(pre_ok[s], at(n, 3, 0))

                    def make(half, blocks):
                        dve.wait_ge(wo_ps[s], at(n, HALVES, half))
                        return nc.vector.scalar_tensor_tensor(t[s][:, blocks, :], by_token(s, 2)[:, blocks, :], UNSCALE,
                                                              xb[s][:, blocks, :], ALU.mult, ALU.add)
                    ln(s, n, LN_G2, make)

                def make_x2(s, n):
                    ln_centre(s, n, LN_G2, "g2")
                    for half in range(HALVES):
                        ln_scale(s, half, row_of("be2"), x1).then_inc(x2_ok[s], 1)

                def gelu_low(s, n):
                    for m in range(HT):
                        dve.wait_ge(gelu_ok[s], at(n, HT, m))
                        dve.wait_ge(gelu_hi[s], at(n, HT, m))
                        nc.vector.tensor_tensor(gelu_hl[s][:, 1, m, :], gelu[s][:, m, :], gelu_hl[s][:, 0, m, :],
                                                ALU.subtract).then_inc(gelu_lo[s], 1)

                def add_mlp(s, n):
                    dve.wait_ge(pre_ok[s], at(n, 3, 1))

                    def make(half, blocks):
                        dve.wait_ge(w2_ps[s], at(n, HALVES, half))
                        return nc.vector.scalar_tensor_tensor(t[s][:, blocks, :], by_token(s, 2)[:, blocks, :], UNSCALE,
                                                              xb[s][:, blocks, :], ALU.mult, ALU.add)
                    ln(s, n, LN_G3, make)

                def add_xa(s, n):
                    dve.wait_ge(pre_ok[s], at(n, 3, 2))
                    ln_centre(s, n, LN_G3, "g3")
                    ln(s, n, LN_L1, lambda half, blocks: ln_scale(s, half, x1[s][:, :, :], t), beside=False)

                def gcn_bias(s, n, j):
                    for half in range(HALVES):
                        blocks = slice(half * HALF, (half + 1) * HALF)
                        dve.wait_ge(wg_ps[s], at(n, 2 * HALVES, j * HALVES + half))
                        nc.vector.scalar_tensor_tensor(wg[s][:, blocks, :], by_token(s, 2)[:, blocks, :], UNSCALE * (j + 1),
                                                       row_of(("bg0", "bg1")[j])[:, blocks, :], ALU.mult, ALU.add)\
                            .then_inc(wg_ok[s], 1)

                def cell_sum(s, n, c):
                    w = cell_width(c)
                    g = [gates[s][:, j, 0:KT * w] for j in range(4)]
                    cc = cell_c[s][:, 0:KT * w]
                    first = CELLS[c][1] == 0
                    dve.wait_ge(gate_ok[s], gate_at(n, c, 1))
                    nc.vector.scalar_tensor_tensor(cc if first else g[GATE_I], g[GATE_I], 1.0, g[GATE_G], ALU.add,
                                                   ALU.mult).then_inc(c_ok[s] if first else ig_ok[s], 1)
                    if not first:
                        i = STEPPED.index(c)
                        dve.wait_ge(gate_ok[s], gate_at(n, c, 2))
                        nc.vector.scalar_tensor_tensor(cc, g[GATE_F], 1.0, cc, ALU.add, ALU.mult).then_inc(fc_ok[s], 1)
                        dve.wait_ge(fc_ok[s], at(n, len(STEPPED), i))
                        nc.vector.scalar_tensor_tensor(cc, cc, 0.5, g[GATE_I], ALU.mult, ALU.add).then_inc(c_ok[s], 1)
                    dve.wait_ge(gate_ok[s], gate_at(n, c, len(GATE_LIST[c]) - 1))
                    nc.vector.tensor_scalar(g[GATE_O], g[GATE_O], 1.0, None, ALU.add).then_inc(o_ok[s], 1)

                def cell_out(s, n, c):
                    w = cell_width(c)
                    o, th = gates[s][:, GATE_O, 0:KT * w], cell_t[s][:, 0:KT * w]
                    if is_last_step(c):
                        h, hi, lo = (cell_tokens(x, c) for x in
                                     (state[s], state_hl[s][:, 0, :, :], state_hl[s][:, 1, :, :]))
                        o, th = (like_cell(x.rearrange("q (k w) -> q k w", k=KT), c) for x in (o, th))
                    else:
                        h, hi, lo = cell_h[s][:, 0:KT * w], cell_hl[s][:, 0, 0:KT * w], cell_hl[s][:, 1, 0:KT * w]
                    dve.wait_ge(o_ok[s], at(n, NCELL, c))
                    dve.wait_ge(tanh_ok[s], at(n, NCELL, c))
                    nc.vector.tensor_tensor(h, o, th, ALU.mult).then_inc(h_ok[s], 1)
                    dve.wait_ge(h_ok[s], at(n, NCELL, c))
                    dve.wait_ge(h_hi[s], at(n, NCELL, c))
                    nc.vector.tensor_tensor(lo, h, hi, ALU.subtract).then_inc(h_lo[s], 1)

                def add_state(s, n):
                    def make(half, blocks):
                        dve.wait_ge(hf_ps[s], at(n, HALVES, half))
                        return nc.vector.scalar_tensor_tensor(t[s][:, blocks, :], by_token(s, 0)[:, blocks, :], 0.5,
                                                              xb[s][:, blocks, :], ALU.mult, ALU.add)
                    ln(s, n, LN_L2, make, beside=False)

                def gat_logits(s, n):
                    dve.wait_ge(s_ps[s], n)
                    nc.vector.tensor_scalar(s1[s], ps[s][:, 3, 0:BLK], -UNSCALE, None, ALU.mult).then_inc(s1_ok[s], 1)
                    for half in range(HALVES):
                        part = logit[s][:, half * HALF:(half + 1) * HALF, :]
                        dve.wait_ge(e_ok[s], at(n, HALVES, half))
                        nc.vector.scalar_tensor_tensor(part, part, 0.2, part, ALU.mult, ALU.min).then_inc(lrelu_ok[s], 1)
                    for half in range(HALVES):
                        wait_apart(lrelu_ok[s], at(n, HALVES, half))
                        for b in range(half * HALF, (half + 1) * HALF):
                            op = nc.vector.tensor_tensor_reduce(att[s][:, b, :], logit[s][:, b, :], mask3[:, :], 1.0, 3.0e38,
                                                                ALU.add, ALU.min, smin[s][:, b:b + 1])
                        op.then_inc(emask_ok[s], 1)

                def gat_sums(s, n):
                    dve.wait_ge(eexp_ok[s], n)
                    nc.vector.reciprocal(ssum[s][:, 0:BLK], ssum[s][:, 0:BLK]).then_inc(einv_ok[s], 1)

                def add_gat(s, n):
                    dve.wait_ge(einv_ok[s], n)

                    def make(half, blocks):
                        dve.wait_ge(av_ps[s], at(n, HALVES, half))
                        for b in range(half * HALF, (half + 1) * HALF):
                            op = nc.vector.scalar_tensor_tensor(t[s][:, b, :], by_token(s, 0)[:, b, :], ssum[s][:, b:b + 1],
                                                                xc[s][:, b, :], ALU.mult, ALU.add)
                        return op
                    ln(s, n, LN_L3, make, beside=False)
                    nc.vector.memset(small[:, 42 + s:43 + s], 0.0).then_inc(banks_free[s], 1)

                def run(name, s, n):
                    if name == "turn_y":
                        add_y(s, n)
                    elif name == "norm_l0":
                        ln_apply(s, n, LN_L0, xa)
                    elif name == "conv":
                        conv_bias(s, n)
                    elif name == "norm_g1":
                        make_x1(s, n)
                    elif name == "v":
                        take_v(s, n)
                    elif name == "scores":
                        mask_scores(s, n)
                    elif name == "exps":
                        invert_sums(s, n)
                    elif name == "attn_out":
                        add_attn(s, n)
                    elif name == "norm_g2":
                        make_x2(s, n)
                    elif name == "gelu_split":
                        gelu_low(s, n)
                    elif name == "mlp_down":
                        add_mlp(s, n)
                    elif name == "norm_g3":
                        add_xa(s, n)
                    elif name == "norm_l1":
                        ln_apply(s, n, LN_L1, xb)
                    elif name.startswith("gcn"):
                        gcn_bias(s, n, int(name[3:]))
                    elif name.startswith("cell"):
                        cell_sum(s, n, int(name[4:]))
                    elif name.startswith("hid"):
                        cell_out(s, n, int(name[3:]))
                    elif name == "turn_state":
                        add_state(s, n)
                    elif name == "norm_l2":
                        ln_apply(s, n, LN_L2, xc)
                    elif name == "gat":
                        gat_logits(s, n)
                    elif name == "gat_exps":
                        gat_sums(s, n)
                    elif name == "gat_mix":
                        add_gat(s, n)
                    elif name == "norm_l3":
                        ln_shift(s, n)
                    elif name in FEAT_OF:
                        low(s, n, FEAT_OF[name])

                for name, s, n in opening():
                    run(name, s, n)
                with dve.Fori(1, ROUNDS) as r:
                    for part in parts(r):
                        with dve.Fori(0, 1):
                            for name, s, n in part:
                                run(name, s, n)
                for name, s, n in closing():
                    run(name, s, n)


def kernel(**inputs):
    import numpy as np
    import concourse.bacc as bacc
    from concourse.bass_utils import run_bass_kernel_spmd

    given = {k: np.asarray(v) for k, v in inputs.items()}

    def turned(a):
        return np.swapaxes(a, -1, -2)

    mats = {"l0_w1": turned(given["L0_gnn_W1"]), "l0_w2": turned(given["L0_gnn_W2"]), "wc": given["L1_gnn_Wc"],
            "wq": given["L1_gnn_Wq"], "wk": given["L1_gnn_Wk"], "wv": given["L1_gnn_Wv"], "wo": given["L1_gnn_Wo"],
            "w1": given["L1_gnn_W1"], "w2": given["L1_gnn_W2"], "wg0": given["L2_gnn_Wg0"], "wg1": given["L2_gnn_Wg1"],
            "w3": given["L3_gnn_W"]}
    for p in range(1, SKIPS + 1):
        mats[f"wih{p}"] = turned(given["L2_gnn_Wih"][p - 1])
        mats[f"whh{p}"] = turned(given["L2_gnn_Whh"][p - 1])

    def tiled(w):
        return w.reshape(-1, P, w.shape[1]).transpose(1, 0, 2).reshape(P, -1)

    vectors = {"b1": given["L0_gnn_b1"], "g1": given["L0_gnn_g1"], "be1": given["L0_gnn_be1"], "b2": given["L0_gnn_b2"],
               "g2": given["L0_gnn_g2"], "be2": given["L0_gnn_be2"], "l1_b1": given["L1_gnn_b1"],
               "bih": given["L2_gnn_bih"], "bhh": given["L2_gnn_bhh"], "a": given["L3_gnn_a"]}
    lines = {r: given[f"L1_gnn_{r}"] for r in ROWS if not r.startswith("bg")}
    lines |= {r: given[f"L2_gnn_{r}"] for r in ROWS if r.startswith("bg")}
    arrays = {
        "in_x": given["x"],
        "in_adj": given["adj"],
        "in_adj_t": turned(given["adj"]),
        "in_wpack": np.concatenate([tiled(mats[name]) for name, _, _ in WEIGHTS], axis=1),
        "in_w3t": tiled(turned(given["L3_gnn_W"])).reshape(P, KT, DIM),
        "in_cols": np.concatenate([vectors[name].reshape(-1, P).T for name, _ in COLS], axis=1),
        "in_rows": np.stack([lines[r] for r in ROWS]),
    }
    arrays = {k: np.ascontiguousarray(v) for k, v in arrays.items()}
    nc = bacc.Bacc("TRN2", target_bir_lowering=False, num_devices=1)
    args = [nc.dram_tensor(k, v.shape, mybir.dt.from_np(v.dtype), kind="ExternalInput").ap() for k, v in arrays.items()]
    out = nc.dram_tensor("out", (BATCH, NODES, DIM), F32, kind="ExternalOutput").ap()
    build(nc, *args, out)
    result = run_bass_kernel_spmd(nc, [arrays], core_ids=[0])
    return result.results[0]["out"]
```
